# Optimizing a Trainium2 kernel written in Bass

```python
import numpy as np
import jax
import jax.numpy as jnp

def _softmax(x, axis=-1):
    return jax.nn.softmax(x, axis=axis)

def _gelu(x):
    return jax.nn.gelu(x, approximate=True)

def _silu(x):
    return jax.nn.silu(x)

def _sigmoid(x):
    return jax.nn.sigmoid(x)

def _layernorm(x, axis=-1, eps=1e-05):
    m = jnp.mean(x, axis=axis, keepdims=True)
    v = jnp.var(x, axis=axis, keepdims=True)
    return (x - m) / jnp.sqrt(v + eps)

def _scatter_add(tgt, idx, src, axis=0):
    return tgt.at[idx].add(src)

def _segment_sum(src, seg, n):
    return jax.ops.segment_sum(src, seg, n)
kernel_name = 'mk_perceiver_d1_seqx_r4_c70477'

def setup_inputs(seed: int=0):
    np.random.seed(seed)
    _w = jnp.asarray

    def _rec_inputs():
        import jax
        import jax.numpy as jnp
        _rk = jax.random.key(seed)
        x = 7.22e-05 + 1 * jax.random.normal(jax.random.fold_in(_rk, 1), (64, 64, 256), jnp.float32)
        _lenS = 64 - jax.random.randint(jax.random.fold_in(_rk, 7), (64,), 0, max(1, 64 // 4) + 1, jnp.int32)
        _lenS2 = 256 - jax.random.randint(jax.random.fold_in(_rk, 8), (64,), 0, max(1, 256 // 4) + 1, jnp.int32)
        _ctx_1024P = jax.random.normal(jax.random.fold_in(_rk, 11), (64, 16, 256), jnp.float32)
        _ctx_1024c = jax.random.dirichlet(jax.random.fold_in(_rk, 511), 0.3 * jnp.ones((16,), jnp.float32), (64, 256))
        _ctx_1024t = jnp.einsum('bsk,bkd->bsd', _ctx_1024c, _ctx_1024P)
        _ctx_1024t = _ctx_1024t * jax.lax.rsqrt(jnp.mean(jnp.square(_ctx_1024t)) + 1e-12) * 0.953939
        ctx_1024 = 4.13588e-05 + 0.999923 * (_ctx_1024t + 0.3 * jax.random.normal(jax.random.fold_in(_rk, 611), (64, 256, 256), jnp.float32))
        _validS = jnp.arange(64)[None, :] < _lenS[:, None]
        _validS2 = jnp.arange(256)[None, :] < _lenS2[:, None]
        _causal = jnp.tril(jnp.ones((64, 64), dtype=bool))
        mask_BxS2_bf1 = jnp.ones((64, 256), dtype=bool)
        return (x, ctx_1024, mask_BxS2_bf1)
    x, ctx_1024, mask_BxS2_bf1 = _rec_inputs()

    def _L0_xattn_setup():
        import jax, jax.numpy as jnp
        import numpy as np
        N_HEADS = 16
        key = jax.random.key(seed)
        ks = jax.random.split(key, 12)
        b, s, qd, cd, md = (4, 512, 256, 256, 256)
        inp = {'q': jax.random.normal(ks[0], (b, s, qd), jnp.float32), 'k': jax.random.normal(ks[1], (b, s, cd), jnp.float32), 'v': jax.random.normal(ks[2], (b, s, cd), jnp.float32), 'attention_mask': jnp.ones((b, s), dtype=bool), 'Wq': jax.random.normal(ks[3], (qd, md), jnp.float32) / np.sqrt(qd), 'bq': jnp.zeros((md,), jnp.float32), 'Wk': jax.random.normal(ks[4], (cd, md), jnp.float32) / np.sqrt(cd), 'bk': jnp.zeros((md,), jnp.float32), 'Wv': jax.random.normal(ks[5], (cd, md), jnp.float32) / np.sqrt(cd), 'bv': jnp.zeros((md,), jnp.float32), 'Wo': jax.random.normal(ks[6], (md, qd), jnp.float32) / np.sqrt(md), 'bo': jnp.zeros((qd,), jnp.float32)}
        return inp
    _L0_xattn_all = _L0_xattn_setup()
    _L0_xattn_in = {k: v for k, v in _L0_xattn_all.items() if k in ('Wq', 'bq', 'Wk', 'bk', 'Wv', 'bv', 'Wo', 'bo')}
    del _L0_xattn_all

    def _L0_attn_setup():
        import jax, jax.numpy as jnp
        import numpy as np
        DIM = 256
        HEADS = 16
        HEAD_DIM = DIM // HEADS
        FEAT = 64
        B, N = (4, 1024)

        def _elu1(x):
            return jnp.where(x > 0, x + 1.0, jnp.exp(x))
        key = jax.random.key(seed)
        k_x, k_qkv, k_proj, k_wo, k_bo = jax.random.split(key, 5)
        x = jax.random.normal(k_x, (B, N, DIM), dtype=jnp.float32)
        w_qkv = jax.random.normal(k_qkv, (DIM, 3 * DIM), dtype=jnp.float32) * (1.0 / np.sqrt(DIM))
        proj_matrix = jax.random.normal(k_proj, (HEADS, HEAD_DIM, FEAT), dtype=jnp.float32) * (1.0 / np.sqrt(HEAD_DIM))
        w_out = jax.random.normal(k_wo, (DIM, DIM), dtype=jnp.float32) * (1.0 / np.sqrt(DIM))
        b_out = jax.random.normal(k_bo, (DIM,), dtype=jnp.float32) * 0.01
        return {'x': x, 'w_qkv': w_qkv, 'proj_matrix': proj_matrix, 'w_out': w_out, 'b_out': b_out}
    _L0_attn_all = _L0_attn_setup()
    _L0_attn_in = {k: v for k, v in _L0_attn_all.items() if k in ('w_qkv', 'proj_matrix', 'w_out', 'b_out')}
    del _L0_attn_all

    def _L0_ffn_setup():
        import jax, jax.numpy as jnp
        import numpy as np
        B, T, C, H, E, K, F = (2, 512, 256, 16, 8, 2, 512)
        EPS = 1e-05

        def layernorm(x, w):
            m = x.mean(-1, keepdims=True)
            v = x.var(-1, keepdims=True)
            return (x - m) * jax.lax.rsqrt(v + EPS) * w

        def attention(x, c_attn_w, c_proj_w):
            b, t, c = x.shape
            hd = c // H
            q, k, v = jnp.split(x @ c_attn_w, 3, axis=-1)
            q = q.reshape(b, t, H, hd).transpose(0, 2, 1, 3)
            k = k.reshape(b, t, H, hd).transpose(0, 2, 1, 3)
            v = v.reshape(b, t, H, hd).transpose(0, 2, 1, 3)
            att = jnp.einsum('bhqd,bhkd->bhqk', q, k) / jnp.sqrt(jnp.asarray(hd, x.dtype))
            causal = jnp.tril(jnp.ones((t, t), bool))
            att = jnp.where(causal, att, jnp.asarray(-jnp.inf, att.dtype))
            att = jax.nn.softmax(att, axis=-1)
            y = jnp.einsum('bhqk,bhkd->bhqd', att, v)
            y = y.transpose(0, 2, 1, 3).reshape(b, t, c)
            return y @ c_proj_w

        def moe_mlp(x, router_w, w1, w2):
            b, t, c = x.shape
            xf = x.reshape(-1, c)
            router_logits = xf @ router_w
            probs = jax.nn.softmax(router_logits.astype(jnp.float32), axis=-1)
            rw, sel = jax.lax.top_k(probs, K)
            rw = rw / rw.sum(axis=-1, keepdims=True)
            rw = rw.astype(x.dtype)
            w1e = w1.reshape(c, E, F).transpose(1, 0, 2)
            w2e = w2.reshape(E, F, c)
            h = jax.nn.gelu(jnp.einsum('nc,ecf->enf', xf, w1e), approximate=False)
            y_all = jnp.einsum('enf,efc->nec', h, w2e)
            y_sel = jnp.take_along_axis(y_all, sel[:, :, None], axis=1)
            y = (y_sel * rw[:, :, None]).sum(axis=1)
            return y.reshape(b, t, c)
        key = jax.random.key(seed)
        ks = jax.random.split(key, 6)
        s = 0.02
        return {'x': jax.random.normal(ks[0], (B, T, C), jnp.float32), 'ln1_w': jnp.ones((C,), jnp.float32), 'c_attn_w': jax.random.normal(ks[1], (C, 3 * C), jnp.float32) * s, 'c_proj_w': jax.random.normal(ks[2], (C, C), jnp.float32) * s, 'ln2_w': jnp.ones((C,), jnp.float32), 'router_w': jax.random.normal(ks[3], (C, E), jnp.float32) * s, 'w1': jnp.clip(jax.random.normal(ks[4], (C, E * F), jnp.float32) * s, -0.06, 0.06), 'w2': jnp.clip(jax.random.normal(ks[5], (E * F, C), jnp.float32) * s, -0.06, 0.06)}
    _L0_ffn_all = _L0_ffn_setup()
    _L0_ffn_in = {k: v for k, v in _L0_ffn_all.items() if k in ('ln1_w', 'c_attn_w', 'c_proj_w', 'ln2_w', 'router_w', 'w1', 'w2')}
    del _L0_ffn_all
    return {'x': x, 'ctx_1024': ctx_1024, 'mask_BxS2_bf1': mask_BxS2_bf1, 'L0_xattn_Wq': _L0_xattn_in['Wq'], 'L0_xattn_bq': _L0_xattn_in['bq'], 'L0_xattn_Wk': _L0_xattn_in['Wk'], 'L0_xattn_bk': _L0_xattn_in['bk'], 'L0_xattn_Wv': _L0_xattn_in['Wv'], 'L0_xattn_bv': _L0_xattn_in['bv'], 'L0_xattn_Wo': _L0_xattn_in['Wo'], 'L0_xattn_bo': _L0_xattn_in['bo'], 'L0_attn_w_qkv': _L0_attn_in['w_qkv'], 'L0_attn_proj_matrix': _L0_attn_in['proj_matrix'], 'L0_attn_w_out': _L0_attn_in['w_out'], 'L0_attn_b_out': _L0_attn_in['b_out'], 'L0_ffn_ln1_w': _L0_ffn_in['ln1_w'], 'L0_ffn_c_attn_w': _L0_ffn_in['c_attn_w'], 'L0_ffn_c_proj_w': _L0_ffn_in['c_proj_w'], 'L0_ffn_ln2_w': _L0_ffn_in['ln2_w'], 'L0_ffn_router_w': _L0_ffn_in['router_w'], 'L0_ffn_w1': _L0_ffn_in['w1'], 'L0_ffn_w2': _L0_ffn_in['w2']}

def reference(x, ctx_1024, mask_BxS2_bf1, L0_xattn_Wq, L0_xattn_bq, L0_xattn_Wk, L0_xattn_bk, L0_xattn_Wv, L0_xattn_bv, L0_xattn_Wo, L0_xattn_bo, L0_attn_w_qkv, L0_attn_proj_matrix, L0_attn_w_out, L0_attn_b_out, L0_ffn_ln1_w, L0_ffn_c_attn_w, L0_ffn_c_proj_w, L0_ffn_ln2_w, L0_ffn_router_w, L0_ffn_w1, L0_ffn_w2):
    import jax
    import jax.numpy as jnp

    def _L0_xattn_ref(q, k, v, attention_mask, Wq, bq, Wk, bk, Wv, bv, Wo, bo):
        import jax, jax.numpy as jnp
        import numpy as np
        N_HEADS = 16
        b, s, _ = q.shape
        n = N_HEADS
        qh = (q @ Wq + bq).reshape(b, s, n, -1).transpose(0, 2, 1, 3)
        kh = (k @ Wk + bk).reshape(b, k.shape[1], n, -1).transpose(0, 2, 1, 3)
        vh = (v @ Wv + bv).reshape(b, v.shape[1], n, -1).transpose(0, 2, 1, 3)
        scale = qh.shape[-1] ** (-0.5)
        sim = jnp.einsum('bnid,bnjd->bnij', qh, kh) * scale
        inv = ~attention_mask
        neg = jnp.finfo(sim.dtype).min
        sim = jnp.where(inv[:, None, None, :], neg, sim)
        attn = jax.nn.softmax(sim, axis=-1)
        out = jnp.einsum('bnij,bnjd->bnid', attn, vh)
        out = out.transpose(0, 2, 1, 3).reshape(b, s, -1)
        return out @ Wo + bo

    def _L0_attn_ref(x, w_qkv, proj_matrix, w_out, b_out):
        import jax, jax.numpy as jnp
        import numpy as np
        DIM = 256
        HEADS = 16
        HEAD_DIM = DIM // HEADS
        FEAT = 64
        B, N = (4, 1024)

        def _elu1(x):
            return jnp.where(x > 0, x + 1.0, jnp.exp(x))
        b, n, d = x.shape
        h, hd = (HEADS, HEAD_DIM)
        qkv = x @ w_qkv
        q, k, v = jnp.split(qkv, 3, axis=-1)
        to_heads = lambda t: t.reshape(b, n, h, hd).transpose(0, 2, 1, 3)
        q, k, v = (to_heads(q), to_heads(k), to_heads(v))
        q_proj = _elu1(jnp.einsum('bhnd,hdf->bhnf', q, proj_matrix))
        k_proj = _elu1(jnp.einsum('bhnd,hdf->bhnf', k, proj_matrix))
        kv = jnp.einsum('bhnf,bhnd->bhfd', k_proj, v)
        attn = jnp.einsum('bhnf,bhfd->bhnd', q_proj, kv)
        k_sum = k_proj.sum(axis=2)
        z = 1.0 / (jnp.einsum('bhnf,bhf->bhn', q_proj, k_sum) + 1e-08)
        attn = attn * z[..., None]
        out = attn.transpose(0, 2, 1, 3).reshape(b, n, d)
        return out @ w_out + b_out

    def _L0_ffn_ref(x, ln1_w, c_attn_w, c_proj_w, ln2_w, router_w, w1, w2):
        import jax, jax.numpy as jnp
        import numpy as np
        B, T, C, H, E, K, F = (2, 512, 256, 16, 8, 2, 512)
        EPS = 1e-05

        def layernorm(x, w):
            m = x.mean(-1, keepdims=True)
            v = x.var(-1, keepdims=True)
            return (x - m) * jax.lax.rsqrt(v + EPS) * w

        def attention(x, c_attn_w, c_proj_w):
            b, t, c = x.shape
            hd = c // H
            q, k, v = jnp.split(x @ c_attn_w, 3, axis=-1)
            q = q.reshape(b, t, H, hd).transpose(0, 2, 1, 3)
            k = k.reshape(b, t, H, hd).transpose(0, 2, 1, 3)
            v = v.reshape(b, t, H, hd).transpose(0, 2, 1, 3)
            att = jnp.einsum('bhqd,bhkd->bhqk', q, k) / jnp.sqrt(jnp.asarray(hd, x.dtype))
            causal = jnp.tril(jnp.ones((t, t), bool))
            att = jnp.where(causal, att, jnp.asarray(-jnp.inf, att.dtype))
            att = jax.nn.softmax(att, axis=-1)
            y = jnp.einsum('bhqk,bhkd->bhqd', att, v)
            y = y.transpose(0, 2, 1, 3).reshape(b, t, c)
            return y @ c_proj_w

        def moe_mlp(x, router_w, w1, w2):
            b, t, c = x.shape
            xf = x.reshape(-1, c)
            router_logits = xf @ router_w
            probs = jax.nn.softmax(router_logits.astype(jnp.float32), axis=-1)
            rw, sel = jax.lax.top_k(probs, K)
            rw = rw / rw.sum(axis=-1, keepdims=True)
            rw = rw.astype(x.dtype)
            w1e = w1.reshape(c, E, F).transpose(1, 0, 2)
            w2e = w2.reshape(E, F, c)
            h = jax.nn.gelu(jnp.einsum('nc,ecf->enf', xf, w1e), approximate=False)
            y_all = jnp.einsum('enf,efc->nec', h, w2e)
            y_sel = jnp.take_along_axis(y_all, sel[:, :, None], axis=1)
            y = (y_sel * rw[:, :, None]).sum(axis=1)
            return y.reshape(b, t, c)
        x = x + attention(layernorm(x, ln1_w), c_attn_w, c_proj_w)
        x = x + moe_mlp(layernorm(x, ln2_w), router_w, w1, w2)
        return x
    x = x + _L0_xattn_ref(_layernorm(x, axis=-1), ctx_1024, ctx_1024, mask_BxS2_bf1, L0_xattn_Wq, L0_xattn_bq, L0_xattn_Wk, L0_xattn_bk, L0_xattn_Wv, L0_xattn_bv, L0_xattn_Wo, L0_xattn_bo)
    x = x + _L0_attn_ref(_layernorm(x, axis=-1), L0_attn_w_qkv, L0_attn_proj_matrix, L0_attn_w_out, L0_attn_b_out)
    x = x + _L0_ffn_ref(_layernorm(x, axis=-1), L0_ffn_ln1_w, L0_ffn_c_attn_w, L0_ffn_c_proj_w, L0_ffn_ln2_w, L0_ffn_router_w, L0_ffn_w1, L0_ffn_w2)
    return x

_drawn_inputs = setup_inputs


def setup_inputs(seed=0):
    import zlib

    import numpy as np

    out = dict(_drawn_inputs(seed))
    spreads = {'L0_xattn_bq': (0.0, 0.334),
     'L0_xattn_bk': (0.0, 0.8),
     'L0_xattn_bv': (0.0, 0.1),
     'L0_xattn_bo': (0.0, 0.1),
     'L0_ffn_ln1_w': (1.0, 0.6),
     'L0_ffn_ln2_w': (1.0, 0.6)}
    factors = {'L0_attn_proj_matrix': 6.251, 'L0_attn_b_out': 6.954}
    for name, (base, spread) in spreads.items():
        noise = np.random.default_rng([zlib.crc32(name.encode()), seed]).standard_normal(out[name].shape)
        drawn = base * np.exp(spread * noise) if base else spread * noise
        out[name] = jnp.asarray(drawn.astype(out[name].dtype))
    for name, factor in factors.items():
        out[name] = (out[name] * factor).astype(out[name].dtype)
    return out
```

```python
from contextlib import ExitStack

import concourse.bass as bass
from concourse import mybir
import numpy as np

F32 = mybir.dt.float32
U32 = mybir.dt.uint32
U8 = mybir.dt.uint8
ALU = mybir.AluOpType
ACT = mybir.ActivationFunctionType
AX = mybir.AxisListType

P = 128
B, SQ, D = 64, 64, 256
SK = 256
NH, HD = 16, 16
C = D // P
NP_ = NH // 2
FEAT = 64
E, FF = 8, 512
FB = FF // P
TILES = B * SQ // P
SLOTS = 2
ITERS = TILES // SLOTS
SCALE = float(HD) ** -0.5
EPS = 1e-5
NEG = -3.4e38
RING = 3


PE_STEPS = (["xT1", "q1", "k1a", "k1b", "v1a", "v1b", "s0", "s1"]
            + [n for p in range(NP_) for n in ([f"pT{p}"] + ([f"s{p + 2}"] if p + 2 < NP_ else []) + [f"pv{p}"])]
            + ["w1"]
            + ["xT2", "qk2", "v2", "kpA", "kpB", "qpA", "qpB", "kvA", "kvB", "aoA", "aoB", "aT2", "w2"]
            + ["xT3", "qk3", "v3", "s3A", "s3B", "pT3A", "pT3B", "o3A", "o3B", "aT3", "w3"]
            + ["xT4", "rt", "h0"] + [n for e in range(E) for n in ([f"h{e + 1}"] if e + 1 < E else []) + [f"y{e}"]])

ACT_STEPS = (["xT1", "q1", "k1a"] + [n for p in range(NP_) for n in (f"exp{p}", f"pT{p}")]
             + ["xT2", "qk2", "ekA", "ekB", "eqA", "eqB", "kv", "aT2"]
             + ["xT3", "q3", "e3A", "e3B", "pT3A", "aT3"]
             + ["xT4", "eg"] + [f"h{e}" for e in range(E)])

DVE_STEPS = (["var1", "xn1", "madd", "qB", "k1b", "v1a", "v1b", "max0", "nb0"]
             + [n for p in range(NP_) for n in (([f"max{p + 1}", f"nb{p + 1}"] if p + 1 < NP_ else [])
                                                + [f"ri{p}", f"nrm{p}"])]
             + ["o1a", "o1", "x1"]
             + ["var2", "xn2", "v2", "tkA", "kpA", "tkB", "kpB", "tqA", "qpA", "tqB", "qpB", "kv",
                "den", "rden", "ao", "x2", "var0", "h0"]
             + ["var3", "xn3", "kB", "vB", "s3A", "m3A", "d3A", "s3B", "m3B", "d3B", "sumA", "sumB", "r3", "pT3B", "o3", "x3"]
             + ["var4", "xn4", "lg", "top", "ix", "ixf", "dl", "sg", "r4", "w2nd", "g1", "gate"]
             + [f"y{e}" for e in range(E)])

POOL_STEPS = ["rs1", "xb1", "rs2", "xb2", "rs0", "rs3", "rs4", "sum"]

GROUPS = ([("xT1", "act", "xT1"), ("q1", "act", "q1"), ("k1a", "act", "k1a"), ("k1b", "dve", "k1b"),
           ("v1a", "dve", "v1a"), ("v1b", "dve", "v1b"), ("s0", "dve", "max0"), ("s1", "dve", "max1")]
          + [n for p in range(NP_) for n in ([(f"pT{p}", "act", f"pT{p}")]
                                             + ([(f"s{p + 2}", "dve", f"max{p + 2}")] if p + 2 < NP_ else []))]
          + [("w1", "dve", "x1")]
          + [("xT2", "act", "xT2"), ("qk2", "act", "qk2"), ("v2", "dve", "v2"), ("kpA", "dve", "kpA"),
             ("kpB", "dve", "kpB"), ("qpA", "dve", "qpA"), ("qpB", "dve", "qpB"), ("kvA", "act", "kv"),
             ("kvB", "dve", "kv"), ("aoA", "dve", "ao"), ("aoB", "dve", "ao"), ("aT2", "act", "aT2"),
             ("w2", "dve", "x2")]
          + [("xT3", "act", "xT3"), ("qk3", "dve", "kB"), ("v3", "dve", "vB"), ("s3A", "dve", "s3A"),
             ("s3B", "dve", "s3B"), ("pT3A", "act", "pT3A"), ("pT3B", "dve", "pT3B"), ("o3A", "dve", "o3"),
             ("o3B", "dve", "o3"), ("aT3", "act", "aT3"), ("w3", "dve", "x3")]
          + [("xT4", "act", "xT4"), ("rt", "dve", "lg"), ("h0", "act", "h0")]
          + [n for e in range(E) for n in ([(f"h{e + 1}", "act", f"h{e + 1}")] if e + 1 < E else [])
             + [(f"y{e}", "dve", f"y{e}")]])
GROUP_AT = {name: n for n, (name, _, _) in enumerate(GROUPS)}


class Progress:

    def __init__(self, name, sems, steps):
        self.name, self.sems, self.steps, self.at = name, sems, steps, [0] * SLOTS
        assert len(set(steps)) == len(steps)

    def tick(self, u, name):
        assert self.steps[self.at[u] % len(self.steps)] == name, (name, self.steps[self.at[u] % len(self.steps)])
        self.at[u] += 1
        return self.sems[u], 1

    def done(self, u, name, i, bank=None):
        count = len(self.steps) + self.steps.index(name)
        if bank is not None and engine_that_reads(bank) == self.name:
            count = max(count, freed_at(bank, self.steps))
        return self.sems[u], i * len(self.steps) + count + 1

    def done_before(self, u, name, i):
        return self.sems[u], i * len(self.steps) + self.steps.index(name) + 1


def engine_that_reads(group):
    return GROUPS[GROUP_AT[group] - RING][1]


def freed_at(group, steps):
    n = GROUP_AT[group]
    return (len(steps) if n >= RING else 0) + steps.index(GROUPS[n - RING][2])


def build(nc, x, ctxT, mask, wq, bq, wk, bk, wv, bv, wo, bo, wqkv, proj, wout, bout, ln1, wattn, wproj, ln2,
          router, w1, w2, ident_d, hmask_d, causal_d, iota_d, out):
    with ExitStack() as ctx:
        def sb(name, shape, dt=F32):
            return ctx.enter_context(nc.sbuf_tensor(name, shape, dt))

        def per_slot(name, shape, dt=F32):
            return [sb(f"{name}_{u}", shape, dt) for u in range(SLOTS)]

        def sem(name):
            return ctx.enter_context(nc.semaphore(name))

        ident = sb("ident", [P, P])
        hmask = sb("hmask", [P, 2])
        causal = sb("causal", [P, SQ])
        iota8 = sb("iota8", [P, E])
        Wq, Wk, Wv, Wo = (sb(n, [P, C, D]) for n in ("Wq", "Wk", "Wv", "Wo"))
        Wqkv, Wattn = (sb(n, [P, C, 3 * D]) for n in ("Wqkv", "Wattn"))
        Wout, Wproj = (sb(n, [P, C, D]) for n in ("Wout", "Wproj"))
        PB = sb("PB", [P, C, 8 * FEAT])
        Wr = sb("Wr", [P, C, E])
        W1 = sb("W1", [P, C, E * FF])
        W2 = sb("W2", [P, E * FB, D])
        bqT, bkT, ln1T, ln2T = (sb(n, [P, C]) for n in ("bqT", "bkT", "ln1T", "ln2T"))
        bv_b, bo_b, bout_b = (sb(n, [P, D]) for n in ("bv_b", "bo_b", "bout_b"))
        mhalf = sb("mhalf", [P, 1])

        x_in = per_slot("x_in", [P, D])
        ctxs = per_slot("ctxs", [P, C, 2, SK])
        mraw = per_slot("mraw", [P, 2, SK], U8)
        madd = per_slot("madd", [P, 2, SK])
        bst = per_slot("bst", [P, 6])
        mv = per_slot("mv", [P, 4])
        xn = per_slot("xn", [P, D])
        xT = per_slot("xT", [P, C, P])
        xres = per_slot("xres", [P, D])
        xa = per_slot("xa", [P, D])
        xb = per_slot("xb", [P, D])
        qs = per_slot("qs", [P, C, P])
        qB = per_slot("qB", [P, 4, C, 2, 2, SQ])
        kT = per_slot("kT", [P, C, 2, SK])
        vS = per_slot("vS", [P, 2, 2, D])
        pb = [[sb(f"pb{r}_{u}", [P, 2, SK]) for r in range(3)] for u in range(SLOTS)]
        pT = [[sb(f"pT{r}_{u}", [P, 4, P]) for r in range(2)] for u in range(SLOTS)]
        mx = per_slot("mx", [P, 2 * NP_])
        nb = per_slot("nb", [P, 2 * NP_])
        su = per_slot("su", [P, 2 * NP_])
        ri = per_slot("ri", [P, 2 * NP_])
        aT = qs
        at = xn
        qk = [pb[u][2][:, :, :].rearrange("p b (c t) -> p (b c) t", t=P) for u in range(SLOTS)]
        VW = NP_ * 34 + 30
        v2 = per_slot("v2", [P, 2, VW])
        kvb = per_slot("kvb", [P, 2, VW])
        kB = per_slot("kB", [P, C, 2, 8, SQ])
        vB = per_slot("vB", [P, 2, D + 32])
        gt = per_slot("gt", [P, 64])
        gix = per_slot("gix", [P, 8], U32)
        acc = xb
        kp = [kT[u][:, :, :, :].rearrange("p a b c -> p (a b c)") for u in range(SLOTS)]
        qp = [vS[u][:, :, :, :].rearrange("p a b c -> p (a b c)") for u in range(SLOTS)]
        pbf = [[pb[u][r][:, :, :].rearrange("p a b -> p (a b)") for r in range(3)] for u in range(SLOTS)]

        ring = [[ctx.enter_context(nc.psum_tensor(f"ring{r}_{u}", [P, 512], F32)) for r in range(RING)]
                for u in range(SLOTS)]
        psO = [ctx.enter_context(nc.psum_tensor(f"psO_{u}", [P, 512], F32)) for u in range(SLOTS)]

        weights_in = sem("weights_in")
        zeroed = sem("zeroed")
        ones_set = sem("ones_set")
        x_loaded = [sem(f"x_loaded{u}") for u in range(SLOTS)]
        ctx_loaded = [sem(f"ctx_loaded{u}") for u in range(SLOTS)]
        mask_loaded = [sem(f"mask_loaded{u}") for u in range(SLOTS)]
        stored = [sem(f"stored{u}") for u in range(SLOTS)]
        wait_taken = sem("wait_taken")
        ln_chain = [sem(f"ln_chain{u}") for u in range(SLOTS)]
        pe_ = Progress("pe", [sem(f"pe_steps{u}") for u in range(SLOTS)], PE_STEPS)
        act_ = Progress("act", [sem(f"act_steps{u}") for u in range(SLOTS)], ACT_STEPS)
        dve_ = Progress("dve", [sem(f"dve_steps{u}") for u in range(SLOTS)], DVE_STEPS)
        pool_ = Progress("pool", [sem(f"pool_steps{u}") for u in range(SLOTS)], POOL_STEPS)
        engine_of = {"act": act_, "dve": dve_}

        def bank(u, name):
            return ring[u][GROUP_AT[name] % RING]

        def reader_of(name):
            return engine_of[engine_that_reads(name)]

        def bank_free(u, name, i):
            engine = reader_of(name)
            return engine.sems[u], i * len(engine.steps) + freed_at(name, engine.steps) + 1

        block = ctx.enter_context(nc.Block())

        loads = [
            (ident[:, :], ident_d), (hmask[:, :], hmask_d), (causal[:, :], causal_d),
            (iota8[:, :], iota_d),
            (Wq[:, :, :], wq.rearrange("(c p) n -> p c n", p=P)),
            (bqT[:, :], bq.rearrange("(c p) -> p c", p=P)),
            (Wk[:, :, :], wk.rearrange("(c p) n -> p c n", p=P)),
            (bkT[:, :], bk.rearrange("(c p) -> p c", p=P)),
            (Wv[:, :, :], wv.rearrange("(c p) n -> p c n", p=P)),
            (bv_b[:, :], bv.rearrange("(o n) -> o n", o=1).to_broadcast([P, D])),
            (bo_b[:, :], bo.rearrange("(o n) -> o n", o=1).to_broadcast([P, D])),
            (Wo[:, :, :], wo.rearrange("(c p) n -> p c n", p=P)),
            (Wqkv[:, :, :], wqkv.rearrange("(c p) n -> p c n", p=P)),
            (Wout[:, :, :], wout.rearrange("(c p) n -> p c n", p=P)),
            (bout_b[:, :], bout.rearrange("(o n) -> o n", o=1).to_broadcast([P, D])),
            (ln1T[:, :], ln1.rearrange("(c p) -> p c", p=P)),
            (Wattn[:, :, :], wattn.rearrange("(c p) n -> p c n", p=P)),
            (Wproj[:, :, :], wproj.rearrange("(c p) n -> p c n", p=P)),
            (ln2T[:, :], ln2.rearrange("(c p) -> p c", p=P)),
            (Wr[:, :, :], router.rearrange("(c p) n -> p c n", p=P)),
            (W1[:, :, :], w1.rearrange("(c p) n -> p c n", p=P)),
            (W2[:, :, :], w2.rearrange("(f p) n -> p f n", p=P)),
        ]
        NW = len(loads) + NH

        @block.sync
        def _(sp):
            with nc.allow_non_contiguous_dma(reason="biases laid along partitions, once"):
                for dst, src in loads:
                    sp.dma_start(dst, src).then_inc(weights_in, 16)
            sp.wait_ge(zeroed, 1)
            for h in range(NH):
                r = HD * (h % 8)
                sp.dma_start(PB[r:r + HD, h // 8, FEAT * (h % 8):FEAT * (h % 8) + FEAT], proj[h]).then_inc(weights_in, 16)
            with sp.Fori(0, ITERS) as i:
                for u in range(SLOTS):
                    sp.wait_ge(*dve_.done_before(u, "xn1", i))
                    sp.wait_ge(*pool_.done_before(u, "xb1", i))
                    sp.dma_start(x_in[u][:, :], x[bass.ds((i * SLOTS + u) * P, P), :]).then_inc(x_loaded[u], 16)
                    sp.wait_ge(*dve_.done_before(u, "madd", i))
                    sp.dma_start(mraw[u][:, :, :],
                                 mask[bass.ds((i * SLOTS + u) * 2, 2), :].rearrange("(o b) k -> o b k", o=1)
                                 .to_broadcast([P, 2, SK])).then_inc(mask_loaded[u], 16)
                    sp.wait_ge(*pe_.done_before(u, "v1b", i))
                    for b in range(2):
                        sp.dma_start(ctxs[u][:, :, b, :],
                                     ctxT[bass.ds(((i * SLOTS + u) * 2 + b) * D, D), :]
                                     .rearrange("(c p) k -> p c k", p=P)).then_inc(ctx_loaded[u], 16)

        @block.gpsimd
        def _(pool):
            pool.memset(PB[:, :, :], 0.0).then_inc(zeroed, 1)
            for u in range(SLOTS):
                pool.memset(v2[u][:, :, :], 0.0).then_inc(ones_set, 1)
                pool.memset(qB[u][:, :, :, :, :, :], 0.0).then_inc(zeroed, 1)
                pool.memset(kB[u][:, :, :, :, :], 0.0).then_inc(zeroed, 1)
                pool.memset(vB[u][:, :, :], 0.0).then_inc(zeroed, 1)
                pool.memset(kvb[u][:, :, :], 0.0).then_inc(zeroed, 1)
            pool.memset(mhalf[:, :], -0.5).then_inc(ones_set, 1)
            pool.wait_ge(ones_set, SLOTS + 1)
            for u in range(SLOTS):
                for b in range(2):
                    ones = v2[u][SQ * b:SQ * b + SQ, b, 0:NP_ * 34].rearrange("p (h w) -> p h w", w=17)[:, :, 16:17]
                    pool.memset(ones, 1.0).then_inc(zeroed, 1)
            for u in range(SLOTS):
                pool.sem_inc(pool_.sems[u], len(POOL_STEPS))
            pool.wait_ge(weights_in, 16 * NW)
            with pool.Fori(0, ITERS) as i:
                def rstd(u, n):
                    pool.wait_ge(*dve_.done(u, f"var{n}", i))
                    pool.tensor_tensor(mv[u][:, 3:4], mv[u][:, 2:3], mhalf[:, :], ALU.pow).then_inc(*pool_.tick(u, f"rs{n}"))

                def add_bias(u, n, src, bias):
                    pool.tensor_tensor(xres[u][:, :], src, bias, ALU.add).then_inc(*pool_.tick(u, f"xb{n}"))

                for u in range(SLOTS):
                    rstd(u, 1)
                    add_bias(u, 1, x_in[u][:, :], bo_b[:, :])
                for u in range(SLOTS):
                    rstd(u, 2)
                    add_bias(u, 2, xa[u][:, :], bout_b[:, :])
                for n in (0, 3):
                    for u in range(SLOTS):
                        rstd(u, n)
                for u in range(SLOTS):
                    rstd(u, 4)
                    pool.tensor_tensor(xb[u][:, :], xb[u][:, :], xa[u][:, :], ALU.add).then_inc(*pool_.tick(u, "sum"))

        @block.tensor
        def _(pe):
            for u in range(SLOTS):
                pe.sem_inc(pe_.sems[u], len(PE_STEPS))
            pe.wait_ge(weights_in, 16 * NW)
            pe.wait_ge(zeroed, 1 + 4 * SLOTS + 2 * SLOTS)
            with pe.Fori(0, ITERS) as i:
                def transpose_x(u, name, source, step, engine=dve_):
                    pe.wait_ge(*engine.done(u, step, i, bank=name))
                    if reader_of(name) is not engine:
                        pe.wait_ge(*bank_free(u, name, i))
                    for c in range(C):
                        t = pe.transpose(bank(u, name)[:, c * P:(c + 1) * P], source[:, c * P:(c + 1) * P], ident[:, :])
                    t.then_inc(*pe_.tick(u, name))

                def features(u, name, col, w, w0, rhs, n):
                    for c in range(C):
                        m = pe.matmul(bank(u, name)[:, col:col + n], w[:, c, w0:w0 + P], rhs(c),
                                      start=c == 0, stop=c == C - 1)
                    return m

                def project_out(u, name, w, step, engine):
                    pe.wait_ge(*engine.done(u, step, i, bank=name))
                    if reader_of(name) is not engine:
                        pe.wait_ge(*bank_free(u, name, i))
                    for c in range(C):
                        m = pe.matmul(bank(u, name)[:, 0:D], aT[u][:, c, :], w[:, c, :], start=c == 0, stop=c == C - 1)
                    m.then_inc(*pe_.tick(u, name))

                def a_q(u):
                    transpose_x(u, "xT1", xn[u], "xn1")

                def a_proj(u):
                    pe.wait_ge(*act_.done(u, "xT1", i, bank="q1"))
                    if reader_of("q1") is not act_:
                        pe.wait_ge(*bank_free(u, "q1", i))
                    for c2 in range(C):
                        m = features(u, "q1", c2 * P, Wq, c2 * P, lambda c: xT[u][:, c, :], P)
                    m.then_inc(*pe_.tick(u, "q1"))
                    pe.wait_ge(ctx_loaded[u], (i + 1) * 32)
                    for c2, name in enumerate(("k1a", "k1b")):
                        pe.wait_ge(*bank_free(u, name, i))
                        m = features(u, name, 0, Wk, c2 * P,
                                     lambda c: ctxs[u][:, c, :, :].rearrange("p b k -> p (b k)"), 2 * SK)
                        m.then_inc(*pe_.tick(u, name))
                    for b, name in enumerate(("v1a", "v1b")):
                        pe.wait_ge(*bank_free(u, name, i))
                        for kh in range(2):
                            for c in range(C):
                                m = pe.matmul(bank(u, name)[:, kh * D:(kh + 1) * D],
                                              ctxs[u][:, c, b, kh * P:(kh + 1) * P], Wv[:, c, :],
                                              start=c == 0, stop=c == C - 1)
                        m.then_inc(*pe_.tick(u, name))

                def a_scores(u, p):
                    c, j = divmod(p, 4)
                    pe.wait_ge(*bank_free(u, f"s{p}", i))
                    if p == 0:
                        pe.wait_ge(*act_.done(u, "k1a", i))
                    for b in range(2):
                        m = pe.matmul(bank(u, f"s{p}")[:, b * SK:(b + 1) * SK],
                                      qB[u][:, j, c, b, :, :].rearrange("p h q -> p (h q)"), kT[u][:, c, b, :], start=True, stop=True)
                    m.then_inc(*pe_.tick(u, f"s{p}"))

                def a_probs_t(u, p):
                    pe.wait_ge(*dve_.done(u, f"nrm{p}", i, bank=f"pT{p}"))
                    if reader_of(f"pT{p}") is not dve_:
                        pe.wait_ge(*bank_free(u, f"pT{p}", i))
                    for b in range(2):
                        for kh in range(2):
                            n = 2 * b + kh
                            t = pe.transpose(bank(u, f"pT{p}")[:, n * P:(n + 1) * P],
                                             pb[u][p % 3][:, b, kh * P:(kh + 1) * P], ident[:, :])
                    t.then_inc(*pe_.tick(u, f"pT{p}"))

                def a_pv(u, p):
                    c, j = divmod(p, 4)
                    pe.wait_ge(*act_.done(u, f"pT{p}", i))
                    if p == 0:
                        pe.wait_ge(*dve_.done(u, "v1b", i))
                    for b in range(2):
                        for kh in range(2):
                            n = 2 * c + b
                            m = pe.matmul(psO[u][32 * j:32 * j + 32, n * P:(n + 1) * P],
                                          vS[u][:, b, kh, 32 * p:32 * p + 32], pT[u][p % 2][:, 2 * b + kh, :],
                                          start=kh == 0, stop=kh == 1)
                    m.then_inc(*pe_.tick(u, f"pv{p}"))

                def b_proj(u):
                    pe.wait_ge(*act_.done(u, "xT2", i, bank="qk2"))
                    if reader_of("qk2") is not act_:
                        pe.wait_ge(*bank_free(u, "qk2", i))
                    for n in range(2 * C):
                        m = features(u, "qk2", n * P, Wqkv, n * P, lambda c: xT[u][:, c, :], P)
                    m.then_inc(*pe_.tick(u, "qk2"))
                    pe.wait_ge(*bank_free(u, "v2", i))
                    for c in range(C):
                        m = pe.matmul(bank(u, "v2")[:, 0:D], xT[u][:, c, :], Wqkv[:, c, 2 * D:3 * D],
                                      start=c == 0, stop=c == C - 1)
                    m.then_inc(*pe_.tick(u, "v2"))

                def b_keys(u):
                    for c, name in enumerate(("kpA", "kpB")):
                        pe.wait_ge(*act_.done(u, "qk2", i, bank=name))
                        if reader_of(name) is not act_:
                            pe.wait_ge(*bank_free(u, name, i))
                        pe.matmul(bank(u, name)[:, :], qk[u][:, C + c, :], PB[:, c, :], start=True,
                                  stop=True).then_inc(*pe_.tick(u, name))

                def b_queries(u):
                    for c, name in enumerate(("qpA", "qpB")):
                        pe.wait_ge(*bank_free(u, name, i))
                        for j in range(4):
                            m = pe.matmul(bank(u, name)[:, j * P:(j + 1) * P], PB[:, c, j * P:(j + 1) * P],
                                          qk[u][:, c, :], start=True, stop=True)
                        m.then_inc(*pe_.tick(u, name))

                def b_kv(u):
                    for c, name in enumerate(("kvA", "kvB")):
                        pe.wait_ge(*dve_.done(u, ("kpA", "kpB")[c], i, bank=name))
                        if reader_of(name) is not dve_:
                            pe.wait_ge(*bank_free(u, name, i))
                        for j in range(4):
                            p = 4 * c + j
                            m = pe.matmul(bank(u, name)[:, j * P:(j + 1) * P], kp[u][:, p * P:(p + 1) * P],
                                          v2[u][:, :, 34 * p:34 * p + 64], start=True, stop=True)
                        m.then_inc(*pe_.tick(u, name))

                def b_attend(u):
                    for c, name in enumerate(("aoA", "aoB")):
                        pe.wait_ge(*act_.done(u, "kv", i, bank=name))
                        pe.wait_ge(*dve_.done(u, "kv", i, bank=name))
                        for j in range(4):
                            p = 4 * c + j
                            m = pe.matmul(bank(u, name)[:, j * P:(j + 1) * P], qp[u][:, p * P:(p + 1) * P],
                                          kvb[u][:, :, 34 * p:34 * p + 64], start=True, stop=True)
                        m.then_inc(*pe_.tick(u, name))

                def c_proj(u):
                    pe.wait_ge(*act_.done(u, "xT3", i, bank="qk3"))
                    if reader_of("qk3") is not act_:
                        pe.wait_ge(*bank_free(u, "qk3", i))
                    for n in range(2 * C):
                        m = features(u, "qk3", n * P, Wattn, n * P, lambda c: xT[u][:, c, :], P)
                    m.then_inc(*pe_.tick(u, "qk3"))
                    pe.wait_ge(*bank_free(u, "v3", i))
                    for b in range(2):
                        for half in range(2):
                            for c in range(C):
                                m = pe.matmul(bank(u, "v3")[SQ * half:SQ * half + SQ, b * D:(b + 1) * D],
                                              xT[u][:, c, b * SQ:(b + 1) * SQ], Wattn[:, c, 2 * D:3 * D],
                                              start=c == 0, stop=c == C - 1)
                    m.then_inc(*pe_.tick(u, "v3"))

                def c_scores(u):
                    for c, name in enumerate(("s3A", "s3B")):
                        pe.wait_ge(*act_.done(u, "q3", i, bank=name))
                        pe.wait_ge(*dve_.done(u, "kB", i, bank=name))
                        for b in range(2):
                            m = pe.matmul(bank(u, name)[SQ * b:SQ * b + SQ, :], qs[u][:, c, b * SQ:(b + 1) * SQ],
                                          kB[u][:, c, b, :, :].rearrange("p h k -> p (h k)"), start=True, stop=True)
                        m.then_inc(*pe_.tick(u, name))

                def c_probs_t(u):
                    for c, name in enumerate(("pT3A", "pT3B")):
                        pe.wait_ge(*act_.done(u, ("e3A", "e3B")[c], i, bank=name))
                        if reader_of(name) is not act_:
                            pe.wait_ge(*bank_free(u, name, i))
                        for j in range(4):
                            t = pe.transpose(bank(u, name)[:, j * P:(j + 1) * P], pbf[u][c][:, j * P:(j + 1) * P], ident[:, :])
                        t.then_inc(*pe_.tick(u, name))

                def c_pv(u):
                    for c, name in enumerate(("o3A", "o3B")):
                        pe.wait_ge(*act_.done(u, "pT3A", i, bank=name))
                        pe.wait_ge(*dve_.done(u, ("vB", "pT3B")[c], i, bank=name))
                        for j in range(4):
                            p = 4 * c + j
                            m = pe.matmul(bank(u, name)[:, j * P:(j + 1) * P], pT[u][c][:, j, :],
                                          vB[u][:, :, 32 * p:32 * p + 64], start=True, stop=True)
                        m.then_inc(*pe_.tick(u, name))

                def d_route(u):
                    pe.wait_ge(*act_.done(u, "xT4", i, bank="rt"))
                    if reader_of("rt") is not act_:
                        pe.wait_ge(*bank_free(u, "rt", i))
                    for c in range(C):
                        m = pe.matmul(bank(u, "rt")[:, 0:E], xT[u][:, c, :], Wr[:, c, :], start=c == 0, stop=c == C - 1)
                    m.then_inc(*pe_.tick(u, "rt"))

                def d_up(u, e):
                    pe.wait_ge(*bank_free(u, f"h{e}", i))
                    for f in range(FB):
                        m = features(u, f"h{e}", f * P, W1, e * FF + f * P, lambda c: xT[u][:, c, :], P)
                    m.then_inc(*pe_.tick(u, f"h{e}"))

                def d_down(u, e):
                    pe.wait_ge(*act_.done(u, f"h{e}", i, bank=f"y{e}"))
                    if reader_of(f"y{e}") is not act_:
                        pe.wait_ge(*bank_free(u, f"y{e}", i))
                    for f in range(FB):
                        m = pe.matmul(bank(u, f"y{e}")[:, 0:D], pT[u][e % 2][:, f, :], W2[:, e * FB + f, :],
                                      start=f == 0, stop=f == FB - 1)
                    m.then_inc(*pe_.tick(u, f"y{e}"))

                def both(f, *args):
                    for u in range(SLOTS):
                        f(u, *args)

                both(a_q)
                both(a_proj)
                both(a_scores, 0)
                both(a_scores, 1)
                for p in range(NP_):
                    for u in range(SLOTS):
                        a_probs_t(u, p)
                        if p + 2 < NP_:
                            a_scores(u, p + 2)
                        a_pv(u, p)
                for u in range(SLOTS):
                    project_out(u, "w1", Wo, "o1", dve_)
                both(lambda u: transpose_x(u, "xT2", xn[u], "xn2"))
                both(b_proj)
                both(b_keys)
                both(b_queries)
                both(b_kv)
                both(b_attend)
                both(lambda u: transpose_x(u, "aT2", at[u], "ao"))
                both(lambda u: project_out(u, "w2", Wout, "aT2", act_))
                both(lambda u: transpose_x(u, "xT3", xn[u], "xn3"))
                both(c_proj)
                both(c_scores)
                both(c_probs_t)
                both(c_pv)
                both(lambda u: transpose_x(u, "aT3", at[u], "o3"))
                both(lambda u: project_out(u, "w3", Wproj, "aT3", act_))
                both(lambda u: transpose_x(u, "xT4", xn[u], "xn4"))
                both(d_route)
                both(d_up, 0)
                for e in range(E):
                    for u in range(SLOTS):
                        if e + 1 < E:
                            d_up(u, e + 1)
                        d_down(u, e)

        @block.scalar
        def _(act):
            for u in range(SLOTS):
                act.sem_inc(act_.sems[u], len(ACT_STEPS))
                act.sem_inc(stored[u], 16)
            act.wait_ge(weights_in, 16 * NW)
            act.wait_ge(zeroed, 1 + 4 * SLOTS + 2 * SLOTS)
            with act.Fori(0, ITERS) as i:
                def copy_out(u, name, dst, scale=None):
                    act.wait_ge(*pe_.done(u, name, i))
                    src = bank(u, name)
                    if scale is None:
                        a = act.activation(dst[:, :, :].rearrange("p c t -> p (c t)"), src[:, 0:C * P], ACT.Copy)
                    else:
                        for c in range(C):
                            a = act.activation(dst[:, c, :], src[:, c * P:(c + 1) * P], ACT.Copy, scale=scale[:, c:c + 1])
                    a.then_inc(*act_.tick(u, name))

                def a_q(u):
                    act.wait_ge(*pe_.done(u, "q1", i))
                    for c in range(C):
                        a = act.activation(qs[u][:, c, :], bank(u, "q1")[:, c * P:(c + 1) * P], ACT.Identity,
                                           bias=bqT[:, c:c + 1])
                    a.then_inc(*act_.tick(u, "q1"))
                    act.wait_ge(*pe_.done(u, "k1a", i))
                    act.activation(kT[u][:, 0, :, :].rearrange("p b k -> p (b k)"), bank(u, "k1a")[:, :], ACT.Identity,
                                   bias=bkT[:, 0:1]).then_inc(*act_.tick(u, "k1a"))

                def a_exp(u, p):
                    act.wait_ge(*dve_.done(u, f"nb{p}", i))
                    for b in range(2):
                        n = 2 * p + b
                        a = act.activation(pb[u][p % 3][:, b, :], pb[u][p % 3][:, b, :], ACT.Exp, bias=nb[u][:, n:n + 1],
                                           scale=SCALE, accum_out=su[u][:, n:n + 1])
                    a.then_inc(*act_.tick(u, f"exp{p}"))

                def a_pt(u, p):
                    act.wait_ge(*pe_.done(u, f"pT{p}", i))
                    act.activation(pT[u][p % 2][:, :, :].rearrange("p a b -> p (a b)"), bank(u, f"pT{p}")[:, :],
                                   ACT.Copy).then_inc(*act_.tick(u, f"pT{p}"))

                def b_qk(u):
                    act.wait_ge(*pe_.done(u, "qk2", i))
                    act.activation(qk[u][:, :, :].rearrange("p c t -> p (c t)"), bank(u, "qk2")[:, :],
                                   ACT.Copy).then_inc(*act_.tick(u, "qk2"))

                def b_exp(u, which):
                    for n, half in enumerate("AB"):
                        act.wait_ge(*pe_.done(u, f"{which}p{half}", i))
                        if which == "q":
                            act.wait_ge(*dve_.done(u, f"kp{half}", i))
                        act.activation(pbf[u][n], bank(u, f"{which}p{half}")[:, :],
                                       ACT.Exp).then_inc(*act_.tick(u, f"e{which}{half}"))

                def b_kv(u):
                    act.wait_ge(*pe_.done(u, "kvA", i))
                    src = bank(u, "kvA")[:, :].rearrange("p (j b w) -> p b j w", j=4, b=2)
                    dst = kvb[u][:, :, 0:4 * 34].rearrange("p b (j w) -> p b j w", w=34)
                    for h in range(2):
                        a = act.activation(dst[64 * h:64 * h + 64, :, :, 17 * h:17 * h + 17],
                                           src[64 * h:64 * h + 64, :, :, 17 * h:17 * h + 17], ACT.Copy)
                    a.then_inc(*act_.tick(u, "kv"))

                def c_q(u):
                    act.wait_ge(*pe_.done(u, "qk3", i))
                    act.activation(qs[u][:, :, :].rearrange("p c t -> p (c t)"), bank(u, "qk3")[:, 0:C * P],
                                   ACT.Copy).then_inc(*act_.tick(u, "q3"))

                def c_exp(u):
                    for n, half in enumerate("AB"):
                        act.wait_ge(*dve_.done(u, f"d3{half}", i))
                        act.activation(pbf[u][n], pbf[u][n], ACT.Exp, scale=SCALE).then_inc(*act_.tick(u, f"e3{half}"))

                def c_pt(u):
                    act.wait_ge(*pe_.done(u, "pT3A", i))
                    act.activation(pT[u][0][:, :, :].rearrange("p a b -> p (a b)"), bank(u, "pT3A")[:, :],
                                   ACT.Copy).then_inc(*act_.tick(u, "pT3A"))

                def d_gate(u):
                    act.wait_ge(*dve_.done(u, "dl", i))
                    act.activation(gt[u][:, 32:33], gt[u][:, 24:25], ACT.Exp).then_inc(*act_.tick(u, "eg"))

                def d_gelu(u, e):
                    act.wait_ge(*pe_.done(u, f"h{e}", i))
                    act.activation(pT[u][e % 2][:, :, :].rearrange("p a b -> p (a b)"), bank(u, f"h{e}")[:, :],
                                   ACT.Gelu).then_inc(*act_.tick(u, f"h{e}"))

                def both(f, *args):
                    for u in range(SLOTS):
                        f(u, *args)

                both(lambda u: copy_out(u, "xT1", xT[u]))
                both(a_q)
                both(a_exp, 0)
                for p in range(NP_):
                    for u in range(SLOTS):
                        if p:
                            a_exp(u, p)
                        a_pt(u, p)
                both(lambda u: copy_out(u, "xT2", xT[u]))
                both(b_qk)
                both(b_exp, "k")
                both(b_exp, "q")
                both(b_kv)
                both(lambda u: copy_out(u, "aT2", aT[u]))
                both(lambda u: copy_out(u, "xT3", xT[u], ln1T))
                both(c_q)
                both(c_exp)
                both(c_pt)
                both(lambda u: copy_out(u, "aT3", aT[u]))
                both(lambda u: copy_out(u, "xT4", xT[u], ln2T))
                both(d_gate)
                for e in range(E):
                    both(d_gelu, e)
                for u in range(SLOTS):
                    act.wait_ge(*dve_.done(u, f"y{E - 1}", i))
                    act.dma_start(out[bass.ds((i * SLOTS + u) * P, P), :], acc[u][:, :]).then_inc(stored[u], 16)
            for u in range(SLOTS):
                act.wait_ge(stored[u], 16 * (ITERS + 1))

        @block.vector
        def _(dve):
            for u in range(SLOTS):
                dve.sem_inc(dve_.sems[u], len(DVE_STEPS))
            dve.wait_ge(weights_in, 16 * NW)
            dve.wait_ge(zeroed, 1 + 4 * SLOTS + 2 * SLOTS)
            with dve.Fori(0, ITERS) as i:
                chained = [0] * SLOTS
                CHAIN = 10

                def link(u, ins):
                    ins.then_inc(ln_chain[u], 1)
                    chained[u] += 1
                    dve.wait_ge(ln_chain[u], i * CHAIN + chained[u])

                def stats(u, n, src):
                    dve.sem_inc(wait_taken, 1)
                    link(u, dve.bn_stats(bst[u][:, :], src[:, :]))
                    dve.sem_inc(wait_taken, 1)
                    link(u, dve.bn_aggr(mv[u][:, 0:2], bst[u][:, :]))
                    dve.tensor_scalar(mv[u][:, 2:3], mv[u][:, 1:2], EPS, None, ALU.add).then_inc(*dve_.tick(u, f"var{n}"))

                def normalize(u, n, src):
                    dve.wait_ge(*pool_.done(u, f"rs{n}", i))
                    dve.tensor_scalar(xn[u][:, :], src[:, :], mv[u][:, 0:1], mv[u][:, 3:4], ALU.subtract,
                                      ALU.mult).then_inc(*dve_.tick(u, f"xn{n}"))

                def a_stats(u):
                    dve.wait_ge(x_loaded[u], (i + 1) * 16)
                    stats(u, 1, x_in[u])

                def a_norm(u):
                    dve.wait_ge(*pe_.done_before(u, "xT4", i))
                    normalize(u, 1, x_in[u])
                    dve.wait_ge(mask_loaded[u], (i + 1) * 16)
                    dve.tensor_scalar(madd[u][:, :, :], mraw[u][:, :, :], -NEG, NEG, ALU.mult,
                                      ALU.add).then_inc(*dve_.tick(u, "madd"))

                def a_query(u):
                    dve.wait_ge(*act_.done(u, "q1", i))
                    for j in range(4):
                        r = slice(32 * j, 32 * j + 32)
                        src = qs[u][r, :, :].rearrange("p c (b q) -> p (c b) q", b=2)
                        t = dve.tensor_tensor(qB[u][r, j, :, :, :, :].rearrange("p c b h q -> p (c b) h q"),
                                              src.unsqueeze(2).to_broadcast([32, 4, 2, SQ]),
                                              hmask[r, :].unsqueeze(1).unsqueeze(3).to_broadcast([32, 4, 2, SQ]), ALU.mult)
                    t.then_inc(*dve_.tick(u, "qB"))

                def a_kv(u):
                    dve.wait_ge(*pe_.done(u, "k1b", i))
                    dve.tensor_scalar(kT[u][:, 1, :, :].rearrange("p b k -> p (b k)"), bank(u, "k1b")[:, :],
                                      bkT[:, 1:2], None, ALU.add).then_inc(*dve_.tick(u, "k1b"))
                    for b, name in enumerate(("v1a", "v1b")):
                        dve.wait_ge(*pe_.done(u, name, i))
                        dve.tensor_tensor(vS[u][:, b, :, :], bank(u, name)[:, :].rearrange("p (k n) -> p k n", k=2),
                                          bv_b[:, :].unsqueeze(1).to_broadcast([P, 2, D]),
                                          ALU.add).then_inc(*dve_.tick(u, name))

                def a_max(u, p):
                    dve.wait_ge(*pe_.done(u, f"s{p}", i))
                    dve.sem_inc(wait_taken, 1)
                    for b in range(2):
                        n = 2 * p + b
                        t = dve.tensor_tensor_reduce(pb[u][p % 3][:, b, :], bank(u, f"s{p}")[:, b * SK:(b + 1) * SK],
                                                     madd[u][:, b, :], 1.0, NEG, ALU.add, ALU.max, mx[u][:, n:n + 1])
                    t.then_inc(*dve_.tick(u, f"max{p}"))
                    dve.wait_ge(*dve_.done(u, f"max{p}", i))
                    dve.tensor_scalar(nb[u][:, 2 * p:2 * p + 2], mx[u][:, 2 * p:2 * p + 2], -SCALE, None,
                                      ALU.mult).then_inc(*dve_.tick(u, f"nb{p}"))

                def a_divide(u, p):
                    dve.wait_ge(*act_.done(u, f"exp{p}", i))
                    dve.reciprocal(ri[u][:, 2 * p:2 * p + 2], su[u][:, 2 * p:2 * p + 2]).then_inc(*dve_.tick(u, f"ri{p}"))
                    dve.wait_ge(*dve_.done(u, f"ri{p}", i))
                    for b in range(2):
                        n = 2 * p + b
                        t = dve.tensor_scalar(pb[u][p % 3][:, b, :], pb[u][p % 3][:, b, :], ri[u][:, n:n + 1], None, ALU.mult)
                    t.then_inc(*dve_.tick(u, f"nrm{p}"))

                def a_out(u):
                    dve.wait_ge(*pe_.done(u, f"pv{NP_ - 1}", i))
                    o = psO[u][:, :].rearrange("p (n h q) -> p n h q", n=4, h=2)
                    a = aT[u][:, :, :].rearrange("p c (b q) -> p (c b) q", b=2)
                    dve.tensor_scalar(a, o[:, :, 0, :], hmask[:, 0:1], None, ALU.mult).then_inc(*dve_.tick(u, "o1a"))
                    dve.wait_ge(*dve_.done(u, "o1a", i))
                    dve.scalar_tensor_tensor(out=a, in0=o[:, :, 1, :], scalar=hmask[:, 1:2], in1=a, op0=ALU.mult,
                                             op1=ALU.add).then_inc(*dve_.tick(u, "o1"))

                def add_residual(u, name, group, src, dst, pool_step=None):
                    dve.wait_ge(*pe_.done(u, group, i))
                    if pool_step:
                        dve.wait_ge(*pool_.done(u, pool_step, i))
                    dve.tensor_tensor(dst[:, :], bank(u, group)[:, 0:D], src[:, :], ALU.add).then_inc(*dve_.tick(u, name))
                    dve.wait_ge(*dve_.done(u, name, i))

                def b_value(u):
                    dve.wait_ge(*pe_.done(u, "v2", i))
                    for b in range(2):
                        r = slice(SQ * b, SQ * b + SQ)
                        t = dve.tensor_copy(v2[u][r, b, 0:NP_ * 34].rearrange("p (h w) -> p h w", w=17)[:, :, 0:HD],
                                            bank(u, "v2")[r, 0:D].rearrange("p (h d) -> p h d", d=HD))
                    t.then_inc(*dve_.tick(u, "v2"))

                def b_feature(u, which, dst):
                    for n, half in enumerate("AB"):
                        dve.wait_ge(*act_.done(u, f"e{which}{half}", i))
                        dve.tensor_scalar(pbf[u][n], pbf[u][n], 1.0, None, ALU.min).then_inc(*dve_.tick(u, f"t{which}{half}"))
                        dve.wait_ge(*dve_.done(u, f"t{which}{half}", i))
                        dve.scalar_tensor_tensor(out=dst[:, n * 512:(n + 1) * 512], in0=bank(u, f"{which}p{half}")[:, :],
                                                 scalar=1.0, in1=pbf[u][n], op0=ALU.add,
                                                 op1=ALU.max).then_inc(*dve_.tick(u, f"{which}p{half}"))

                def b_kv(u):
                    dve.wait_ge(*pe_.done(u, "kvB", i))
                    src = bank(u, "kvB")[:, :].rearrange("p (j b w) -> p b j w", j=4, b=2)
                    dst = kvb[u][:, :, 4 * 34:8 * 34].rearrange("p b (j w) -> p b j w", w=34)
                    for h in range(2):
                        t = dve.tensor_copy(dst[64 * h:64 * h + 64, :, :, 17 * h:17 * h + 17],
                                            src[64 * h:64 * h + 64, :, :, 17 * h:17 * h + 17])
                    t.then_inc(*dve_.tick(u, "kv"))

                def b_out(u):
                    dve.wait_ge(*pe_.done(u, "aoB", i))

                    def cols(c, b):
                        o = bank(u, ("aoA", "aoB")[c])[SQ * b:SQ * b + SQ, :].rearrange("p (j b w) -> p j b w", j=4, b=2)
                        return o[:, :, b, 0:34].rearrange("p j (h w) -> p j h w", h=2)

                    for c in range(C):
                        for b in range(2):
                            t = dve.tensor_scalar(su[u][SQ * b:SQ * b + SQ, 8 * c:8 * c + 8].rearrange("p (j h) -> p j h", h=2),
                                                  cols(c, b)[:, :, :, 16], 1e-8, None, ALU.add)
                    t.then_inc(*dve_.tick(u, "den"))
                    dve.wait_ge(*dve_.done(u, "den", i))
                    dve.reciprocal(ri[u][:, :], su[u][:, :]).then_inc(*dve_.tick(u, "rden"))
                    dve.wait_ge(*dve_.done(u, "rden", i))
                    for c in range(C):
                        for b in range(2):
                            r = slice(SQ * b, SQ * b + SQ)
                            t = dve.tensor_tensor(
                                at[u][r, c * P:(c + 1) * P].rearrange("p (j h d) -> p j h d", j=4, h=2), cols(c, b)[:, :, :, 0:HD],
                                ri[u][r, 8 * c:8 * c + 8].rearrange("p (j h) -> p j h", h=2).unsqueeze(3)
                                .to_broadcast([SQ, 4, 2, HD]), ALU.mult)
                    t.then_inc(*dve_.tick(u, "ao"))

                def c_keys(u):
                    dve.wait_ge(*act_.done(u, "q3", i))
                    for j in range(4):
                        r = slice(32 * j, 32 * j + 32)
                        src = bank(u, "qk3")[r, C * P:2 * C * P].rearrange("p (n k) -> p n k", k=SQ)
                        dst = kB[u][r, :, :, 2 * j:2 * j + 2, :].rearrange("p c b h k -> p (c b) h k")
                        t = dve.tensor_tensor(dst, src.unsqueeze(2).to_broadcast([32, 4, 2, SQ]),
                                              hmask[r, :].unsqueeze(1).unsqueeze(3).to_broadcast([32, 4, 2, SQ]), ALU.mult)
                    t.then_inc(*dve_.tick(u, "kB"))

                def c_value(u):
                    dve.wait_ge(*pe_.done(u, "v3", i))
                    src = bank(u, "v3")[:, :].rearrange("p (b j h d) -> p b j h d", b=2, j=NP_, h=2)
                    dst = vB[u][:, :, 0:D].rearrange("p b (j h d) -> p b j h d", j=NP_, h=2)
                    for h in range(2):
                        r = slice(64 * h, 64 * h + 64)
                        t = dve.tensor_copy(dst[r, :, :, h, :], src[r, :, :, h, :])
                    t.then_inc(*dve_.tick(u, "vB"))

                def heads(ap):
                    return ap.rearrange("p (h k) -> p h k", k=SQ)

                def c_max(u):
                    for n, half in enumerate("AB"):
                        dve.wait_ge(*pe_.done(u, f"s3{half}", i))
                        dve.tensor_tensor(heads(pbf[u][n]), heads(bank(u, f"s3{half}")[:, :]),
                                          causal[:, :].unsqueeze(1).to_broadcast([P, 8, SQ]),
                                          ALU.add).then_inc(*dve_.tick(u, f"s3{half}"))
                        dve.wait_ge(*dve_.done(u, f"s3{half}", i))
                        dve.tensor_reduce(mx[u][:, 8 * n:8 * n + 8], heads(pbf[u][n]), AX.X,
                                          ALU.max).then_inc(*dve_.tick(u, f"m3{half}"))
                        dve.wait_ge(*dve_.done(u, f"m3{half}", i))
                        dve.tensor_tensor(heads(pbf[u][n]), heads(pbf[u][n]),
                                          mx[u][:, 8 * n:8 * n + 8].unsqueeze(2).to_broadcast([P, 8, SQ]),
                                          ALU.subtract).then_inc(*dve_.tick(u, f"d3{half}"))

                def c_sum(u):
                    for n, half in enumerate("AB"):
                        dve.wait_ge(*act_.done(u, f"e3{half}", i))
                        dve.tensor_reduce(su[u][:, 8 * n:8 * n + 8], heads(pbf[u][n]), AX.X,
                                          ALU.add).then_inc(*dve_.tick(u, f"sum{half}"))
                    dve.wait_ge(*dve_.done(u, "sumB", i))
                    dve.reciprocal(ri[u][:, :], su[u][:, :]).then_inc(*dve_.tick(u, "r3"))
                    dve.wait_ge(*pe_.done(u, "pT3B", i))
                    dve.tensor_copy(pT[u][1][:, :, :].rearrange("p a b -> p (a b)"),
                                    bank(u, "pT3B")[:, :]).then_inc(*dve_.tick(u, "pT3B"))

                def c_out(u):
                    dve.wait_ge(*pe_.done(u, "o3B", i))
                    for c in range(C):
                        for b in range(2):
                            r = slice(SQ * b, SQ * b + SQ)
                            o = bank(u, ("o3A", "o3B")[c])[r, :].rearrange("p (j b w) -> p j b w", j=4, b=2)
                            t = dve.tensor_tensor(
                                at[u][r, c * P:(c + 1) * P].rearrange("p (j h d) -> p j h d", j=4, h=2),
                                o[:, :, b, 0:32].rearrange("p j (h d) -> p j h d", h=2),
                                ri[u][r, 8 * c:8 * c + 8].rearrange("p (j h) -> p j h", h=2).unsqueeze(3)
                                .to_broadcast([SQ, 4, 2, HD]), ALU.mult)
                    t.then_inc(*dve_.tick(u, "o3"))

                def d_top(u):
                    g = gt[u]
                    dve.wait_ge(*pe_.done(u, "rt", i))
                    dve.tensor_copy(g[:, 0:8], bank(u, "rt")[:, 0:E]).then_inc(*dve_.tick(u, "lg"))
                    dve.wait_ge(*dve_.done(u, "lg", i))
                    dve.sem_inc(wait_taken, 1)
                    dve.max(g[:, 8:16], g[:, 0:8]).then_inc(*dve_.tick(u, "top"))
                    dve.wait_ge(*dve_.done(u, "top", i))
                    dve.sem_inc(wait_taken, 1)
                    dve.max_index(gix[u][:, :], g[:, 8:16], g[:, 0:8]).then_inc(*dve_.tick(u, "ix"))
                    dve.wait_ge(*dve_.done(u, "ix", i))
                    dve.tensor_copy(g[:, 16:24], gix[u][:, :]).then_inc(*dve_.tick(u, "ixf"))
                    dve.tensor_tensor(g[:, 24:25], g[:, 9:10], g[:, 8:9], ALU.subtract).then_inc(*dve_.tick(u, "dl"))

                def d_gate(u):
                    g = gt[u]
                    dve.wait_ge(*act_.done(u, "eg", i))
                    dve.tensor_scalar(g[:, 33:34], g[:, 32:33], 1.0, None, ALU.add).then_inc(*dve_.tick(u, "sg"))
                    dve.wait_ge(*dve_.done(u, "sg", i))
                    dve.reciprocal(g[:, 34:35], g[:, 33:34]).then_inc(*dve_.tick(u, "r4"))
                    dve.wait_ge(*dve_.done(u, "r4", i))
                    dve.tensor_tensor(g[:, 35:36], g[:, 34:35], g[:, 32:33], ALU.mult).then_inc(*dve_.tick(u, "w2nd"))
                    dve.wait_ge(*dve_.done(u, "w2nd", i))
                    dve.tensor_scalar(g[:, 40:48], iota8[:, :], g[:, 17:18], g[:, 35:36], ALU.is_equal,
                                      ALU.mult)
                    dve.tensor_scalar(g[:, 48:56], iota8[:, :], g[:, 16:17], g[:, 34:35], ALU.is_equal,
                                      ALU.mult).then_inc(*dve_.tick(u, "g1"))
                    dve.wait_ge(*dve_.done(u, "g1", i))
                    dve.tensor_tensor(g[:, 56:64], g[:, 48:56], g[:, 40:48], ALU.add).then_inc(*dve_.tick(u, "gate"))

                def d_add(u, e):
                    dve.wait_ge(*pe_.done(u, f"y{e}", i))
                    if e == 0:
                        dve.wait_ge(*dve_.done(u, "gate", i))
                        dve.wait_ge(*pool_.done(u, "sum", i))
                    else:
                        dve.wait_ge(*dve_.done(u, f"y{e - 1}", i))
                    dve.scalar_tensor_tensor(out=acc[u][:, :], in0=bank(u, f"y{e}")[:, 0:D], scalar=gt[u][:, 56 + e:57 + e],
                                             in1=acc[u][:, :], op0=ALU.mult,
                                             op1=ALU.add).then_inc(*dve_.tick(u, f"y{e}"))

                def both(f, *args):
                    for u in range(SLOTS):
                        f(u, *args)

                both(a_stats)
                both(a_norm)
                both(a_query)
                both(a_kv)
                both(a_max, 0)
                for p in range(NP_):
                    for u in range(SLOTS):
                        if p + 1 < NP_:
                            a_max(u, p + 1)
                        a_divide(u, p)
                both(a_out)
                for u in range(SLOTS):
                    add_residual(u, "x1", "w1", xres[u], xa[u], "xb1")
                    stats(u, 2, xa[u])
                for u in range(SLOTS):
                    normalize(u, 2, xa[u])
                both(b_value)
                for u in range(SLOTS):
                    b_feature(u, "k", kp[u])
                for u in range(SLOTS):
                    b_feature(u, "q", qp[u])
                both(b_kv)
                both(b_out)
                for u in range(SLOTS):
                    dve.wait_ge(stored[u], (i + 1) * 16)
                    add_residual(u, "x2", "w2", xres[u], xb[u], "xb2")
                    stats(u, 0, xb[u])
                for u in range(SLOTS):
                    dve.wait_ge(*pool_.done(u, "rs0", i))
                    dve.tensor_scalar(xres[u][:, :], xb[u][:, :], mv[u][:, 0:1], mv[u][:, 3:4], ALU.subtract,
                                      ALU.mult).then_inc(*dve_.tick(u, "h0"))
                    dve.wait_ge(*dve_.done(u, "h0", i))
                    stats(u, 3, xres[u])
                for u in range(SLOTS):
                    normalize(u, 3, xres[u])
                both(c_keys)
                both(c_value)
                both(c_max)
                both(c_sum)
                both(c_out)
                for u in range(SLOTS):
                    add_residual(u, "x3", "w3", xres[u], xa[u])
                    stats(u, 4, xa[u])
                for u in range(SLOTS):
                    normalize(u, 4, xa[u])
                both(d_top)
                both(d_gate)
                for e in range(E):
                    both(d_add, e)
                assert chained == [CHAIN] * SLOTS

    return nc


_INS = ["x", "ctx_1024", "mask_BxS2_bf1", "L0_xattn_Wq", "L0_xattn_bq", "L0_xattn_Wk", "L0_xattn_bk", "L0_xattn_Wv",
        "L0_xattn_bv", "L0_xattn_Wo", "L0_xattn_bo", "L0_attn_w_qkv", "L0_attn_proj_matrix", "L0_attn_w_out",
        "L0_attn_b_out", "L0_ffn_ln1_w", "L0_ffn_c_attn_w", "L0_ffn_c_proj_w", "L0_ffn_ln2_w", "L0_ffn_router_w",
        "L0_ffn_w1", "L0_ffn_w2"]


def kernel(**inputs):
    import concourse.bacc as bacc
    from concourse.bass_utils import run_bass_kernel_spmd

    arrays = {n: np.ascontiguousarray(inputs[n]) for n in _INS}
    arrays["x"] = arrays["x"].reshape(B * SQ, D)
    arrays["ctx_1024"] = np.ascontiguousarray(arrays["ctx_1024"].transpose(0, 2, 1)).reshape(B * D, SK)
    q = np.arange(P) % SQ
    arrays["ident"] = np.eye(P, dtype=np.float32)
    arrays["hmask"] = (np.arange(P)[:, None] // HD % 2 == np.arange(2)[None, :]).astype(np.float32)
    arrays["causal"] = np.where(np.arange(SQ)[None, :] > q[:, None], NEG, 0.0).astype(np.float32)
    arrays["iota8"] = np.tile(np.arange(E, dtype=np.float32), (P, 1))

    nc = bacc.Bacc("TRN2", target_bir_lowering=False, num_devices=1)
    aps = [nc.dram_tensor(f"in_{n}", a.shape, mybir.dt.from_np(a.dtype), kind="ExternalInput").ap()
           for n, a in arrays.items()]
    out = nc.dram_tensor("out_0", (B * SQ, D), F32, kind="ExternalOutput").ap()
    build(nc, *aps, out)
    r = run_bass_kernel_spmd(nc, [{f"in_{n}": a for n, a in arrays.items()}], core_ids=[0])
    return r.results[0]["out_0"].reshape(B, SQ, D)
```

```python
from contextlib import ExitStack

import concourse.bass as bass
from concourse import mybir
import numpy as np

F32 = mybir.dt.float32
U32 = mybir.dt.uint32
BF16 = mybir.dt.bfloat16
U8 = mybir.dt.uint8
ALU = mybir.AluOpType
ACT = mybir.ActivationFunctionType
AX = mybir.AxisListType

P = 128
B, SQ, D = 64, 64, 256
SK = 256
NH, HD = 16, 16
C = D // P
NP_ = NH // 2
FEAT = 64
E, FF = 8, 512
FB = FF // P
TILES = B * SQ // P
SLOTS = 2
ITERS = TILES // SLOTS
TOP = 2
ROWS = TOP * B * SQ
BLOCKS = ROWS // P + E
XW = D + 4
NOWHERE = 1 << 20
ESLOTS = 4
SCALE = float(HD) ** -0.5
EPS = 1e-5
NEG = -3.4e38
RING = 3


PE_STEPS = (["k1a", "k1b", "v1a", "v1b", "xT1", "q1", "s0", "s1"]
            + [n for p in range(NP_) for n in (([f"s{p + 2}"] if p + 2 < NP_ else []) + [f"pT{p}"] + ([f"pv{p - 1}"] if p else []))]
            + [f"pv{NP_ - 1}", "w1"]
            + ["xT2", "qk2", "v2", "kpA", "kpB", "qpA", "qpB", "kvA", "kvB", "aoA", "aoB", "aT2", "w2"]
            + ["xT3", "qk3", "v3", "s3A", "s3B", "pT3A", "pT3B", "o3A", "o3B", "aT3", "w3"]
            + ["xT4", "rt", "rk"])

ACT_STEPS = (["k1a", "k1b", "v1a", "v1b", "xT1", "q1", "qB", "exp0"] + [n for p in range(NP_) for n in (([f"exp{p + 1}"] if p + 1 < NP_ else []) + [f"pT{p}"])]
             + ["xT2", "qk2", "ekA", "ekB", "eqA", "eqB", "kv", "aT2"]
             + ["xT3", "qk3", "kB", "e3A", "e3B", "pT3A", "pT3B", "aT3"]
             + ["xT4", "eg"])

DVE_STEPS = (["var1", "xn1", "madd", "qB", "max0", "nb0", "max1", "nb1"]
             + [n for p in range(NP_) for n in ([f"ri{p}", f"nrm{p}"]
                                                + ([f"max{p + 2}", f"nb{p + 2}"] if p + 2 < NP_ else []))]
             + ["o1a", "o1", "x1"]
             + ["var2", "xn2", "v2", "tkA", "kpA", "tkB", "kpB", "tqA", "qpA", "tqB", "qpB", "kv",
                "den", "rden", "ao", "x2", "var0", "h0"]
             + ["var3", "xn3", "kB", "vB", "s3A", "m3A", "d3A", "s3B", "m3B", "d3B", "sumA", "sumB", "r3", "o3", "x3"]
             + ["var4", "xn4", "lg", "top", "ix", "ixf", "oh", "dl", "gate", "rk", "meta"])

POOL_STEPS = ["rs1", "xb1", "rs2", "xb2", "rs0", "rs3", "rs4", "sum", "copy", "sent"]

EPE_STEPS = ["xT", "up", "hT", "down"]
EACT_STEPS = ["xT", "gelu"]
EDVE_STEPS = ["hT", "y"]
EPOOL_STEPS = ["sent"]

GROUPS = ([("k1a", "act", "k1a"), ("k1b", "act", "k1b"), ("v1a", "act", "v1a"), ("v1b", "act", "v1b"),
           ("xT1", "act", "xT1"), ("q1", "act", "q1"), ("s0", "dve", "max0"), ("s1", "dve", "max1")]
          + [n for p in range(NP_) for n in (([(f"s{p + 2}", "dve", f"max{p + 2}")] if p + 2 < NP_ else [])
                                             + [(f"pT{p}", "act", f"pT{p}")])]
          + [("w1", "dve", "x1")]
          + [("xT2", "act", "xT2"), ("qk2", "act", "qk2"), ("v2", "dve", "v2"), ("kpA", "dve", "kpA"),
             ("kpB", "dve", "kpB"), ("qpA", "dve", "qpA"), ("qpB", "dve", "qpB"), ("kvA", "act", "kv"),
             ("kvB", "dve", "kv"), ("aoA", "dve", "ao"), ("aoB", "dve", "ao"), ("aT2", "act", "aT2"),
             ("w2", "dve", "x2")]
          + [("xT3", "act", "xT3"), ("qk3", "act", "qk3"), ("v3", "dve", "vB"), ("s3A", "dve", "s3A"),
             ("s3B", "dve", "s3B"), ("pT3A", "act", "pT3A"), ("pT3B", "act", "pT3B"), ("o3A", "dve", "o3"),
             ("o3B", "dve", "o3"), ("aT3", "act", "aT3"), ("w3", "dve", "x3")]
          + [("xT4", "act", "xT4"), ("rt", "dve", "lg"), ("rk", "dve", "rk")])
GROUP_AT = {name: n for n, (name, _, _) in enumerate(GROUPS)}


class Progress:

    def __init__(self, name, sems, steps):
        self.name, self.sems, self.steps, self.at = name, sems, steps, [0] * len(sems)
        self.credits = [(1 + 3 * u) * len(steps) for u in range(len(sems))]
        assert len(set(steps)) == len(steps)

    def tick(self, u, name):
        assert self.steps[self.at[u] % len(self.steps)] == name, (name, self.steps[self.at[u] % len(self.steps)])
        self.at[u] += 1
        return self.sems[u], 1

    def done(self, u, name, i, bank=None):
        count = self.steps.index(name)
        if bank is not None and engine_that_reads(bank) == self.name:
            count = max(count, freed_at(bank, self.steps))
        return self.sems[u], i * len(self.steps) + self.credits[u] + count + 1

    def done_before(self, u, name, i):
        return self.sems[u], i * len(self.steps) + self.credits[u] - len(self.steps) + self.steps.index(name) + 1


def bank_before(group):
    n = GROUP_AT[group]
    return n - RING if n >= RING else max(m for m in range(len(GROUPS)) if m % RING == n)


def engine_that_reads(group):
    return GROUPS[bank_before(group)][1]


def freed_at(group, steps):
    return (0 if GROUP_AT[group] >= RING else -len(steps)) + steps.index(GROUPS[bank_before(group)][2])


def build(nc, x, ctxT, mask, wq, bq, wk, bk, wv, bv, wo, bo, wqkv, proj, wout, bout, ln1, wattn, wproj, ln2,
          router, w1, w2, ident_d, hmask_d, causal_d, iota_d, before_d, earlier_d, row_d, dst_d, sorted_d, base_d, result_d, out):
    with ExitStack() as ctx:
        def sb(name, shape, dt=F32):
            return ctx.enter_context(nc.sbuf_tensor(name, shape, dt))

        def per_slot(name, shape, dt=F32):
            return [sb(f"{name}_{u}", shape, dt) for u in range(SLOTS)]

        def sem(name):
            return ctx.enter_context(nc.semaphore(name))

        ident = sb("ident", [P, P])
        hmask = sb("hmask", [P, 2])
        causal = sb("causal", [P, SQ])
        iota8 = sb("iota8", [P, E])
        Wq, Wk, Wv, Wo = (sb(n, [P, C, D]) for n in ("Wq", "Wk", "Wv", "Wo"))
        Wqkv, Wattn = (sb(n, [P, C, 3 * D]) for n in ("Wqkv", "Wattn"))
        Wout, Wproj = (sb(n, [P, C, D]) for n in ("Wout", "Wproj"))
        PB = sb("PB", [P, C, 8 * FEAT])
        Wr = sb("Wr", [P, C, E])
        before = sb("before", [P, P], BF16)
        ones_b = sb("ones_b", [P, P], BF16)
        earlier = sb("earlier", [P, E, E])
        W1 = sb("W1", [P, C, E * FF])
        W2 = sb("W2", [P, E * FB, D])
        bqT, bkT, bvT, ln1T, ln2T = (sb(n, [P, C]) for n in ("bqT", "bkT", "bvT", "ln1T", "ln2T"))
        bo_b, bout_b = (sb(n, [P, D]) for n in ("bo_b", "bout_b"))
        mhalf = sb("mhalf", [P, 1])

        x_in = per_slot("x_in", [P, D])
        ctxs = per_slot("ctxs", [P, C, 2, SK])
        mraw = per_slot("mraw", [P, 2, SK], U8)
        madd = per_slot("madd", [P, 2, SK])
        bst = per_slot("bst", [P, 6])
        mv = per_slot("mv", [P, 4])
        xn = per_slot("xn", [P, D])
        xT = per_slot("xT", [P, C, P])
        xres = per_slot("xres", [P, D])
        xa = per_slot("xa", [P, D])
        xb = per_slot("xb", [P, XW])
        qs = per_slot("qs", [P, C, P])
        qB = per_slot("qB", [P, 4, C, 2, 2, SQ])
        kT = per_slot("kT", [P, C, 2, SK])
        vS = per_slot("vS", [P, 2, 2, D])
        pb = [[sb(f"pb{r}_{u}", [P, 2, SK]) for r in range(3)] for u in range(SLOTS)]
        pT = [[sb(f"pT{r}_{u}", [P, 4, P]) for r in range(2)] for u in range(SLOTS)]
        mx = per_slot("mx", [P, 2 * NP_])
        nb = per_slot("nb", [P, 2 * NP_])
        su = per_slot("su", [P, 2 * NP_])
        ri = per_slot("ri", [P, 2 * NP_])
        aT = qs
        at = xn
        qk = [pb[u][2][:, :, :].rearrange("p b (c t) -> p (b c) t", t=P) for u in range(SLOTS)]
        VW = NP_ * 34 + 30
        v2 = per_slot("v2", [P, 2, VW])
        kvb = per_slot("kvb", [P, 2, VW])
        kB = per_slot("kB", [P, C, 2, 8, SQ])
        vB = per_slot("vB", [P, 2, D + 32])
        gt = per_slot("gt", [P, 64])
        gix = per_slot("gix", [P, 8], U32)
        oh = per_slot("oh", [P, TOP * E])
        ohb = per_slot("ohb", [P, TOP * E], BF16)
        rk = per_slot("rk", [P, 2 * TOP * E])
        cum8 = [pb[u][0][:, 0, 0:E * E].rearrange("p (a b) -> p a b", a=E) for u in range(SLOTS)]
        sc = [pb[u][0][:, 1, :] for u in range(SLOTS)]
        pos = per_slot("pos", [P, TOP], U32)
        dst = per_slot("dst", [P, TOP])
        used = sb("used", [P, E])
        first = sb("first", [P, E])
        unused = sb("unused", [P, 1])
        kp = [kT[u][:, :, :, :].rearrange("p a b c -> p (a b c)") for u in range(SLOTS)]
        qp = [vS[u][:, :, :, :].rearrange("p a b c -> p (a b c)") for u in range(SLOTS)]
        xr = [[pb[u][2][:, :, :].rearrange("p a b -> p (a b)")[:, 0:XW],
               pT[u][1][:, :, :].rearrange("p a b -> p (a b)")[:, 0:XW]] for u in range(SLOTS)]
        pbf = [[pb[u][r][:, :, :].rearrange("p a b -> p (a b)") for r in range(3)] for u in range(SLOTS)]

        ring = [[ctx.enter_context(nc.psum_tensor(f"ring{r}_{u}", [P, 512], F32)) for r in range(RING)]
                for u in range(SLOTS)]
        psO = [ctx.enter_context(nc.psum_tensor(f"psO_{u}", [P, 512], F32)) for u in range(SLOTS)]

        def half_of(flat, h, n):
            return flat[:, h * n:(h + 1) * n]

        VS = [(v % SLOTS, v // SLOTS) for v in range(ESLOTS)]
        xs = [half_of(ctxs[u][:, :, :, :].rearrange("p a b c -> p (a b c)"), h, XW) for u, h in VS]
        xTe = [(xT[u], qs[u])[h] for u, h in VS]
        he = [pbf[u][h] for u, h in VS]
        hTe = [pT[u][h] for u, h in VS]
        ye = [(x_in[u], xres[u])[h] for u, h in VS]
        where = [sb(f"where_{v}", [P, 1], U32) for v in range(ESLOTS)]
        yd = [half_of(kT[u][:, :, :, :].rearrange("p a b c -> p (a b c)"), h, TOP * D) for u, h in VS]
        bd = [half_of(vS[u][:, :, :, :].rearrange("p a b c -> p (a b c)"), h, XW) for u, h in VS]
        banks = [b for u in range(SLOTS) for b in ring[u] + [psO[u]]]
        ebank = [banks[2 * v:2 * v + 2] for v in range(ESLOTS)]

        weights_in = sem("weights_in")
        experts_in = sem("experts_in")
        rows_cleared = sem("rows_cleared")
        rows_sent = [sem(f"rows_sent{u}") for u in range(SLOTS)]
        block_loaded = [sem(f"block_loaded{v}") for v in range(ESLOTS)]
        result_sent = [sem(f"result_sent{v}") for v in range(ESLOTS)]
        tile_loaded = [sem(f"tile_loaded{v}") for v in range(ESLOTS)]
        first_added = [sem(f"first_added{v}") for v in range(ESLOTS)]
        second_added = [sem(f"second_added{v}") for v in range(ESLOTS)]
        out_stored = [sem(f"out_stored{v}") for v in range(ESLOTS)]
        state_set = sem("state_set")
        dst_moved = [sem(f"dst_moved{u}") for u in range(SLOTS)]
        epe_ = Progress("pe", [sem(f"expert_pe_steps{v}") for v in range(ESLOTS)], EPE_STEPS)
        eact_ = Progress("act", [sem(f"expert_act_steps{v}") for v in range(ESLOTS)], EACT_STEPS)
        edve_ = Progress("dve", [sem(f"expert_dve_steps{v}") for v in range(ESLOTS)], EDVE_STEPS)
        epool_ = Progress("pool", [sem(f"expert_pool_steps{v}") for v in range(ESLOTS)], EPOOL_STEPS)
        zeroed = sem("zeroed")
        ones_set = sem("ones_set")
        x_loaded = [sem(f"x_loaded{u}") for u in range(SLOTS)]
        ctx_loaded = [sem(f"ctx_loaded{u}") for u in range(SLOTS)]
        mask_loaded = [sem(f"mask_loaded{u}") for u in range(SLOTS)]
        stored = [sem(f"stored{u}") for u in range(SLOTS)]
        wait_taken = sem("wait_taken")
        sp_wait_taken = sem("sp_wait_taken")
        pool_wait_taken = sem("pool_wait_taken")
        chain_links = [sem(f"chain_links{u}") for u in range(SLOTS)]
        pe_ = Progress("pe", [sem(f"pe_steps{u}") for u in range(SLOTS)], PE_STEPS)
        act_ = Progress("act", [sem(f"act_steps{u}") for u in range(SLOTS)], ACT_STEPS)
        dve_ = Progress("dve", [sem(f"dve_steps{u}") for u in range(SLOTS)], DVE_STEPS)
        pool_ = Progress("pool", [sem(f"pool_steps{u}") for u in range(SLOTS)], POOL_STEPS)
        engine_of = {"act": act_, "dve": dve_}

        def bank(u, name):
            return ring[u][GROUP_AT[name] % RING]

        def reader_of(name):
            return engine_of[engine_that_reads(name)]

        def bank_free(u, name, i):
            engine = reader_of(name)
            return engine.sems[u], i * len(engine.steps) + engine.credits[u] + freed_at(name, engine.steps) + 1

        CHAIN = 10 + 21

        ITERS_WRITTEN = 2

        def in_turn(engine, half):
            half(0, 0, None, None)
            with engine.Fori(0, ITERS - 1) as i:
                half(1, i, 0, i)
                half(0, i + 1, 1, i)
            half(1, ITERS - 1, 0, ITERS - 1)
            half(None, None, 1, ITERS - 1)

        block = ctx.enter_context(nc.Block())

        loads = [
            (ident[:, :], ident_d), (hmask[:, :], hmask_d), (causal[:, :], causal_d),
            (iota8[:, :], iota_d), (before[:, :], before_d), (earlier[:, :, :], earlier_d),
            *((dst[u][:, :], dst_d[u]) for u in range(SLOTS)),
            (Wq[:, :, :], wq.rearrange("(c p) n -> p c n", p=P)),
            (bqT[:, :], bq.rearrange("(c p) -> p c", p=P)),
            (Wk[:, :, :], wk.rearrange("(c p) n -> p c n", p=P)),
            (bkT[:, :], bk.rearrange("(c p) -> p c", p=P)),
            (Wv[:, :, :], wv.rearrange("(c p) n -> p c n", p=P)),
            (bvT[:, :], bv.rearrange("(c p) -> p c", p=P)),
            (bo_b[:, :], bo.rearrange("(o n) -> o n", o=1).to_broadcast([P, D])),
            (Wo[:, :, :], wo.rearrange("(c p) n -> p c n", p=P)),
            (Wqkv[:, :, :], wqkv.rearrange("(c p) n -> p c n", p=P)),
            (Wout[:, :, :], wout.rearrange("(c p) n -> p c n", p=P)),
            (bout_b[:, :], bout.rearrange("(o n) -> o n", o=1).to_broadcast([P, D])),
            (ln1T[:, :], ln1.rearrange("(c p) -> p c", p=P)),
            (Wattn[:, :, :], wattn.rearrange("(c p) n -> p c n", p=P)),
            (Wproj[:, :, :], wproj.rearrange("(c p) n -> p c n", p=P)),
            (ln2T[:, :], ln2.rearrange("(c p) -> p c", p=P)),
            (Wr[:, :, :], router.rearrange("(c p) n -> p c n", p=P)),
        ]
        NW = len(loads) + NH

        @block.sync
        def _(sp):
            with nc.allow_non_contiguous_dma(reason="biases laid along partitions, once"):
                for dst, src in loads:
                    sp.dma_start(dst, src).then_inc(weights_in, 16)
            sp.wait_ge(zeroed, 1)
            for h in range(NH):
                r = HD * (h % 8)
                sp.dma_start(PB[r:r + HD, h // 8, FEAT * (h % 8):FEAT * (h % 8) + FEAT], proj[h]).then_inc(weights_in, 16)
            sp.wait_ge(weights_in, 16 * NW)
            sp.dma_start(sorted_d.rearrange("(s p) n -> s p n", p=P),
                         row_d.unsqueeze(0).to_broadcast([BLOCKS, P, XW])).then_inc(rows_cleared, 16)
            sp.dma_start(W1[:, :, :], w1.rearrange("(c p) n -> p c n", p=P)).then_inc(experts_in, 16)
            sp.dma_start(W2[:, :, :], w2.rearrange("(f p) n -> p f n", p=P)).then_inc(experts_in, 16)
            with sp.Fori(0, ITERS) as i:
                for u in range(SLOTS):
                    sp.wait_ge(*dve_.done_before(u, "xn1", i))
                    sp.sem_inc(sp_wait_taken, 1)
                    sp.wait_ge(*pool_.done_before(u, "xb1", i))
                    sp.sem_inc(sp_wait_taken, 1)
                    sp.dma_start(x_in[u][:, :], x[bass.ds((i * SLOTS + u) * P, P), :]).then_inc(x_loaded[u], 16)
                    sp.wait_ge(*dve_.done_before(u, "madd", i))
                    sp.sem_inc(sp_wait_taken, 1)
                    sp.dma_start(mraw[u][:, :, :],
                                 mask[bass.ds((i * SLOTS + u) * 2, 2), :].rearrange("(o b) k -> o b k", o=1)
                                 .to_broadcast([P, 2, SK])).then_inc(mask_loaded[u], 16)
                    sp.wait_ge(*pe_.done_before(u, "v1b", i))
                    sp.sem_inc(sp_wait_taken, 1)
                    for b in range(2):
                        sp.dma_start(ctxs[u][:, :, b, :],
                                     ctxT[bass.ds(((i * SLOTS + u) * 2 + b) * D, D), :]
                                     .rearrange("(c p) k -> p c k", p=P)).then_inc(ctx_loaded[u], 16)
            for u in range(SLOTS):
                sp.wait_ge(*pool_.done(u, "sent", ITERS - 1))
            with sp.Fori(0, BLOCKS // ESLOTS) as i:
                for v in range(ESLOTS):
                    sp.wait_ge(*edve_.done_before(v, "y", i))
                    sp.sem_inc(sp_wait_taken, 1)
                    sp.dma_start(xs[v], sorted_d[bass.ds((i * ESLOTS + v) * P, P), :]).then_inc(block_loaded[v], 16)
            for v in range(ESLOTS):
                sp.wait_ge(*epool_.done(v, "sent", BLOCKS // ESLOTS - 1))
            for u in range(SLOTS):
                sp.wait_ge(stored[u], 16 * (ITERS + 1))
            with sp.Fori(0, TILES // ESLOTS) as i:
                for v in range(ESLOTS):
                    sp.wait_ge(out_stored[v], 16 * (i + 1))
                    sp.sem_inc(sp_wait_taken, 1)
                    t = i * ESLOTS + v
                    sp.dma_start(bd[v], base_d[bass.ds(t * P, P), :]).then_inc(tile_loaded[v], 16)
                    sp.dma_start(yd[v].rearrange("p (k n) -> p k n", k=TOP),
                                 result_d[bass.ds(t * P * TOP, P * TOP), :].rearrange("(p k) n -> p k n", k=TOP)).then_inc(tile_loaded[v], 16)

        @block.gpsimd
        def _(pool):
            pool.memset(PB[:, :, :], 0.0).then_inc(zeroed, 1)
            for u in range(SLOTS):
                pool.memset(v2[u][:, :, :], 0.0).then_inc(ones_set, 1)
                pool.memset(qB[u][:, :, :, :, :, :], 0.0).then_inc(zeroed, 1)
                pool.memset(kB[u][:, :, :, :, :], 0.0).then_inc(zeroed, 1)
                pool.memset(vB[u][:, :, :], 0.0).then_inc(zeroed, 1)
                pool.memset(kvb[u][:, :, :], 0.0).then_inc(zeroed, 1)
            for u in range(SLOTS):
                pool.memset(xb[u][:, D:XW], 0.0).then_inc(state_set, 1)
            pool.memset(ones_b[:, :], 1.0).then_inc(state_set, 1)
            pool.memset(used[:, :], float(P)).then_inc(state_set, 1)
            pool.memset(first[:, :], 0.0).then_inc(state_set, 1)
            pool.memset(unused[:, :], 0.0).then_inc(state_set, 1)
            pool.memset(mhalf[:, :], -0.5).then_inc(ones_set, 1)
            pool.wait_ge(ones_set, SLOTS + 1)
            for u in range(SLOTS):
                for b in range(2):
                    ones = v2[u][SQ * b:SQ * b + SQ, b, 0:NP_ * 34].rearrange("p (h w) -> p h w", w=17)[:, :, 16:17]
                    pool.memset(ones, 1.0).then_inc(zeroed, 1)
            for u in range(SLOTS):
                pool.sem_inc(pool_.sems[u], pool_.credits[u])
            for v in range(ESLOTS):
                pool.sem_inc(epool_.sems[v], epool_.credits[v])
            pool.wait_ge(weights_in, 16 * NW)
            def rstd(u, i, n):
                pool.wait_ge(*dve_.done(u, f"var{n}", i))
                pool.tensor_tensor(mv[u][:, 3:4], mv[u][:, 2:3], mhalf[:, :], ALU.pow).then_inc(*pool_.tick(u, f"rs{n}"))

            def add_bias(u, i, n, src, bias):
                pool.tensor_tensor(xres[u][:, :], src[u][:, :], bias[:, :], ALU.add).then_inc(*pool_.tick(u, f"xb{n}"))

            def add_blocks(u, i):
                pool.tensor_tensor(xb[u][:, 0:D], xb[u][:, 0:D], xa[u][:, :], ALU.add).then_inc(*pool_.tick(u, "sum"))

            def copy_rows(u, i):
                pool.wait_ge(*dve_.done(u, "xn4", i))
                pool.sem_inc(pool_wait_taken, 1)
                pool.tensor_copy(xr[u][1][:, 0:D], xr[u][0][:, 0:D]).then_inc(*pool_.tick(u, "copy"))

            def sort_rows(u, i):
                pool.wait_ge(*dve_.done(u, "meta", i))
                pool.wait_ge(*pool_.done(u, "copy", i))
                pool.wait_ge(rows_cleared, 16)
                pool.sem_inc(pool_wait_taken, 1)
                for k in range(TOP):
                    pool.indirect_dma_start(sorted_d, bass.IndirectOffsetOnAxis(ap=pos[u][:, k:k + 1], axis=0),
                                            xr[u][k], None).then_inc(rows_sent[u], 16)
                pool.wait_ge(rows_sent[u], (i + 1) * (16 * TOP))
                pool.sem_inc(*pool_.tick(u, "sent"))

            def half(f, fi, s, si):
                def first(step, *args):
                    if f is not None:
                        step(f, fi, *args)

                def second(step, *args):
                    if s is not None:
                        step(s, si, *args)

                first(rstd, 1)
                first(add_bias, 1, x_in, bo_b)
                second(rstd, 0)
                second(rstd, 3)
                second(rstd, 4)
                second(add_blocks)
                first(rstd, 2)
                first(add_bias, 2, xa, bout_b)
                second(copy_rows)
                second(sort_rows)

            in_turn(pool, half)
            with pool.Fori(0, BLOCKS // ESLOTS) as i:
                def send(v):
                    pool.wait_ge(*edve_.done(v, "y", i))
                    pool.sem_inc(pool_wait_taken, 1)
                    pool.indirect_dma_start(result_d, bass.IndirectOffsetOnAxis(ap=where[v][:, 0:1], axis=0), ye[v][:, :], None,
                                            bounds_check=ROWS - 1, oob_is_err=False).then_inc(result_sent[v], 16)

                def sent(v):
                    pool.wait_ge(result_sent[v], 16 * (i + 1))
                    pool.sem_inc(*epool_.tick(v, "sent"))

                send(0)
                for v in range(1, ESLOTS):
                    send(v)
                    sent(v - 1)
                sent(ESLOTS - 1)

        @block.tensor
        def _(pe):
            for u in range(SLOTS):
                pe.sem_inc(pe_.sems[u], pe_.credits[u])
            for v in range(ESLOTS):
                pe.sem_inc(epe_.sems[v], epe_.credits[v])
            pe.wait_ge(weights_in, 16 * NW)
            pe.wait_ge(state_set, SLOTS + 4)
            pe.wait_ge(zeroed, 1 + 4 * SLOTS + 2 * SLOTS)
            def transpose_x(u, i, name, source, step, engine=dve_):
                pe.wait_ge(*engine.done(u, step, i, bank=name))
                if reader_of(name) is not engine:
                    pe.wait_ge(*bank_free(u, name, i))
                for c in range(C):
                    t = pe.transpose(bank(u, name)[:, c * P:(c + 1) * P], source[:, c * P:(c + 1) * P], ident[:, :])
                t.then_inc(*pe_.tick(u, name))

            def features(u, name, col, w, w0, rhs, n):
                for c in range(C):
                    m = pe.matmul(bank(u, name)[:, col:col + n], w[:, c, w0:w0 + P], rhs(c),
                                  start=c == 0, stop=c == C - 1)
                return m

            def project_out(u, i, name, w, step, engine):
                pe.wait_ge(*engine.done(u, step, i, bank=name))
                if reader_of(name) is not engine:
                    pe.wait_ge(*bank_free(u, name, i))
                for c in range(C):
                    m = pe.matmul(bank(u, name)[:, 0:D], aT[u][:, c, :], w[:, c, :], start=c == 0, stop=c == C - 1)
                m.then_inc(*pe_.tick(u, name))

            def a_keys(u, i):
                pe.wait_ge(ctx_loaded[u], (i + 1) * 32)
                for c2, name in enumerate(("k1a", "k1b")):
                    pe.wait_ge(*bank_free(u, name, i))
                    m = features(u, name, 0, Wk, c2 * P,
                                 lambda c: ctxs[u][:, c, :, :].rearrange("p b k -> p (b k)"), 2 * SK)
                    m.then_inc(*pe_.tick(u, name))

            def a_values(u, i):
                for b, name in enumerate(("v1a", "v1b")):
                    pe.wait_ge(*bank_free(u, name, i))
                    for kh in range(2):
                        for c in range(C):
                            m = pe.matmul(bank(u, name)[:, kh * D:(kh + 1) * D],
                                          ctxs[u][:, c, b, kh * P:(kh + 1) * P], Wv[:, c, :],
                                          start=c == 0, stop=c == C - 1)
                    m.then_inc(*pe_.tick(u, name))

            def a_x_t(u, i):
                transpose_x(u, i, "xT1", xn[u], "xn1")

            def a_q(u, i):
                pe.wait_ge(*act_.done(u, "xT1", i, bank="q1"))
                if reader_of("q1") is not act_:
                    pe.wait_ge(*bank_free(u, "q1", i))
                for c2 in range(C):
                    m = features(u, "q1", c2 * P, Wq, c2 * P, lambda c: xT[u][:, c, :], P)
                m.then_inc(*pe_.tick(u, "q1"))

            def a_scores(u, i, p):
                c, j = divmod(p, 4)
                if p == 0:
                    pe.wait_ge(*act_.done(u, "qB", i, bank="s0"))
                    pe.wait_ge(*dve_.done(u, "qB", i, bank="s0"))
                else:
                    pe.wait_ge(*bank_free(u, f"s{p}", i))
                for b in range(2):
                    m = pe.matmul(bank(u, f"s{p}")[:, b * SK:(b + 1) * SK],
                                  qB[u][:, j, c, b, :, :].rearrange("p h q -> p (h q)"), kT[u][:, c, b, :], start=True, stop=True)
                m.then_inc(*pe_.tick(u, f"s{p}"))

            def a_probs_t(u, i, p):
                pe.wait_ge(*dve_.done(u, f"nrm{p}", i, bank=f"pT{p}"))
                if reader_of(f"pT{p}") is not dve_:
                    pe.wait_ge(*bank_free(u, f"pT{p}", i))
                for b in range(2):
                    for kh in range(2):
                        n = 2 * b + kh
                        t = pe.transpose(bank(u, f"pT{p}")[:, n * P:(n + 1) * P],
                                         pb[u][p % 3][:, b, kh * P:(kh + 1) * P], ident[:, :])
                t.then_inc(*pe_.tick(u, f"pT{p}"))

            def a_pv(u, i, p):
                c, j = divmod(p, 4)
                pe.wait_ge(*act_.done(u, f"pT{p}", i))
                for b in range(2):
                    for kh in range(2):
                        n = 2 * c + b
                        m = pe.matmul(psO[u][32 * j:32 * j + 32, n * P:(n + 1) * P],
                                      vS[u][:, b, kh, 32 * p:32 * p + 32], pT[u][p % 2][:, 2 * b + kh, :],
                                      start=kh == 0, stop=kh == 1)
                m.then_inc(*pe_.tick(u, f"pv{p}"))

            def b_proj(u, i):
                pe.wait_ge(*act_.done(u, "xT2", i, bank="qk2"))
                if reader_of("qk2") is not act_:
                    pe.wait_ge(*bank_free(u, "qk2", i))
                for n in range(2 * C):
                    m = features(u, "qk2", n * P, Wqkv, n * P, lambda c: xT[u][:, c, :], P)
                m.then_inc(*pe_.tick(u, "qk2"))
                pe.wait_ge(*bank_free(u, "v2", i))
                for c in range(C):
                    m = pe.matmul(bank(u, "v2")[:, 0:D], xT[u][:, c, :], Wqkv[:, c, 2 * D:3 * D],
                                  start=c == 0, stop=c == C - 1)
                m.then_inc(*pe_.tick(u, "v2"))

            def b_keys(u, i):
                for c, name in enumerate(("kpA", "kpB")):
                    pe.wait_ge(*act_.done(u, "qk2", i, bank=name))
                    if reader_of(name) is not act_:
                        pe.wait_ge(*bank_free(u, name, i))
                    pe.matmul(bank(u, name)[:, :], qk[u][:, C + c, :], PB[:, c, :], start=True,
                              stop=True).then_inc(*pe_.tick(u, name))

            def b_queries(u, i):
                for c, name in enumerate(("qpA", "qpB")):
                    pe.wait_ge(*bank_free(u, name, i))
                    for j in range(4):
                        m = pe.matmul(bank(u, name)[:, j * P:(j + 1) * P], PB[:, c, j * P:(j + 1) * P],
                                      qk[u][:, c, :], start=True, stop=True)
                    m.then_inc(*pe_.tick(u, name))

            def b_kv(u, i):
                for c, name in enumerate(("kvA", "kvB")):
                    pe.wait_ge(*dve_.done(u, ("kpA", "kpB")[c], i, bank=name))
                    if reader_of(name) is not dve_:
                        pe.wait_ge(*bank_free(u, name, i))
                    for j in range(4):
                        p = 4 * c + j
                        m = pe.matmul(bank(u, name)[:, j * P:(j + 1) * P], kp[u][:, p * P:(p + 1) * P],
                                      v2[u][:, :, 34 * p:34 * p + 64], start=True, stop=True)
                    m.then_inc(*pe_.tick(u, name))

            def b_attend(u, i):
                for c, name in enumerate(("aoA", "aoB")):
                    pe.wait_ge(*act_.done(u, "kv", i, bank=name))
                    pe.wait_ge(*dve_.done(u, "kv", i, bank=name))
                    for j in range(4):
                        p = 4 * c + j
                        m = pe.matmul(bank(u, name)[:, j * P:(j + 1) * P], qp[u][:, p * P:(p + 1) * P],
                                      kvb[u][:, :, 34 * p:34 * p + 64], start=True, stop=True)
                    m.then_inc(*pe_.tick(u, name))

            def c_proj(u, i):
                pe.wait_ge(*act_.done(u, "xT3", i, bank="qk3"))
                if reader_of("qk3") is not act_:
                    pe.wait_ge(*bank_free(u, "qk3", i))
                for n in range(2 * C):
                    m = features(u, "qk3", n * P, Wattn, n * P, lambda c: xT[u][:, c, :], P)
                m.then_inc(*pe_.tick(u, "qk3"))
                pe.wait_ge(*bank_free(u, "v3", i))
                for b in range(2):
                    for half in range(2):
                        for c in range(C):
                            m = pe.matmul(bank(u, "v3")[SQ * half:SQ * half + SQ, b * D:(b + 1) * D],
                                          xT[u][:, c, b * SQ:(b + 1) * SQ], Wattn[:, c, 2 * D:3 * D],
                                          start=c == 0, stop=c == C - 1)
                m.then_inc(*pe_.tick(u, "v3"))

            def c_scores(u, i):
                for c, name in enumerate(("s3A", "s3B")):
                    pe.wait_ge(*act_.done(u, "kB", i, bank=name))
                    pe.wait_ge(*dve_.done(u, "kB", i, bank=name))
                    for b in range(2):
                        m = pe.matmul(bank(u, name)[SQ * b:SQ * b + SQ, :], qk[u][:, c, b * SQ:(b + 1) * SQ],
                                      kB[u][:, c, b, :, :].rearrange("p h k -> p (h k)"), start=True, stop=True)
                    m.then_inc(*pe_.tick(u, name))

            def c_probs_t(u, i):
                for c, name in enumerate(("pT3A", "pT3B")):
                    pe.wait_ge(*act_.done(u, ("e3A", "e3B")[c], i, bank=name))
                    if reader_of(name) is not act_:
                        pe.wait_ge(*bank_free(u, name, i))
                    for j in range(4):
                        t = pe.transpose(bank(u, name)[:, j * P:(j + 1) * P], pbf[u][c][:, j * P:(j + 1) * P], ident[:, :])
                    t.then_inc(*pe_.tick(u, name))

            def c_pv(u, i):
                for c, name in enumerate(("o3A", "o3B")):
                    pe.wait_ge(*act_.done(u, ("pT3A", "pT3B")[c], i, bank=name))
                    pe.wait_ge(*dve_.done(u, "vB", i, bank=name))
                    for j in range(4):
                        p = 4 * c + j
                        m = pe.matmul(bank(u, name)[:, j * P:(j + 1) * P], pT[u][c][:, j, :],
                                      vB[u][:, :, 32 * p:32 * p + 64], start=True, stop=True)
                    m.then_inc(*pe_.tick(u, name))

            def d_route(u, i):
                pe.wait_ge(*act_.done(u, "xT4", i, bank="rt"))
                if reader_of("rt") is not act_:
                    pe.wait_ge(*bank_free(u, "rt", i))
                for c in range(C):
                    m = pe.matmul(bank(u, "rt")[:, 0:E], xT[u][:, c, :], Wr[:, c, :], start=c == 0, stop=c == C - 1)
                m.then_inc(*pe_.tick(u, "rt"))

            def d_rank(u, i):
                pe.wait_ge(*dve_.done(u, "oh", i, bank="rk"))
                pe.matmul(bank(u, "rk")[:, 0:TOP * E], before[:, :], ohb[u][:, :], start=True, stop=True)
                pe.matmul(bank(u, "rk")[:, TOP * E:2 * TOP * E], ones_b[:, :], ohb[u][:, :], start=True,
                          stop=True).then_inc(*pe_.tick(u, "rk"))

            def a_project(u, i):
                project_out(u, i, "w1", Wo, "o1", dve_)

            def b_x_t(u, i):
                transpose_x(u, i, "xT2", xn[u], "xn2")

            def b_out_t(u, i):
                transpose_x(u, i, "aT2", at[u], "ao")

            def b_project(u, i):
                project_out(u, i, "w2", Wout, "aT2", act_)

            def c_x_t(u, i):
                transpose_x(u, i, "xT3", xn[u], "xn3")

            def c_out_t(u, i):
                transpose_x(u, i, "aT3", at[u], "o3")

            def c_project(u, i):
                project_out(u, i, "w3", Wproj, "aT3", act_)

            def d_x_t(u, i):
                transpose_x(u, i, "xT4", xr[u][0], "xn4")

            def a_pair(u, i, p):
                if p + 2 < NP_:
                    a_scores(u, i, p + 2)
                a_probs_t(u, i, p)
                if p:
                    a_pv(u, i, p - 1)

            def half(f, fi, s, si):
                def first(step, *args):
                    if f is not None:
                        step(f, fi, *args)

                def second(step, *args):
                    if s is not None:
                        step(s, si, *args)

                first(a_keys)
                second(b_keys)
                first(a_values)
                second(b_queries)
                first(a_x_t)
                second(b_kv)
                first(a_q)
                second(b_attend)
                first(a_scores, 0)
                first(a_scores, 1)
                second(b_out_t)
                first(a_pair, 0)
                second(b_project)
                first(a_pair, 1)
                first(a_pair, 2)
                second(c_x_t)
                first(a_pair, 3)
                second(c_proj)
                first(a_pair, 4)
                second(c_scores)
                first(a_pair, 5)
                second(c_probs_t)
                first(a_pair, 6)
                second(c_pv)
                second(c_out_t)
                first(a_pair, 7)
                second(c_project)
                first(a_pv, 7)
                first(a_project)
                second(d_x_t)
                first(b_x_t)
                second(d_route)
                first(b_proj)
                second(d_rank)

            in_turn(pe, half)
            pe.wait_ge(experts_in, 32)
            with pe.Fori(0, BLOCKS // ESLOTS) as i:
                def e_xT(v):
                    pe.wait_ge(block_loaded[v], 16 * (i + 1))
                    pe.wait_ge(*edve_.done_before(v, "hT", i))
                    for c in range(C):
                        t = pe.transpose(ebank[v][0][:, c * P:(c + 1) * P], xs[v][:, c * P:(c + 1) * P], ident[:, :])
                    t.then_inc(*epe_.tick(v, "xT"))

                def e_up(v):
                    expert = pe.value_load(xs[v][0:1, D:D + 1].bitcast(U32), min_val=0, max_val=E - 1)
                    pe.wait_ge(*eact_.done(v, "xT", i))
                    pe.wait_ge(*edve_.done_before(v, "y", i))
                    for c in range(C):
                        m = pe.matmul(ebank[v][1][:, :], xTe[v][:, c, :], W1[:, c, bass.ds(expert * FF, FF)],
                                      start=c == 0, stop=c == C - 1)
                    m.then_inc(*epe_.tick(v, "up"))
                    return expert

                def e_hT(v):
                    pe.wait_ge(*eact_.done(v, "gelu", i))
                    for f in range(FB):
                        t = pe.transpose(ebank[v][0][:, f * P:(f + 1) * P], he[v][:, f * P:(f + 1) * P], ident[:, :])
                    t.then_inc(*epe_.tick(v, "hT"))

                def e_down(v, expert):
                    pe.wait_ge(*edve_.done(v, "hT", i))
                    for f in range(FB):
                        m = pe.matmul(ebank[v][1][:, 0:D], hTe[v][:, f, :],
                                      W2[:, bass.ds(expert * FB + f, 1), :].rearrange("p o n -> p (o n)"),
                                      start=f == 0, stop=f == FB - 1)
                    m.then_inc(*epe_.tick(v, "down"))

                e_xT(0)
                e_xT(1)
                e0 = e_up(0)
                e1 = e_up(1)
                e_xT(2)
                e_xT(3)
                e_hT(0)
                e2 = e_up(2)
                e_hT(1)
                e3 = e_up(3)
                e_down(0, e0)
                e_down(1, e1)
                e_hT(2)
                e_hT(3)
                e_down(2, e2)
                e_down(3, e3)

        @block.scalar
        def _(act):
            for u in range(SLOTS):
                act.sem_inc(act_.sems[u], act_.credits[u])
                act.sem_inc(stored[u], 16)
            for v in range(ESLOTS):
                act.sem_inc(eact_.sems[v], eact_.credits[v])
                act.sem_inc(out_stored[v], 16)
            act.wait_ge(weights_in, 16 * NW)
            act.wait_ge(zeroed, 1 + 4 * SLOTS + 2 * SLOTS)
            def copy_out(u, i, name, dst, scale=None):
                act.wait_ge(*pe_.done(u, name, i))
                src = bank(u, name)
                if scale is None:
                    a = act.activation(dst[:, :, :].rearrange("p c t -> p (c t)"), src[:, 0:C * P], ACT.Copy)
                else:
                    for c in range(C):
                        a = act.activation(dst[:, c, :], src[:, c * P:(c + 1) * P], ACT.Copy, scale=scale[:, c:c + 1])
                a.then_inc(*act_.tick(u, name))

            def a_keys(u, i):
                for c, name in enumerate(("k1a", "k1b")):
                    act.wait_ge(*pe_.done(u, name, i))
                    act.activation(kT[u][:, c, :, :].rearrange("p b k -> p (b k)"), bank(u, name)[:, :], ACT.Identity,
                                   bias=bkT[:, c:c + 1]).then_inc(*act_.tick(u, name))

            def a_values(u, i):
                for b, name in enumerate(("v1a", "v1b")):
                    act.wait_ge(*pe_.done(u, name, i))
                    act.activation(vS[u][:, b, :, :].rearrange("p k n -> p (k n)"), bank(u, name)[:, :],
                                   ACT.Copy).then_inc(*act_.tick(u, name))

            def a_x_t(u, i):
                copy_out(u, i, "xT1", xT[u])

            def a_q(u, i):
                act.wait_ge(*pe_.done(u, "q1", i))
                for c in range(C):
                    a = act.activation(qs[u][:, c, :], bank(u, "q1")[:, c * P:(c + 1) * P], ACT.Identity,
                                       bias=bqT[:, c:c + 1])
                a.then_inc(*act_.tick(u, "q1"))
                act.wait_ge(*act_.done(u, "q1", i))
                for j in range(4):
                    r = slice(32 * j, 32 * j + 32)
                    a = act.activation(qB[u][r, j, :, :, 1, :].rearrange("p c b q -> p (c b) q"),
                                       qs[u][r, :, :].rearrange("p c (b q) -> p (c b) q", b=2), ACT.Copy, scale=hmask[r, 1:2])
                a.then_inc(*act_.tick(u, "qB"))

            def b_x_t(u, i):
                copy_out(u, i, "xT2", xT[u])

            def b_out_t(u, i):
                copy_out(u, i, "aT2", aT[u])

            def c_x_t(u, i):
                copy_out(u, i, "xT3", xT[u], ln1T)

            def c_out_t(u, i):
                copy_out(u, i, "aT3", aT[u])

            def d_x_t(u, i):
                copy_out(u, i, "xT4", xT[u], ln2T)

            def d_store(u, i):
                act.wait_ge(*dve_.done(u, "gate", i))
                act.wait_ge(*pool_.done(u, "sum", i))
                act.dma_start(base_d[bass.ds((i * SLOTS + u) * P, P), :], xb[u][:, :]).then_inc(stored[u], 16)

            def a_exp(u, i, p):
                act.wait_ge(*dve_.done(u, f"nb{p}", i))
                for b in range(2):
                    n = 2 * p + b
                    a = act.activation(pb[u][p % 3][:, b, :], pb[u][p % 3][:, b, :], ACT.Exp, bias=nb[u][:, n:n + 1],
                                       scale=SCALE, accum_out=su[u][:, n:n + 1])
                a.then_inc(*act_.tick(u, f"exp{p}"))

            def a_pt(u, i, p):
                act.wait_ge(*pe_.done(u, f"pT{p}", i))
                act.activation(pT[u][p % 2][:, :, :].rearrange("p a b -> p (a b)"), bank(u, f"pT{p}")[:, :],
                               ACT.Copy).then_inc(*act_.tick(u, f"pT{p}"))

            def b_qk(u, i):
                act.wait_ge(*pe_.done(u, "qk2", i))
                act.activation(qk[u][:, :, :].rearrange("p c t -> p (c t)"), bank(u, "qk2")[:, :],
                               ACT.Copy).then_inc(*act_.tick(u, "qk2"))

            def b_exp(u, i, which):
                for n, half in enumerate("AB"):
                    act.wait_ge(*pe_.done(u, f"{which}p{half}", i))
                    if which == "q":
                        act.wait_ge(*dve_.done(u, f"kp{half}", i))
                    act.activation(pbf[u][n], bank(u, f"{which}p{half}")[:, :],
                                   ACT.Exp).then_inc(*act_.tick(u, f"e{which}{half}"))

            def b_kv(u, i):
                act.wait_ge(*pe_.done(u, "kvA", i))
                src = bank(u, "kvA")[:, :].rearrange("p (j b w) -> p b j w", j=4, b=2)
                dst = kvb[u][:, :, 0:4 * 34].rearrange("p b (j w) -> p b j w", w=34)
                for h in range(2):
                    a = act.activation(dst[64 * h:64 * h + 64, :, :, 17 * h:17 * h + 17],
                                       src[64 * h:64 * h + 64, :, :, 17 * h:17 * h + 17], ACT.Copy)
                a.then_inc(*act_.tick(u, "kv"))

            def c_q(u, i):
                act.wait_ge(*pe_.done(u, "qk3", i))
                act.activation(qk[u][:, :, :].rearrange("p c t -> p (c t)"), bank(u, "qk3")[:, :],
                               ACT.Copy).then_inc(*act_.tick(u, "qk3"))
                act.wait_ge(*act_.done(u, "qk3", i))
                for j in range(4):
                    r = slice(32 * j, 32 * j + 32)
                    a = act.activation(kB[u][r, :, :, 2 * j + 1, :].rearrange("p c b k -> p (c b) k"),
                                       qk[u][r, C:2 * C, :].rearrange("p c (b k) -> p (c b) k", b=2), ACT.Copy, scale=hmask[r, 1:2])
                a.then_inc(*act_.tick(u, "kB"))

            def c_exp(u, i):
                for n, half in enumerate("AB"):
                    act.wait_ge(*dve_.done(u, f"d3{half}", i))
                    act.activation(pbf[u][n], pbf[u][n], ACT.Exp, scale=SCALE).then_inc(*act_.tick(u, f"e3{half}"))

            def c_pt(u, i):
                for n, name in enumerate(("pT3A", "pT3B")):
                    act.wait_ge(*pe_.done(u, name, i))
                    act.activation(pT[u][n][:, :, :].rearrange("p a b -> p (a b)"), bank(u, name)[:, :],
                                   ACT.Copy).then_inc(*act_.tick(u, name))

            def d_gate(u, i):
                act.wait_ge(*dve_.done(u, "dl", i))
                act.activation(gt[u][:, 32:33], gt[u][:, 24:25], ACT.Exp).then_inc(*act_.tick(u, "eg"))

            def half(f, fi, s, si):
                def first(step, *args):
                    if f is not None:
                        step(f, fi, *args)

                def second(step, *args):
                    if s is not None:
                        step(s, si, *args)

                first(a_keys)
                second(b_exp, "k")
                first(a_values)
                second(b_exp, "q")
                first(a_x_t)
                second(b_kv)
                first(a_q)
                first(a_exp, 0)
                second(b_out_t)
                first(a_exp, 1)
                first(a_pt, 0)
                first(a_exp, 2)
                first(a_pt, 1)
                first(a_exp, 3)
                first(a_pt, 2)
                second(c_x_t)
                first(a_exp, 4)
                first(a_pt, 3)
                second(c_q)
                first(a_exp, 5)
                first(a_pt, 4)
                second(c_exp)
                first(a_exp, 6)
                first(a_pt, 5)
                second(c_pt)
                first(a_exp, 7)
                first(a_pt, 6)
                second(c_out_t)
                first(a_pt, 7)
                second(d_x_t)
                first(b_x_t)
                second(d_gate)
                first(b_qk)
                second(d_store)

            in_turn(act, half)
            with act.Fori(0, BLOCKS // ESLOTS) as i:
                def e_xT(v):
                    act.wait_ge(*epe_.done(v, "xT", i))
                    for c in range(C):
                        a = act.activation(xTe[v][:, c, :], ebank[v][0][:, c * P:(c + 1) * P], ACT.Copy, scale=ln2T[:, c:c + 1])
                    a.then_inc(*eact_.tick(v, "xT"))

                def e_gelu(v):
                    act.wait_ge(*epe_.done(v, "up", i))
                    act.activation(he[v], ebank[v][1][:, :], ACT.Gelu).then_inc(*eact_.tick(v, "gelu"))

                e_xT(0)
                e_xT(1)
                e_gelu(0)
                e_gelu(1)
                e_xT(2)
                e_xT(3)
                e_gelu(2)
                e_gelu(3)
            with act.Fori(0, TILES // ESLOTS) as i:
                for v in range(ESLOTS):
                    act.wait_ge(second_added[v], i + 1)
                    act.dma_start(out[bass.ds((i * ESLOTS + v) * P, P), :], bd[v][:, 0:D]).then_inc(out_stored[v], 16)
            for v in range(ESLOTS):
                act.wait_ge(out_stored[v], 16 * (TILES // ESLOTS + 1))

        @block.vector
        def _(dve):
            for u in range(SLOTS):
                dve.sem_inc(dve_.sems[u], dve_.credits[u])
                if u:
                    dve.sem_inc(chain_links[u], u * 3 * CHAIN)
            for v in range(ESLOTS):
                dve.sem_inc(edve_.sems[v], edve_.credits[v])
            dve.wait_ge(weights_in, 16 * NW)
            dve.wait_ge(state_set, SLOTS + 4)
            dve.wait_ge(zeroed, 1 + 4 * SLOTS + 2 * SLOTS)
            chained = [0] * SLOTS

            def link(u, i, ins):
                ins.then_inc(chain_links[u], 1)
                chained[u] += 1
                dve.wait_ge(chain_links[u], i * CHAIN + u * 3 * CHAIN + (chained[u] - 1) % CHAIN + 1)

            def stats(u, i, n, src):
                dve.sem_inc(wait_taken, 1)
                link(u, i, dve.bn_stats(bst[u][:, :], src[:, 0:D]))
                dve.sem_inc(wait_taken, 1)
                link(u, i, dve.bn_aggr(mv[u][:, 0:2], bst[u][:, :]))
                dve.tensor_scalar(mv[u][:, 2:3], mv[u][:, 1:2], EPS, None, ALU.add).then_inc(*dve_.tick(u, f"var{n}"))

            def normalize(u, i, n, src, dst=xn):
                dve.wait_ge(*pool_.done(u, f"rs{n}", i))
                dve.tensor_scalar(dst[u][:, 0:D], src[:, 0:D], mv[u][:, 0:1], mv[u][:, 3:4], ALU.subtract,
                                  ALU.mult).then_inc(*dve_.tick(u, f"xn{n}"))

            def a_stats(u, i):
                dve.wait_ge(x_loaded[u], (i + 1) * 16)
                stats(u, i, 1, x_in[u])

            def a_norm(u, i):
                normalize(u, i, 1, x_in[u])
                dve.wait_ge(mask_loaded[u], (i + 1) * 16)
                dve.tensor_scalar(madd[u][:, :, :], mraw[u][:, :, :], -NEG, NEG, ALU.mult,
                                  ALU.add).then_inc(*dve_.tick(u, "madd"))

            def a_query(u, i):
                dve.wait_ge(*act_.done(u, "q1", i))
                for j in range(4):
                    r = slice(32 * j, 32 * j + 32)
                    t = dve.tensor_scalar(qB[u][r, j, :, :, 0, :].rearrange("p c b q -> p (c b) q"),
                                          qs[u][r, :, :].rearrange("p c (b q) -> p (c b) q", b=2), hmask[r, 0:1], None, ALU.mult)
                t.then_inc(*dve_.tick(u, "qB"))

            def a_max(u, i, p):
                dve.wait_ge(*pe_.done(u, f"s{p}", i))
                dve.sem_inc(wait_taken, 1)
                for b in range(2):
                    n = 2 * p + b
                    t = dve.tensor_tensor_reduce(pb[u][p % 3][:, b, :], bank(u, f"s{p}")[:, b * SK:(b + 1) * SK],
                                                 madd[u][:, b, :], 1.0, NEG, ALU.add, ALU.max, mx[u][:, n:n + 1])
                t.then_inc(*dve_.tick(u, f"max{p}"))
                dve.wait_ge(*dve_.done(u, f"max{p}", i))
                dve.tensor_scalar(nb[u][:, 2 * p:2 * p + 2], mx[u][:, 2 * p:2 * p + 2], -SCALE, None,
                                  ALU.mult).then_inc(*dve_.tick(u, f"nb{p}"))

            def a_divide(u, i, p):
                dve.wait_ge(*act_.done(u, f"exp{p}", i))
                dve.reciprocal(ri[u][:, 2 * p:2 * p + 2], su[u][:, 2 * p:2 * p + 2]).then_inc(*dve_.tick(u, f"ri{p}"))
                dve.wait_ge(*dve_.done(u, f"ri{p}", i))
                for b in range(2):
                    n = 2 * p + b
                    t = dve.tensor_scalar(pb[u][p % 3][:, b, :], pb[u][p % 3][:, b, :], ri[u][:, n:n + 1], None, ALU.mult)
                t.then_inc(*dve_.tick(u, f"nrm{p}"))

            def a_out(u, i):
                dve.wait_ge(*pe_.done(u, f"pv{NP_ - 1}", i))
                o = psO[u][:, :].rearrange("p (n h q) -> p n h q", n=4, h=2)
                a = aT[u][:, :, :].rearrange("p c (b q) -> p (c b) q", b=2)
                for c in range(C):
                    t = dve.tensor_scalar(a[:, 2 * c:2 * c + 2, :], o[:, 2 * c:2 * c + 2, 0, :], hmask[:, 0:1], bvT[:, c:c + 1],
                                          ALU.mult, ALU.add)
                t.then_inc(*dve_.tick(u, "o1a"))
                dve.wait_ge(*dve_.done(u, "o1a", i))
                dve.scalar_tensor_tensor(out=a, in0=o[:, :, 1, :], scalar=hmask[:, 1:2], in1=a, op0=ALU.mult,
                                         op1=ALU.add).then_inc(*dve_.tick(u, "o1"))

            def add_residual(u, i, name, group, src, dst, pool_step=None):
                dve.wait_ge(*pe_.done(u, group, i))
                if pool_step:
                    dve.wait_ge(*pool_.done(u, pool_step, i))
                dve.tensor_tensor(dst[:, 0:D], bank(u, group)[:, 0:D], src[:, :], ALU.add).then_inc(*dve_.tick(u, name))
                dve.wait_ge(*dve_.done(u, name, i))

            def b_value(u, i):
                dve.wait_ge(*pe_.done(u, "v2", i))
                for b in range(2):
                    r = slice(SQ * b, SQ * b + SQ)
                    t = dve.tensor_copy(v2[u][r, b, 0:NP_ * 34].rearrange("p (h w) -> p h w", w=17)[:, :, 0:HD],
                                        bank(u, "v2")[r, 0:D].rearrange("p (h d) -> p h d", d=HD))
                t.then_inc(*dve_.tick(u, "v2"))

            def b_feature(u, i, which, dst):
                for n, half in enumerate("AB"):
                    dve.wait_ge(*act_.done(u, f"e{which}{half}", i))
                    dve.tensor_scalar(pbf[u][n], pbf[u][n], 1.0, None, ALU.min).then_inc(*dve_.tick(u, f"t{which}{half}"))
                    dve.wait_ge(*dve_.done(u, f"t{which}{half}", i))
                    dve.scalar_tensor_tensor(out=dst[u][:, n * 512:(n + 1) * 512], in0=bank(u, f"{which}p{half}")[:, :],
                                             scalar=1.0, in1=pbf[u][n], op0=ALU.add,
                                             op1=ALU.max).then_inc(*dve_.tick(u, f"{which}p{half}"))

            def b_kv(u, i):
                dve.wait_ge(*pe_.done(u, "kvB", i))
                src = bank(u, "kvB")[:, :].rearrange("p (j b w) -> p b j w", j=4, b=2)
                dst = kvb[u][:, :, 4 * 34:8 * 34].rearrange("p b (j w) -> p b j w", w=34)
                for h in range(2):
                    t = dve.tensor_copy(dst[64 * h:64 * h + 64, :, :, 17 * h:17 * h + 17],
                                        src[64 * h:64 * h + 64, :, :, 17 * h:17 * h + 17])
                t.then_inc(*dve_.tick(u, "kv"))

            def b_out(u, i):
                dve.wait_ge(*pe_.done(u, "aoB", i))

                def cols(c, b):
                    o = bank(u, ("aoA", "aoB")[c])[SQ * b:SQ * b + SQ, :].rearrange("p (j b w) -> p j b w", j=4, b=2)
                    return o[:, :, b, 0:34].rearrange("p j (h w) -> p j h w", h=2)

                for c in range(C):
                    for b in range(2):
                        t = dve.tensor_scalar(su[u][SQ * b:SQ * b + SQ, 8 * c:8 * c + 8].rearrange("p (j h) -> p j h", h=2),
                                              cols(c, b)[:, :, :, 16], 1e-8, None, ALU.add)
                t.then_inc(*dve_.tick(u, "den"))
                dve.wait_ge(*dve_.done(u, "den", i))
                dve.reciprocal(ri[u][:, :], su[u][:, :]).then_inc(*dve_.tick(u, "rden"))
                dve.wait_ge(*dve_.done(u, "rden", i))
                for c in range(C):
                    for b in range(2):
                        r = slice(SQ * b, SQ * b + SQ)
                        t = dve.tensor_tensor(
                            at[u][r, c * P:(c + 1) * P].rearrange("p (j h d) -> p j h d", j=4, h=2), cols(c, b)[:, :, :, 0:HD],
                            ri[u][r, 8 * c:8 * c + 8].rearrange("p (j h) -> p j h", h=2).unsqueeze(3)
                            .to_broadcast([SQ, 4, 2, HD]), ALU.mult)
                t.then_inc(*dve_.tick(u, "ao"))

            def a_residual(u, i):
                add_residual(u, i, "x1", "w1", xres[u], xa[u], "xb1")
                stats(u, i, 2, xa[u])

            def b_norm(u, i):
                normalize(u, i, 2, xa[u])

            def b_residual(u, i):
                dve.wait_ge(stored[u], (i + 1) * 16)
                add_residual(u, i, "x2", "w2", xres[u], xb[u], "xb2")
                stats(u, i, 0, xb[u])

            def c_residual(u, i):
                dve.wait_ge(*pool_.done(u, "rs0", i))
                dve.tensor_scalar(xres[u][:, :], xb[u][:, 0:D], mv[u][:, 0:1], mv[u][:, 3:4], ALU.subtract,
                                  ALU.mult).then_inc(*dve_.tick(u, "h0"))
                dve.wait_ge(*dve_.done(u, "h0", i))
                stats(u, i, 3, xres[u])

            def c_norm(u, i):
                normalize(u, i, 3, xres[u])

            def d_residual(u, i):
                add_residual(u, i, "x3", "w3", xres[u], xa[u])
                stats(u, i, 4, xa[u])

            def d_norm(u, i):
                normalize(u, i, 4, xa[u], [xr[0][0], xr[1][0]])

            def c_keys(u, i):
                dve.wait_ge(*act_.done(u, "qk3", i))
                for j in range(4):
                    r = slice(32 * j, 32 * j + 32)
                    t = dve.tensor_scalar(kB[u][r, :, :, 2 * j, :].rearrange("p c b k -> p (c b) k"),
                                          qk[u][r, C:2 * C, :].rearrange("p c (b k) -> p (c b) k", b=2), hmask[r, 0:1], None, ALU.mult)
                t.then_inc(*dve_.tick(u, "kB"))

            def c_value(u, i):
                dve.wait_ge(*pe_.done(u, "v3", i))
                src = bank(u, "v3")[:, :].rearrange("p (b j h d) -> p b j h d", b=2, j=NP_, h=2)
                dst = vB[u][:, :, 0:D].rearrange("p b (j h d) -> p b j h d", j=NP_, h=2)
                for h in range(2):
                    r = slice(64 * h, 64 * h + 64)
                    t = dve.tensor_copy(dst[r, :, :, h, :], src[r, :, :, h, :])
                t.then_inc(*dve_.tick(u, "vB"))

            def heads(ap):
                return ap.rearrange("p (h k) -> p h k", k=SQ)

            def c_max(u, i):
                for n, half in enumerate("AB"):
                    dve.wait_ge(*pe_.done(u, f"s3{half}", i))
                    dve.tensor_tensor(heads(pbf[u][n]), heads(bank(u, f"s3{half}")[:, :]),
                                      causal[:, :].unsqueeze(1).to_broadcast([P, 8, SQ]),
                                      ALU.add).then_inc(*dve_.tick(u, f"s3{half}"))
                    dve.wait_ge(*dve_.done(u, f"s3{half}", i))
                    dve.tensor_reduce(mx[u][:, 8 * n:8 * n + 8], heads(pbf[u][n]), AX.X,
                                      ALU.max).then_inc(*dve_.tick(u, f"m3{half}"))
                    dve.wait_ge(*dve_.done(u, f"m3{half}", i))
                    dve.tensor_tensor(heads(pbf[u][n]), heads(pbf[u][n]),
                                      mx[u][:, 8 * n:8 * n + 8].unsqueeze(2).to_broadcast([P, 8, SQ]),
                                      ALU.subtract).then_inc(*dve_.tick(u, f"d3{half}"))

            def c_sum(u, i):
                for n, half in enumerate("AB"):
                    dve.wait_ge(*act_.done(u, f"e3{half}", i))
                    dve.tensor_reduce(su[u][:, 8 * n:8 * n + 8], heads(pbf[u][n]), AX.X,
                                      ALU.add).then_inc(*dve_.tick(u, f"sum{half}"))
                dve.wait_ge(*dve_.done(u, "sumB", i))
                dve.reciprocal(ri[u][:, :], su[u][:, :]).then_inc(*dve_.tick(u, "r3"))

            def c_out(u, i):
                dve.wait_ge(*dve_.done(u, "r3", i))
                dve.wait_ge(*pe_.done(u, "o3B", i))
                for c in range(C):
                    for b in range(2):
                        r = slice(SQ * b, SQ * b + SQ)
                        o = bank(u, ("o3A", "o3B")[c])[r, :].rearrange("p (j b w) -> p j b w", j=4, b=2)
                        t = dve.tensor_tensor(
                            at[u][r, c * P:(c + 1) * P].rearrange("p (j h d) -> p j h d", j=4, h=2),
                            o[:, :, b, 0:32].rearrange("p j (h d) -> p j h d", h=2),
                            ri[u][r, 8 * c:8 * c + 8].rearrange("p (j h) -> p j h", h=2).unsqueeze(3)
                            .to_broadcast([SQ, 4, 2, HD]), ALU.mult)
                t.then_inc(*dve_.tick(u, "o3"))

            def d_top(u, i):
                g = gt[u]
                dve.wait_ge(*pe_.done(u, "rt", i))
                dve.tensor_copy(g[:, 0:8], bank(u, "rt")[:, 0:E]).then_inc(*dve_.tick(u, "lg"))
                dve.wait_ge(*dve_.done(u, "lg", i))
                dve.sem_inc(wait_taken, 1)
                dve.max(g[:, 8:16], g[:, 0:8]).then_inc(*dve_.tick(u, "top"))
                dve.wait_ge(*dve_.done(u, "top", i))
                dve.sem_inc(wait_taken, 1)
                dve.max_index(gix[u][:, :], g[:, 8:16], g[:, 0:8]).then_inc(*dve_.tick(u, "ix"))
                dve.wait_ge(*dve_.done(u, "ix", i))
                dve.tensor_copy(g[:, 16:24], gix[u][:, :]).then_inc(*dve_.tick(u, "ixf"))
                dve.wait_ge(*dve_.done(u, "ixf", i))
                for k in range(TOP):
                    dve.tensor_scalar(oh[u][:, k * E:(k + 1) * E], iota8[:, :], g[:, 16 + k:17 + k], None, ALU.is_equal)
                for k in range(TOP):
                    t = dve.tensor_scalar(ohb[u][:, k * E:(k + 1) * E], iota8[:, :], g[:, 16 + k:17 + k], None, ALU.is_equal)
                t.then_inc(*dve_.tick(u, "oh"))
                dve.tensor_tensor(g[:, 24:25], g[:, 9:10], g[:, 8:9], ALU.subtract).then_inc(*dve_.tick(u, "dl"))

            def d_gate(u, i):
                g = gt[u]
                dve.wait_ge(*act_.done(u, "eg", i))
                link(u, i, dve.tensor_scalar(g[:, 33:34], g[:, 32:33], 1.0, None, ALU.add))
                link(u, i, dve.reciprocal(xb[u][:, D:D + 1], g[:, 33:34]))
                dve.tensor_tensor(xb[u][:, D + 1:D + 2], xb[u][:, D:D + 1], g[:, 32:33],
                                  ALU.mult).then_inc(*dve_.tick(u, "gate"))

            def d_place(u, i):
                s, r = sc[u], rk[u]
                end, over, over2, new, skip, ahead = (s[:, n * E:(n + 1) * E] for n in range(6))
                at_, hop = s[:, 48:64], s[:, 64:80]
                both_ = lambda ap: ap.rearrange("p (k e) -> p k e", k=TOP)
                each = lambda ap: ap.unsqueeze(1).to_broadcast([P, TOP, E])
                dve.wait_ge(*pe_.done(u, "rk", i))
                dve.tensor_copy(r[:, :], bank(u, "rk")[:, 0:2 * TOP * E]).then_inc(*dve_.tick(u, "rk"))
                dve.wait_ge(*dve_.done(u, "rk", i))
                link(u, i, dve.tensor_tensor(r[:, E:2 * E], r[:, E:2 * E], r[:, 2 * E:3 * E], ALU.add))
                link(u, i, dve.tensor_tensor(end, r[:, 2 * E:3 * E], r[:, 3 * E:4 * E], ALU.add))
                link(u, i, dve.tensor_tensor(end, end, used[:, :], ALU.add))
                dve.tensor_scalar(over, end, float(P), None, ALU.is_gt)
                link(u, i, dve.tensor_scalar(over2, end, float(2 * P), None, ALU.is_gt))
                link(u, i, dve.tensor_tensor(new, over, over2, ALU.add))
                link(u, i, dve.tensor_tensor(cum8[u][:, :, :], earlier[:, :, :], new.unsqueeze(1).to_broadcast([P, E, E]), ALU.mult))
                link(u, i, dve.tensor_reduce(skip, cum8[u][:, :, :], AX.X, ALU.add))
                link(u, i, dve.tensor_scalar(ahead, skip, float(P), unused[:, 0:1], ALU.mult, ALU.add))
                link(u, i, dve.scalar_tensor_tensor(out=ahead, in0=ahead, scalar=-float(P), in1=first[:, :], op0=ALU.add, op1=ALU.subtract))
                link(u, i, dve.tensor_tensor(both_(at_), both_(r[:, 0:2 * E]), each(used[:, :]), ALU.add))
                link(u, i, dve.scalar_tensor_tensor(out=both_(hop), in0=both_(at_), scalar=float(P), in1=each(ahead), op0=ALU.is_ge, op1=ALU.mult))
                link(u, i, dve.tensor_tensor(at_, at_, hop, ALU.add))
                link(u, i, dve.tensor_tensor(both_(at_), both_(at_), each(first[:, :]), ALU.add))
                dve.tensor_tensor(hop[:, 0:E], over, ahead, ALU.mult)
                link(u, i, dve.scalar_tensor_tensor(out=used[:, :], in0=new, scalar=-float(P), in1=end, op0=ALU.mult, op1=ALU.add))
                dve.tensor_reduce(hop[:, E:E + 1], new, AX.X, ALU.add)
                link(u, i, dve.scalar_tensor_tensor(out=first[:, :], in0=new, scalar=float(P), in1=first[:, :], op0=ALU.mult, op1=ALU.add))
                link(u, i, dve.tensor_tensor(first[:, :], first[:, :], hop[:, 0:E], ALU.add))
                link(u, i, dve.scalar_tensor_tensor(out=unused[:, :], in0=hop[:, E:E + 1], scalar=float(P), in1=unused[:, :], op0=ALU.mult, op1=ALU.add))
                link(u, i, dve.tensor_tensor(at_, at_, oh[u][:, :], ALU.mult))
                link(u, i, dve.tensor_reduce(gt[u][:, 40:42], both_(at_), AX.X, ALU.add))
                dve.wait_ge(*pool_.done_before(u, "sent", i))
                dve.tensor_copy(pos[u][:, :], gt[u][:, 40:42])
                dve.wait_ge(*pool_.done(u, "copy", i))
                for k in range(TOP):
                    last = xr[u][k][:, D:XW].bitcast(U32)
                    dve.tensor_copy(last[:, 0:1], gix[u][:, k:k + 1])
                    dve.tensor_copy(last[:, 1:2], dst[u][:, k:k + 1])
                    t = dve.memset(last[:, 2:4], 0)
                t.then_inc(*dve_.tick(u, "meta"))
                dve.wait_ge(*dve_.done(u, "meta", i))
                dve.tensor_scalar(dst[u][:, :], dst[u][:, :], float(SLOTS * P * TOP), None, ALU.add).then_inc(dst_moved[u], 1)

            def half(f, fi, s, si):
                def first(step, *args):
                    if f is not None:
                        step(f, fi, *args)

                def second(step, *args):
                    if s is not None:
                        step(s, si, *args)

                first(a_stats)
                second(b_feature, "k", kp)
                first(a_norm)
                second(b_feature, "q", qp)
                second(b_kv)
                first(a_query)
                second(b_out)
                first(a_max, 0)
                first(a_max, 1)
                first(a_divide, 0)
                first(a_max, 2)
                second(b_residual)
                first(a_divide, 1)
                first(a_max, 3)
                second(c_residual)
                first(a_divide, 2)
                first(a_max, 4)
                second(c_norm)
                first(a_divide, 3)
                first(a_max, 5)
                second(c_keys)
                second(c_value)
                first(a_divide, 4)
                first(a_max, 6)
                second(c_max)
                first(a_divide, 5)
                first(a_max, 7)
                second(c_sum)
                first(a_divide, 6)
                second(c_out)
                first(a_divide, 7)
                second(d_residual)
                first(a_out)
                first(a_residual)
                second(d_norm)
                first(b_norm)
                second(d_top)
                second(d_gate)
                first(b_value)
                second(d_place)

            in_turn(dve, half)
            assert chained == [CHAIN * ITERS_WRITTEN] * SLOTS, chained
            with dve.Fori(0, BLOCKS // ESLOTS) as i:
                def e_hT(v):
                    dve.wait_ge(*epe_.done(v, "hT", i))
                    dve.tensor_copy(hTe[v][:, :, :].rearrange("p a b -> p (a b)"), ebank[v][0][:, :]).then_inc(*edve_.tick(v, "hT"))

                def e_y(v):
                    dve.wait_ge(*epe_.done(v, "down", i))
                    dve.wait_ge(*epool_.done_before(v, "sent", i))
                    dve.tensor_copy(where[v][:, :], xs[v][:, D + 1:D + 2].bitcast(U32))
                    dve.tensor_copy(ye[v][:, :], ebank[v][1][:, 0:D]).then_inc(*edve_.tick(v, "y"))

                e_hT(0)
                e_hT(1)
                e_y(0)
                e_y(1)
                e_hT(2)
                e_hT(3)
                e_y(2)
                e_y(3)
            with dve.Fori(0, TILES // ESLOTS) as i:
                for v in range(ESLOTS):
                    dve.wait_ge(tile_loaded[v], 32 * (i + 1))
                    dve.scalar_tensor_tensor(out=bd[v][:, 0:D], in0=yd[v][:, 0:D], scalar=bd[v][:, D:D + 1], in1=bd[v][:, 0:D],
                                             op0=ALU.mult, op1=ALU.add).then_inc(first_added[v], 1)
                for v in range(ESLOTS):
                    dve.wait_ge(first_added[v], i + 1)
                    dve.scalar_tensor_tensor(out=bd[v][:, 0:D], in0=yd[v][:, D:2 * D], scalar=bd[v][:, D + 1:D + 2],
                                             in1=bd[v][:, 0:D], op0=ALU.mult, op1=ALU.add).then_inc(second_added[v], 1)

    return nc


_INS = ["x", "ctx_1024", "mask_BxS2_bf1", "L0_xattn_Wq", "L0_xattn_bq", "L0_xattn_Wk", "L0_xattn_bk", "L0_xattn_Wv",
        "L0_xattn_bv", "L0_xattn_Wo", "L0_xattn_bo", "L0_attn_w_qkv", "L0_attn_proj_matrix", "L0_attn_w_out",
        "L0_attn_b_out", "L0_ffn_ln1_w", "L0_ffn_c_attn_w", "L0_ffn_c_proj_w", "L0_ffn_ln2_w", "L0_ffn_router_w",
        "L0_ffn_w1", "L0_ffn_w2"]


def kernel(**inputs):
    import concourse.bacc as bacc
    from concourse.bass_utils import run_bass_kernel_spmd

    arrays = {n: np.ascontiguousarray(inputs[n]) for n in _INS}
    arrays["x"] = arrays["x"].reshape(B * SQ, D)
    arrays["ctx_1024"] = np.ascontiguousarray(arrays["ctx_1024"].transpose(0, 2, 1)).reshape(B * D, SK)
    q = np.arange(P) % SQ
    arrays["ident"] = np.eye(P, dtype=np.float32)
    arrays["hmask"] = (np.arange(P)[:, None] // HD % 2 == np.arange(2)[None, :]).astype(np.float32)
    arrays["causal"] = np.where(np.arange(SQ)[None, :] > q[:, None], NEG, 0.0).astype(np.float32)
    arrays["iota8"] = np.tile(np.arange(E, dtype=np.float32), (P, 1))
    arrays["before"] = np.triu(np.ones((P, P), np.float32), 1).astype(mybir.dt.np(BF16))
    arrays["earlier"] = np.broadcast_to(np.tril(np.ones((E, E), np.float32), -1), (P, E, E)).copy()
    empty = np.zeros((P, XW), np.uint32)
    empty[:, D + 1] = NOWHERE
    arrays["empty_row"] = empty.view(np.float32)
    arrays["dst"] = (np.arange(SLOTS * P * TOP).reshape(SLOTS, P, TOP)).astype(np.float32)

    nc = bacc.Bacc("TRN2", target_bir_lowering=False, num_devices=1)
    aps = [nc.dram_tensor(f"in_{n}", a.shape, mybir.dt.from_np(a.dtype), kind="ExternalInput").ap()
           for n, a in arrays.items()]
    out = nc.dram_tensor("out_0", (B * SQ, D), F32, kind="ExternalOutput").ap()
    scratch = [nc.dram_tensor(n, shape, F32, kind="Internal").ap()
               for n, shape in (("sorted_rows", (BLOCKS * P, XW)), ("base", (B * SQ, XW)), ("results", (ROWS, D)))]
    build(nc, *aps, *scratch, out)
    r = run_bass_kernel_spmd(nc, [{f"in_{n}": a for n, a in arrays.items()}], core_ids=[0])
    return r.results[0]["out_0"].reshape(B, SQ, D)
```

```python
from contextlib import ExitStack

import concourse.bass as bass
from concourse import mybir
import numpy as np

F32 = mybir.dt.float32
U32 = mybir.dt.uint32
BF16 = mybir.dt.bfloat16
U8 = mybir.dt.uint8
ALU = mybir.AluOpType
ACT = mybir.ActivationFunctionType
AX = mybir.AxisListType

P = 128
B, SQ, D = 64, 64, 256
SK = 256
NH, HD = 16, 16
C = D // P
NP_ = NH // 2
FEAT = 64
E, FF = 8, 512
FB = FF // P
TILES = B * SQ // P
SLOTS = 2
ITERS = TILES // SLOTS
TOP = 2
ROWS = TOP * B * SQ
BLOCKS = ROWS // P + E
XW = D + 4
NOWHERE = 1 << 20
ESLOTS = 4
SCALE = float(HD) ** -0.5
assert SCALE == 0.25
EPS = 1e-5
MASKED = 3.4e38
RING = 3


PE_STEPS = (["k1a", "k1b", "v1a", "v1b", "xT1", "q1", "s0", "s1"]
            + [n for p in range(NP_) for n in (([f"s{p + 2}"] if p + 2 < NP_ else []) + [f"pT{p}"] + ([f"pv{p - 1}"] if p else []))]
            + [f"pv{NP_ - 1}", "w1"]
            + ["xT2", "qk2", "v2", "kpA", "kpB", "qpA", "qpB", "kvA", "kvB", "aoA", "aoB", "aT2", "w2"]
            + ["xT3", "qk3", "v3", "s3A", "s3B", "pT3A", "pT3B", "o3A", "o3B", "aT3", "w3"]
            + ["xT4", "rt", "rk"])

ACT_STEPS = (["k1a", "k1b", "v1a", "v1b", "xT1", "q1", "qB", "exp0"] + [n for p in range(NP_) for n in (([f"exp{p + 1}"] if p + 1 < NP_ else []) + [f"pT{p}"])]
             + ["xT2", "qk2", "ekA", "ekB", "eqA", "eqB", "kv", "aT2"]
             + ["xT3", "qk3", "kB", "e3A", "e3B", "pT3A", "pT3B", "aT3"]
             + ["xT4", "eg"])

DVE_STEPS = (["var1", "xn1", "madd", "qB", "min0", "min1"]
             + [n for p in range(NP_) for n in ([f"ri{p}", f"nrm{p}"]
                                                + ([f"min{p + 2}"] if p + 2 < NP_ else []))]
             + ["o1a", "o1", "x1"]
             + ["var2", "xn2", "v2", "tkA", "kpA", "tkB", "kpB", "tqA", "qpA", "tqB", "qpB", "kv",
                "den", "rden", "ao", "x2", "var0", "h0"]
             + ["var3", "xn3", "kB", "vB", "s3A", "m3A", "d3A", "s3B", "m3B", "d3B", "sumA", "sumB", "r3", "o3", "x3"]
             + ["var4", "xn4", "top", "dl", "ix", "oh", "gate", "rk", "pos"])

POOL_STEPS = ["rs1", "xb1", "rs2", "xb2", "rs0", "rs3", "rs4", "sum", "copy", "moved", "sent"]

EPE_STEPS = ["xT", "up", "hT", "down"]
EACT_STEPS = ["xT", "gelu"]
EDVE_STEPS = ["hT", "y"]
EPOOL_STEPS = ["sent"]

GROUPS = ([("k1a", "act", "k1a"), ("k1b", "act", "k1b"), ("v1a", "act", "v1a"), ("v1b", "act", "v1b"),
           ("xT1", "act", "xT1"), ("q1", "act", "q1"), ("s0", "dve", "min0"), ("s1", "dve", "min1")]
          + [n for p in range(NP_) for n in (([(f"s{p + 2}", "dve", f"min{p + 2}")] if p + 2 < NP_ else [])
                                             + [(f"pT{p}", "act", f"pT{p}")])]
          + [("w1", "dve", "x1")]
          + [("xT2", "act", "xT2"), ("qk2", "act", "qk2"), ("v2", "dve", "v2"), ("kpA", "dve", "kpA"),
             ("kpB", "dve", "kpB"), ("qpA", "dve", "qpA"), ("qpB", "dve", "qpB"), ("kvA", "act", "kv"),
             ("kvB", "dve", "kv"), ("aoA", "dve", "ao"), ("aoB", "dve", "ao"), ("aT2", "act", "aT2"),
             ("w2", "dve", "x2")]
          + [("xT3", "act", "xT3"), ("qk3", "act", "qk3"), ("v3", "dve", "vB"), ("s3A", "dve", "s3A"),
             ("s3B", "dve", "s3B"), ("pT3A", "act", "pT3A"), ("pT3B", "act", "pT3B"), ("o3A", "dve", "o3"),
             ("o3B", "dve", "o3"), ("aT3", "act", "aT3"), ("w3", "dve", "x3")]
          + [("xT4", "act", "xT4"), ("rt", "dve", "ix"), ("rk", "dve", "rk")])
GROUP_AT = {name: n for n, (name, _, _) in enumerate(GROUPS)}


class Progress:

    def __init__(self, name, sems, steps):
        self.name, self.sems, self.steps, self.at = name, sems, steps, [0] * len(sems)
        self.credits = [(1 + 3 * u) * len(steps) for u in range(len(sems))]
        assert len(set(steps)) == len(steps)

    def tick(self, u, name):
        assert self.steps[self.at[u] % len(self.steps)] == name, (name, self.steps[self.at[u] % len(self.steps)])
        self.at[u] += 1
        return self.sems[u], 1

    def done(self, u, name, i, bank=None):
        count = self.steps.index(name)
        if bank is not None and engine_that_reads(bank) == self.name:
            count = max(count, freed_at(bank, self.steps))
        return self.sems[u], i * len(self.steps) + self.credits[u] + count + 1

    def done_before(self, u, name, i):
        return self.sems[u], i * len(self.steps) + self.credits[u] - len(self.steps) + self.steps.index(name) + 1


def bank_before(group):
    n = GROUP_AT[group]
    return n - RING if n >= RING else max(m for m in range(len(GROUPS)) if m % RING == n)


def engine_that_reads(group):
    return GROUPS[bank_before(group)][1]


def freed_at(group, steps):
    return (0 if GROUP_AT[group] >= RING else -len(steps)) + steps.index(GROUPS[bank_before(group)][2])


def build(nc, x, ctxT, mask, wq, bq, wk, bk, wv, bv, wo, bo, wqkv, proj, wout, bout, ln1, wattn, wproj, ln2,
          router, w1, w2, ident_d, hmask_d, causal_d, iota_d, before_d, earlier_d, row_d, token_d, sorted_d, out):
    with ExitStack() as ctx:
        def sb(name, shape, dt=F32):
            return ctx.enter_context(nc.sbuf_tensor(name, shape, dt))

        def per_slot(name, shape, dt=F32):
            return [sb(f"{name}_{u}", shape, dt) for u in range(SLOTS)]

        def sem(name):
            return ctx.enter_context(nc.semaphore(name))

        ident = sb("ident", [P, P])
        hmask = sb("hmask", [P, 4])
        causal = sb("causal", [P, SQ])
        iota8 = sb("iota8", [P, E])
        Wq, Wk, Wv, Wo = (sb(n, [P, C, D]) for n in ("Wq", "Wk", "Wv", "Wo"))
        Wqkv, Wattn = (sb(n, [P, C, 3 * D]) for n in ("Wqkv", "Wattn"))
        Wout, Wproj = (sb(n, [P, C, D]) for n in ("Wout", "Wproj"))
        PB = sb("PB", [P, C, 8 * FEAT])
        Wr = sb("Wr", [P, C, E])
        before = sb("before", [P, P], BF16)
        ones_b = sb("ones_b", [P, P], BF16)
        earlier = sb("earlier", [P, E, E])
        W1 = sb("W1", [P, C, E * FF])
        W2 = sb("W2", [P, E * FB, D])
        bqT, bkT, bvT, ln1T, ln2T = (sb(n, [P, C]) for n in ("bqT", "bkT", "bvT", "ln1T", "ln2T"))
        bo_b, bout_b = (sb(n, [P, D]) for n in ("bo_b", "bout_b"))
        mhalf = sb("mhalf", [P, 1])

        x_in = per_slot("x_in", [P, D])
        ctxs = per_slot("ctxs", [P, C, 2, SK])
        mraw = per_slot("mraw", [P, 2, SK], U8)
        madd = per_slot("madd", [P, 2, SK])
        bst = per_slot("bst", [P, 6])
        mv = per_slot("mv", [P, 4])
        xn = per_slot("xn", [P, D])
        xT = per_slot("xT", [P, C, P])
        xres = per_slot("xres", [P, D])
        xa = per_slot("xa", [P, D])
        xb = per_slot("xb", [P, D])
        qs = per_slot("qs", [P, C, P])
        qB = per_slot("qB", [P, 4, C, 2, 2, SQ])
        kT = per_slot("kT", [P, C, 2, SK])
        vS = per_slot("vS", [P, 2, 2, D])
        pb = [[sb(f"pb{r}_{u}", [P, 2, SK]) for r in range(3)] for u in range(SLOTS)]
        pT = [[sb(f"pT{r}_{u}", [P, 4, P]) for r in range(2)] for u in range(SLOTS)]
        mn = per_slot("mn", [P, 2 * NP_])
        su = per_slot("su", [P, 2 * NP_])
        ri = per_slot("ri", [P, 2 * NP_])
        aT = qs
        at = xn
        qk = [pb[u][2][:, :, :].rearrange("p b (c t) -> p (b c) t", t=P) for u in range(SLOTS)]
        VW = NP_ * 34 + 30
        v2 = per_slot("v2", [P, 2, VW])
        kvb = per_slot("kvb", [P, 2, VW])
        kB = per_slot("kB", [P, C, 2, 8, SQ])
        vB = per_slot("vB", [P, 2, D + 32])
        gt = per_slot("gt", [P, 64])
        gix = per_slot("gix", [P, 8], U32)
        ohb = per_slot("ohb", [P, TOP * E], BF16)
        cum8 = [pb[u][0][:, 0, 0:E * E].rearrange("p (a b) -> p a b", a=E) for u in range(SLOTS)]
        sc = [pb[u][0][:, 1, :] for u in range(SLOTS)]
        pos = per_slot("pos", [P, TOP], U32)
        token = per_slot("token", [P, 1])
        used = sb("used", [P, E])
        first = sb("first", [P, E])
        unused = sb("unused", [P, 1])
        kp = [kT[u][:, :, :, :].rearrange("p a b c -> p (a b c)") for u in range(SLOTS)]
        qp = [vS[u][:, :, :, :].rearrange("p a b c -> p (a b c)") for u in range(SLOTS)]
        xr = [[pb[u][2][:, :, :].rearrange("p a b -> p (a b)")[:, 0:XW],
               pT[u][1][:, :, :].rearrange("p a b -> p (a b)")[:, 0:XW]] for u in range(SLOTS)]
        pbf = [[pb[u][r][:, :, :].rearrange("p a b -> p (a b)") for r in range(3)] for u in range(SLOTS)]

        ring = [[ctx.enter_context(nc.psum_tensor(f"ring{r}_{u}", [P, 512], F32)) for r in range(RING)]
                for u in range(SLOTS)]
        psO = [ctx.enter_context(nc.psum_tensor(f"psO_{u}", [P, 512], F32)) for u in range(SLOTS)]

        def half_of(flat, h, n):
            return flat[:, h * n:(h + 1) * n]

        VS = [(v % SLOTS, v // SLOTS) for v in range(ESLOTS)]
        xs = [half_of(ctxs[u][:, :, :, :].rearrange("p a b c -> p (a b c)"), h, XW) for u, h in VS]
        xTe = [(xT[u], qs[u])[h] for u, h in VS]
        he = [pbf[u][h] for u, h in VS]
        hTe = [pT[u][h] for u, h in VS]
        ye = [(x_in[u], xres[u])[h] for u, h in VS]
        where = [sb(f"where_{v}", [P, 1], U32) for v in range(ESLOTS)]
        banks = [b for u in range(SLOTS) for b in ring[u] + [psO[u]]]
        ebank = [banks[2 * v:2 * v + 2] for v in range(ESLOTS)]

        first_weights_in = sem("first_weights_in")
        weights_in = sem("weights_in")
        experts_in = sem("experts_in")
        rows_cleared = sem("rows_cleared")
        rows_sent = [sem(f"rows_sent{u}") for u in range(SLOTS)]
        block_loaded = [sem(f"block_loaded{v}") for v in range(ESLOTS)]
        result_sent = [sem(f"result_sent{v}") for v in range(ESLOTS)]
        state_set = sem("state_set")
        epe_ = Progress("pe", [sem(f"expert_pe_steps{v}") for v in range(ESLOTS)], EPE_STEPS)
        eact_ = Progress("act", [sem(f"expert_act_steps{v}") for v in range(ESLOTS)], EACT_STEPS)
        edve_ = Progress("dve", [sem(f"expert_dve_steps{v}") for v in range(ESLOTS)], EDVE_STEPS)
        epool_ = Progress("pool", [sem(f"expert_pool_steps{v}") for v in range(ESLOTS)], EPOOL_STEPS)
        zeroed = sem("zeroed")
        ones_set = sem("ones_set")
        x_loaded = [sem(f"x_loaded{u}") for u in range(SLOTS)]
        ctx_loaded = [sem(f"ctx_loaded{u}") for u in range(SLOTS)]
        mask_loaded = [sem(f"mask_loaded{u}") for u in range(SLOTS)]
        stored = [sem(f"stored{u}") for u in range(SLOTS)]
        wait_taken = sem("wait_taken")
        sp_wait_taken = sem("sp_wait_taken")
        pool_wait_taken = sem("pool_wait_taken")
        chain_links = [sem(f"chain_links{u}") for u in range(SLOTS)]
        pe_ = Progress("pe", [sem(f"pe_steps{u}") for u in range(SLOTS)], PE_STEPS)
        act_ = Progress("act", [sem(f"act_steps{u}") for u in range(SLOTS)], ACT_STEPS)
        dve_ = Progress("dve", [sem(f"dve_steps{u}") for u in range(SLOTS)], DVE_STEPS)
        pool_ = Progress("pool", [sem(f"pool_steps{u}") for u in range(SLOTS)], POOL_STEPS)
        engine_of = {"act": act_, "dve": dve_}

        def bank(u, name):
            return ring[u][GROUP_AT[name] % RING]

        def reader_of(name):
            return engine_of[engine_that_reads(name)]

        def bank_free(u, name, i):
            engine = reader_of(name)
            return engine.sems[u], i * len(engine.steps) + engine.credits[u] + freed_at(name, engine.steps) + 1

        CHAIN = 10 + 12

        ITERS_WRITTEN = 2

        def in_turn(engine, half):
            half(0, 0, None, None)
            with engine.Fori(0, ITERS - 1) as i:
                half(1, i, 0, i)
                half(0, i + 1, 1, i)
            half(1, ITERS - 1, 0, ITERS - 1)
            half(None, None, 1, ITERS - 1)

        block = ctx.enter_context(nc.Block())

        first_loads = [
            (ident[:, :], ident_d),
            (Wk[:, :, :], wk.rearrange("(c p) n -> p c n", p=P)),
            (bkT[:, :], bk.rearrange("(c p) -> p c", p=P)),
            (Wv[:, :, :], wv.rearrange("(c p) n -> p c n", p=P)),
            (bo_b[:, :], bo.rearrange("(o n) -> o n", o=1).to_broadcast([P, D])),
            (Wq[:, :, :], wq.rearrange("(c p) n -> p c n", p=P)),
            (bqT[:, :], bq.rearrange("(c p) -> p c", p=P)),
            (hmask[:, :], hmask_d),
            (bvT[:, :], bv.rearrange("(c p) -> p c", p=P)),
            (bout_b[:, :], bout.rearrange("(o n) -> o n", o=1).to_broadcast([P, D])),
        ]
        loads = [
            (Wo[:, :, :], wo.rearrange("(c p) n -> p c n", p=P)),
            (Wqkv[:, :, :], wqkv.rearrange("(c p) n -> p c n", p=P)),
            (Wout[:, :, :], wout.rearrange("(c p) n -> p c n", p=P)),
            (ln1T[:, :], ln1.rearrange("(c p) -> p c", p=P)),
            (Wattn[:, :, :], wattn.rearrange("(c p) n -> p c n", p=P)),
            (Wproj[:, :, :], wproj.rearrange("(c p) n -> p c n", p=P)),
            (causal[:, :], causal_d), (iota8[:, :], iota_d), (before[:, :], before_d), (earlier[:, :, :], earlier_d),
            *((token[u][:, :], token_d[u]) for u in range(SLOTS)),
            (ln2T[:, :], ln2.rearrange("(c p) -> p c", p=P)),
            (Wr[:, :, :], router.rearrange("(c p) n -> p c n", p=P)),
        ]
        NF = len(first_loads)
        NW = len(loads) + NH

        @block.sync
        def _(sp):
            with nc.allow_non_contiguous_dma(reason="biases laid along partitions, once"):
                for dst_, src in first_loads:
                    sp.dma_start(dst_, src).then_inc(first_weights_in, 16)
            with sp.Fori(0, ITERS) as i:
                for u in range(SLOTS):
                    sp.wait_ge(*dve_.done_before(u, "xn1", i))
                    sp.sem_inc(sp_wait_taken, 1)
                    sp.wait_ge(*pool_.done_before(u, "xb1", i))
                    sp.sem_inc(sp_wait_taken, 1)
                    sp.dma_start(x_in[u][:, :], x[bass.ds((i * SLOTS + u) * P, P), :]).then_inc(x_loaded[u], 16)
                    sp.wait_ge(*dve_.done_before(u, "madd", i))
                    sp.sem_inc(sp_wait_taken, 1)
                    sp.dma_start(mraw[u][:, :, :],
                                 mask[bass.ds((i * SLOTS + u) * 2, 2), :].rearrange("(o b) k -> o b k", o=1)
                                 .to_broadcast([P, 2, SK])).then_inc(mask_loaded[u], 16)
                    sp.wait_ge(*pe_.done_before(u, "v1b", i))
                    sp.sem_inc(sp_wait_taken, 1)
                    for b in range(2):
                        sp.dma_start(ctxs[u][:, :, b, :],
                                     ctxT[bass.ds(((i * SLOTS + u) * 2 + b) * D, D), :]
                                     .rearrange("(c p) k -> p c k", p=P)).then_inc(ctx_loaded[u], 16)
            for u in range(SLOTS):
                sp.wait_ge(*pool_.done(u, "sent", ITERS - 1))
            with sp.Fori(0, BLOCKS // ESLOTS) as i:
                for v in range(ESLOTS):
                    sp.wait_ge(*edve_.done_before(v, "y", i))
                    sp.sem_inc(sp_wait_taken, 1)
                    sp.dma_start(xs[v], sorted_d[bass.ds((i * ESLOTS + v) * P, P), :]).then_inc(block_loaded[v], 16)

        @block.gpsimd
        def _(pool):
            pool.memset(PB[:, :, :], 0.0).then_inc(zeroed, 1)
            for u in range(SLOTS):
                pool.memset(v2[u][:, :, :], 0.0).then_inc(ones_set, 1)
                pool.memset(qB[u][:, :, :, :, :, :], 0.0).then_inc(zeroed, 1)
                pool.memset(kB[u][:, :, :, :, :], 0.0).then_inc(zeroed, 1)
                pool.memset(vB[u][:, :, :], 0.0).then_inc(zeroed, 1)
                pool.memset(kvb[u][:, :, :], 0.0).then_inc(zeroed, 1)
            pool.memset(ones_b[:, :], 1.0).then_inc(state_set, 1)
            pool.memset(used[:, :], float(P)).then_inc(state_set, 1)
            pool.memset(first[:, :], 0.0).then_inc(state_set, 1)
            pool.memset(unused[:, :], -float(P)).then_inc(state_set, 1)
            pool.memset(mhalf[:, :], -0.5).then_inc(ones_set, 1)
            pool.wait_ge(ones_set, SLOTS + 1)
            for u in range(SLOTS):
                for b in range(2):
                    ones = v2[u][SQ * b:SQ * b + SQ, b, 0:NP_ * 34].rearrange("p (h w) -> p h w", w=17)[:, :, 16:17]
                    pool.memset(ones, 1.0).then_inc(zeroed, 1)
            for u in range(SLOTS):
                pool.sem_inc(pool_.sems[u], pool_.credits[u])
            for v in range(ESLOTS):
                pool.sem_inc(epool_.sems[v], epool_.credits[v])
            pool.wait_ge(first_weights_in, 16 * NF)
            def rstd(u, i, n):
                pool.wait_ge(*dve_.done(u, f"var{n}", i))
                pool.tensor_tensor(mv[u][:, 3:4], mv[u][:, 2:3], mhalf[:, :], ALU.pow).then_inc(*pool_.tick(u, f"rs{n}"))

            def add_bias(u, i, n, src, bias):
                pool.tensor_tensor(xres[u][:, :], src[u][:, :], bias[:, :], ALU.add).then_inc(*pool_.tick(u, f"xb{n}"))

            def add_blocks(u, i):
                pool.tensor_tensor(xb[u][:, 0:D], xb[u][:, 0:D], xa[u][:, :], ALU.add).then_inc(*pool_.tick(u, "sum"))

            def copy_rows(u, i):
                pool.wait_ge(*dve_.done(u, "xn4", i))
                pool.sem_inc(pool_wait_taken, 1)
                pool.tensor_copy(xr[u][1][:, 0:D], xr[u][0][:, 0:D])

            def tag_rows(u, i):
                pool.wait_ge(*pool_.done_before(u, "moved", i))
                pool.sem_inc(pool_wait_taken, 1)
                pool.wait_ge(*dve_.done(u, "gate", i))
                pool.sem_inc(pool_wait_taken, 1)
                for k in range(TOP):
                    last = xr[u][k][:, D:XW].bitcast(U32)
                    pool.tensor_copy(last[:, 0:1], gix[u][:, k:k + 1])
                    pool.tensor_copy(last[:, 1:2], token[u][:, :])
                    pool.tensor_copy(xr[u][k][:, D + 2:D + 3], gt[u][:, 34 + k:35 + k])
                    m = pool.memset(last[:, 3:4], 0)
                m.then_inc(*pool_.tick(u, "copy"))

            def sort_rows(u, i):
                pool.wait_ge(*dve_.done(u, "pos", i))
                pool.wait_ge(*pool_.done(u, "copy", i))
                pool.wait_ge(rows_cleared, 16)
                pool.sem_inc(pool_wait_taken, 1)
                pool.tensor_scalar(token[u][:, :], token[u][:, :], float(SLOTS * P), None,
                                   ALU.add).then_inc(*pool_.tick(u, "moved"))
                for k in range(TOP):
                    pool.indirect_dma_start(sorted_d, bass.IndirectOffsetOnAxis(ap=pos[u][:, k:k + 1], axis=0),
                                            xr[u][k], None).then_inc(rows_sent[u], 16)
                pool.wait_ge(rows_sent[u], (i + 1) * (16 * TOP))
                pool.sem_inc(*pool_.tick(u, "sent"))

            def half(f, fi, s, si):
                def first(step, *args):
                    if f is not None:
                        step(f, fi, *args)

                def second(step, *args):
                    if s is not None:
                        step(s, si, *args)

                first(rstd, 1)
                first(add_bias, 1, x_in, bo_b)
                second(rstd, 0)
                second(rstd, 3)
                second(rstd, 4)
                second(add_blocks)
                first(rstd, 2)
                first(add_bias, 2, xa, bout_b)
                second(copy_rows)
                second(tag_rows)
                second(sort_rows)
                if s is None:
                    pool.wait_ge(weights_in, 16 * NW)

            in_turn(pool, half)
            for u in range(SLOTS):
                pool.wait_ge(stored[u], 16 * (ITERS + 1))
            with pool.Fori(0, BLOCKS // ESLOTS) as i:
                for v in range(ESLOTS):
                    pool.wait_ge(*edve_.done(v, "y", i))
                    pool.sem_inc(pool_wait_taken, 1)
                    pool.indirect_dma_start(out, bass.IndirectOffsetOnAxis(ap=where[v][:, 0:1], axis=0), ye[v][:, :], None,
                                            bounds_check=B * SQ - 1, oob_is_err=False,
                                            compute_op=ALU.add).then_inc(result_sent[v], 16)
                    pool.wait_ge(result_sent[v], 16 * (i + 1))
                    pool.sem_inc(*epool_.tick(v, "sent"))

        @block.tensor
        def _(pe):
            for u in range(SLOTS):
                pe.sem_inc(pe_.sems[u], pe_.credits[u])
            for v in range(ESLOTS):
                pe.sem_inc(epe_.sems[v], epe_.credits[v])
            pe.wait_ge(first_weights_in, 16 * NF)
            pe.wait_ge(state_set, 4)
            pe.wait_ge(zeroed, 1 + 4 * SLOTS + 2 * SLOTS)
            def transpose_x(u, i, name, source, step, engine=dve_):
                pe.wait_ge(*engine.done(u, step, i, bank=name))
                if reader_of(name) is not engine:
                    pe.wait_ge(*bank_free(u, name, i))
                for c in range(C):
                    t = pe.transpose(bank(u, name)[:, c * P:(c + 1) * P], source[:, c * P:(c + 1) * P], ident[:, :])
                t.then_inc(*pe_.tick(u, name))

            def features(u, name, col, w, w0, rhs, n):
                for c in range(C):
                    m = pe.matmul(bank(u, name)[:, col:col + n], w[:, c, w0:w0 + P], rhs(c),
                                  start=c == 0, stop=c == C - 1)
                return m

            def project_out(u, i, name, w, step, engine):
                pe.wait_ge(*engine.done(u, step, i, bank=name))
                if reader_of(name) is not engine:
                    pe.wait_ge(*bank_free(u, name, i))
                for c in range(C):
                    m = pe.matmul(bank(u, name)[:, 0:D], aT[u][:, c, :], w[:, c, :], start=c == 0, stop=c == C - 1)
                m.then_inc(*pe_.tick(u, name))

            def a_keys(u, i):
                pe.wait_ge(ctx_loaded[u], (i + 1) * 32)
                for c2, name in enumerate(("k1a", "k1b")):
                    pe.wait_ge(*bank_free(u, name, i))
                    m = features(u, name, 0, Wk, c2 * P,
                                 lambda c: ctxs[u][:, c, :, :].rearrange("p b k -> p (b k)"), 2 * SK)
                    m.then_inc(*pe_.tick(u, name))

            def a_values(u, i):
                for b, name in enumerate(("v1a", "v1b")):
                    pe.wait_ge(*bank_free(u, name, i))
                    for kh in range(2):
                        for c in range(C):
                            m = pe.matmul(bank(u, name)[:, kh * D:(kh + 1) * D],
                                          ctxs[u][:, c, b, kh * P:(kh + 1) * P], Wv[:, c, :],
                                          start=c == 0, stop=c == C - 1)
                    m.then_inc(*pe_.tick(u, name))

            def a_x_t(u, i):
                transpose_x(u, i, "xT1", xn[u], "xn1")

            def a_q(u, i):
                pe.wait_ge(*act_.done(u, "xT1", i, bank="q1"))
                if reader_of("q1") is not act_:
                    pe.wait_ge(*bank_free(u, "q1", i))
                for c2 in range(C):
                    m = features(u, "q1", c2 * P, Wq, c2 * P, lambda c: xT[u][:, c, :], P)
                m.then_inc(*pe_.tick(u, "q1"))

            def a_scores(u, i, p):
                c, j = divmod(p, 4)
                if p == 0:
                    pe.wait_ge(*act_.done(u, "qB", i, bank="s0"))
                    pe.wait_ge(*dve_.done(u, "qB", i, bank="s0"))
                else:
                    pe.wait_ge(*bank_free(u, f"s{p}", i))
                for b in range(2):
                    m = pe.matmul(bank(u, f"s{p}")[:, b * SK:(b + 1) * SK],
                                  qB[u][:, j, c, b, :, :].rearrange("p h q -> p (h q)"), kT[u][:, c, b, :], start=True, stop=True)
                m.then_inc(*pe_.tick(u, f"s{p}"))

            def a_probs_t(u, i, p):
                pe.wait_ge(*dve_.done(u, f"nrm{p}", i, bank=f"pT{p}"))
                if reader_of(f"pT{p}") is not dve_:
                    pe.wait_ge(*bank_free(u, f"pT{p}", i))
                for b in range(2):
                    for kh in range(2):
                        n = 2 * b + kh
                        t = pe.transpose(bank(u, f"pT{p}")[:, n * P:(n + 1) * P],
                                         pb[u][p % 3][:, b, kh * P:(kh + 1) * P], ident[:, :])
                t.then_inc(*pe_.tick(u, f"pT{p}"))

            def a_pv(u, i, p):
                c, j = divmod(p, 4)
                pe.wait_ge(*act_.done(u, f"pT{p}", i))
                for b in range(2):
                    for kh in range(2):
                        n = 2 * c + b
                        m = pe.matmul(psO[u][32 * j:32 * j + 32, n * P:(n + 1) * P],
                                      vS[u][:, b, kh, 32 * p:32 * p + 32], pT[u][p % 2][:, 2 * b + kh, :],
                                      start=kh == 0, stop=kh == 1)
                m.then_inc(*pe_.tick(u, f"pv{p}"))

            def b_proj(u, i):
                pe.wait_ge(*act_.done(u, "xT2", i, bank="qk2"))
                if reader_of("qk2") is not act_:
                    pe.wait_ge(*bank_free(u, "qk2", i))
                for n in range(2 * C):
                    m = features(u, "qk2", n * P, Wqkv, n * P, lambda c: xT[u][:, c, :], P)
                m.then_inc(*pe_.tick(u, "qk2"))
                pe.wait_ge(*bank_free(u, "v2", i))
                for c in range(C):
                    m = pe.matmul(bank(u, "v2")[:, 0:D], xT[u][:, c, :], Wqkv[:, c, 2 * D:3 * D],
                                  start=c == 0, stop=c == C - 1)
                m.then_inc(*pe_.tick(u, "v2"))

            def b_keys(u, i):
                for c, name in enumerate(("kpA", "kpB")):
                    pe.wait_ge(*act_.done(u, "qk2", i, bank=name))
                    if reader_of(name) is not act_:
                        pe.wait_ge(*bank_free(u, name, i))
                    pe.matmul(bank(u, name)[:, :], qk[u][:, C + c, :], PB[:, c, :], start=True,
                              stop=True).then_inc(*pe_.tick(u, name))

            def b_queries(u, i):
                for c, name in enumerate(("qpA", "qpB")):
                    pe.wait_ge(*bank_free(u, name, i))
                    for j in range(4):
                        m = pe.matmul(bank(u, name)[:, j * P:(j + 1) * P], PB[:, c, j * P:(j + 1) * P],
                                      qk[u][:, c, :], start=True, stop=True)
                    m.then_inc(*pe_.tick(u, name))

            def b_kv(u, i):
                for c, name in enumerate(("kvA", "kvB")):
                    pe.wait_ge(*dve_.done(u, ("kpA", "kpB")[c], i, bank=name))
                    if reader_of(name) is not dve_:
                        pe.wait_ge(*bank_free(u, name, i))
                    for j in range(4):
                        p = 4 * c + j
                        m = pe.matmul(bank(u, name)[:, j * P:(j + 1) * P], kp[u][:, p * P:(p + 1) * P],
                                      v2[u][:, :, 34 * p:34 * p + 64], start=True, stop=True)
                    m.then_inc(*pe_.tick(u, name))

            def b_attend(u, i):
                for c, name in enumerate(("aoA", "aoB")):
                    pe.wait_ge(*act_.done(u, "kv", i, bank=name))
                    pe.wait_ge(*dve_.done(u, "kv", i, bank=name))
                    for j in range(4):
                        p = 4 * c + j
                        m = pe.matmul(bank(u, name)[:, j * P:(j + 1) * P], qp[u][:, p * P:(p + 1) * P],
                                      kvb[u][:, :, 34 * p:34 * p + 64], start=True, stop=True)
                    m.then_inc(*pe_.tick(u, name))

            def c_proj(u, i):
                pe.wait_ge(*act_.done(u, "xT3", i, bank="qk3"))
                if reader_of("qk3") is not act_:
                    pe.wait_ge(*bank_free(u, "qk3", i))
                for n in range(2 * C):
                    m = features(u, "qk3", n * P, Wattn, n * P, lambda c: xT[u][:, c, :], P)
                m.then_inc(*pe_.tick(u, "qk3"))
                pe.wait_ge(*bank_free(u, "v3", i))
                for b in range(2):
                    for half in range(2):
                        for c in range(C):
                            m = pe.matmul(bank(u, "v3")[SQ * half:SQ * half + SQ, b * D:(b + 1) * D],
                                          xT[u][:, c, b * SQ:(b + 1) * SQ], Wattn[:, c, 2 * D:3 * D],
                                          start=c == 0, stop=c == C - 1)
                m.then_inc(*pe_.tick(u, "v3"))

            def c_scores(u, i):
                for c, name in enumerate(("s3A", "s3B")):
                    pe.wait_ge(*act_.done(u, "kB", i, bank=name))
                    pe.wait_ge(*dve_.done(u, "kB", i, bank=name))
                    for b in range(2):
                        m = pe.matmul(bank(u, name)[SQ * b:SQ * b + SQ, :], qk[u][:, c, b * SQ:(b + 1) * SQ],
                                      kB[u][:, c, b, :, :].rearrange("p h k -> p (h k)"), start=True, stop=True)
                    m.then_inc(*pe_.tick(u, name))

            def c_probs_t(u, i):
                for c, name in enumerate(("pT3A", "pT3B")):
                    pe.wait_ge(*act_.done(u, ("e3A", "e3B")[c], i, bank=name))
                    if reader_of(name) is not act_:
                        pe.wait_ge(*bank_free(u, name, i))
                    for j in range(4):
                        t = pe.transpose(bank(u, name)[:, j * P:(j + 1) * P], pbf[u][c][:, j * P:(j + 1) * P], ident[:, :])
                    t.then_inc(*pe_.tick(u, name))

            def c_pv(u, i):
                for c, name in enumerate(("o3A", "o3B")):
                    pe.wait_ge(*act_.done(u, ("pT3A", "pT3B")[c], i, bank=name))
                    pe.wait_ge(*dve_.done(u, "vB", i, bank=name))
                    for j in range(4):
                        p = 4 * c + j
                        m = pe.matmul(bank(u, name)[:, j * P:(j + 1) * P], pT[u][c][:, j, :],
                                      vB[u][:, :, 32 * p:32 * p + 64], start=True, stop=True)
                    m.then_inc(*pe_.tick(u, name))

            def d_route(u, i):
                pe.wait_ge(*act_.done(u, "xT4", i, bank="rt"))
                if reader_of("rt") is not act_:
                    pe.wait_ge(*bank_free(u, "rt", i))
                for c in range(C):
                    m = pe.matmul(bank(u, "rt")[:, 0:E], xT[u][:, c, :], Wr[:, c, :], start=c == 0, stop=c == C - 1)
                m.then_inc(*pe_.tick(u, "rt"))

            def d_rank(u, i):
                pe.wait_ge(*dve_.done(u, "oh", i, bank="rk"))
                r, one, two = bank(u, "rk"), ohb[u][:, 0:E], ohb[u][:, E:2 * E]
                pe.matmul(r[:, 0:E], before[:, :], one, start=True, stop=True)
                pe.matmul(r[:, E:2 * E], before[:, :], two, start=True, stop=False)
                pe.matmul(r[:, E:2 * E], ones_b[:, :], one, start=False, stop=True)
                pe.matmul(r[:, 2 * E:3 * E], ones_b[:, :], one, start=True, stop=False)
                pe.matmul(r[:, 2 * E:3 * E], ones_b[:, :], two, start=False, stop=True).then_inc(*pe_.tick(u, "rk"))

            def a_project(u, i):
                project_out(u, i, "w1", Wo, "o1", dve_)

            def b_x_t(u, i):
                transpose_x(u, i, "xT2", xn[u], "xn2")

            def b_out_t(u, i):
                transpose_x(u, i, "aT2", at[u], "ao")

            def b_project(u, i):
                project_out(u, i, "w2", Wout, "aT2", act_)

            def c_x_t(u, i):
                transpose_x(u, i, "xT3", xn[u], "xn3")

            def c_out_t(u, i):
                transpose_x(u, i, "aT3", at[u], "o3")

            def c_project(u, i):
                project_out(u, i, "w3", Wproj, "aT3", act_)

            def d_x_t(u, i):
                transpose_x(u, i, "xT4", xr[u][0], "xn4")

            def a_pair(u, i, p):
                if p + 2 < NP_:
                    a_scores(u, i, p + 2)
                a_probs_t(u, i, p)
                if p:
                    a_pv(u, i, p - 1)

            def half(f, fi, s, si):
                def first(step, *args):
                    if f is not None:
                        step(f, fi, *args)

                def second(step, *args):
                    if s is not None:
                        step(s, si, *args)

                first(a_keys)
                second(b_keys)
                first(a_values)
                second(b_queries)
                first(a_x_t)
                second(b_kv)
                first(a_q)
                second(b_attend)
                first(a_scores, 0)
                first(a_scores, 1)
                second(b_out_t)
                first(a_pair, 0)
                second(b_project)
                first(a_pair, 1)
                first(a_pair, 2)
                second(c_x_t)
                first(a_pair, 3)
                second(c_proj)
                first(a_pair, 4)
                second(c_scores)
                first(a_pair, 5)
                second(c_probs_t)
                second(c_pv)
                first(a_pair, 6)
                first(a_pair, 7)
                second(c_out_t)
                first(a_pv, 7)
                second(c_project)
                if s is None:
                    pe.wait_ge(weights_in, 16 * NW)
                first(a_project)
                second(d_x_t)
                first(b_x_t)
                second(d_route)
                second(d_rank)
                first(b_proj)

            in_turn(pe, half)
            pe.wait_ge(experts_in, 32)
            with pe.Fori(0, BLOCKS // ESLOTS) as i:
                def e_xT(v):
                    pe.wait_ge(block_loaded[v], 16 * (i + 1))
                    pe.wait_ge(*edve_.done_before(v, "hT", i))
                    for c in range(C):
                        t = pe.transpose(ebank[v][0][:, c * P:(c + 1) * P], xs[v][:, c * P:(c + 1) * P], ident[:, :])
                    t.then_inc(*epe_.tick(v, "xT"))

                def e_up(v):
                    expert = pe.value_load(xs[v][0:1, D:D + 1].bitcast(U32), min_val=0, max_val=E - 1)
                    pe.wait_ge(*eact_.done(v, "xT", i))
                    pe.wait_ge(*edve_.done_before(v, "y", i))
                    for c in range(C):
                        m = pe.matmul(ebank[v][1][:, :], xTe[v][:, c, :], W1[:, c, bass.ds(expert * FF, FF)],
                                      start=c == 0, stop=c == C - 1)
                    m.then_inc(*epe_.tick(v, "up"))
                    return expert

                def e_hT(v):
                    pe.wait_ge(*eact_.done(v, "gelu", i))
                    for f in range(FB):
                        t = pe.transpose(ebank[v][0][:, f * P:(f + 1) * P], he[v][:, f * P:(f + 1) * P], ident[:, :])
                    t.then_inc(*epe_.tick(v, "hT"))

                def e_down(v, expert):
                    pe.wait_ge(*edve_.done(v, "hT", i))
                    for f in range(FB):
                        m = pe.matmul(ebank[v][1][:, 0:D], hTe[v][:, f, :],
                                      W2[:, bass.ds(expert * FB + f, 1), :].rearrange("p o n -> p (o n)"),
                                      start=f == 0, stop=f == FB - 1)
                    m.then_inc(*epe_.tick(v, "down"))

                e_xT(0)
                e_xT(1)
                e0 = e_up(0)
                e1 = e_up(1)
                e_xT(2)
                e_xT(3)
                e_hT(0)
                e2 = e_up(2)
                e_hT(1)
                e3 = e_up(3)
                e_down(0, e0)
                e_down(1, e1)
                e_hT(2)
                e_hT(3)
                e_down(2, e2)
                e_down(3, e3)

        @block.scalar
        def _(act):
            for u in range(SLOTS):
                act.sem_inc(act_.sems[u], act_.credits[u])
                act.sem_inc(stored[u], 16)
            for v in range(ESLOTS):
                act.sem_inc(eact_.sems[v], eact_.credits[v])
            with nc.allow_non_contiguous_dma(reason="layer norms' weights laid along partitions, once"):
                for dst_, src in loads:
                    act.dma_start(dst_, src).then_inc(weights_in, 16)
            act.wait_ge(zeroed, 1)
            for h in range(NH):
                r = HD * (h % 8)
                act.dma_start(PB[r:r + HD, h // 8, FEAT * (h % 8):FEAT * (h % 8) + FEAT], proj[h]).then_inc(weights_in, 16)
            act.wait_ge(first_weights_in, 16 * NF)
            act.wait_ge(zeroed, 1 + 4 * SLOTS + 2 * SLOTS)
            def copy_out(u, i, name, dst, scale=None):
                act.wait_ge(*pe_.done(u, name, i))
                src = bank(u, name)
                if scale is None:
                    a = act.activation(dst[:, :, :].rearrange("p c t -> p (c t)"), src[:, 0:C * P], ACT.Copy)
                else:
                    for c in range(C):
                        a = act.activation(dst[:, c, :], src[:, c * P:(c + 1) * P], ACT.Copy, scale=scale[:, c:c + 1])
                a.then_inc(*act_.tick(u, name))

            def a_keys(u, i):
                for c, name in enumerate(("k1a", "k1b")):
                    act.wait_ge(*pe_.done(u, name, i))
                    act.activation(kT[u][:, c, :, :].rearrange("p b k -> p (b k)"), bank(u, name)[:, :], ACT.Identity,
                                   bias=bkT[:, c:c + 1]).then_inc(*act_.tick(u, name))

            def a_values(u, i):
                for b, name in enumerate(("v1a", "v1b")):
                    act.wait_ge(*pe_.done(u, name, i))
                    act.activation(vS[u][:, b, :, :].rearrange("p k n -> p (k n)"), bank(u, name)[:, :],
                                   ACT.Copy).then_inc(*act_.tick(u, name))

            def a_x_t(u, i):
                copy_out(u, i, "xT1", xT[u])

            def a_q(u, i):
                act.wait_ge(*pe_.done(u, "q1", i))
                for c in range(C):
                    a = act.activation(qs[u][:, c, :], bank(u, "q1")[:, c * P:(c + 1) * P], ACT.Identity,
                                       bias=bqT[:, c:c + 1])
                a.then_inc(*act_.tick(u, "q1"))
                act.wait_ge(*act_.done(u, "q1", i))
                for j in range(4):
                    r = slice(32 * j, 32 * j + 32)
                    a = act.activation(qB[u][r, j, :, :, 1, :].rearrange("p c b q -> p (c b) q"),
                                       qs[u][r, :, :].rearrange("p c (b q) -> p (c b) q", b=2), ACT.Copy, scale=hmask[r, 3:4])
                a.then_inc(*act_.tick(u, "qB"))

            def b_x_t(u, i):
                copy_out(u, i, "xT2", xT[u])

            def b_out_t(u, i):
                copy_out(u, i, "aT2", aT[u])

            def c_x_t(u, i):
                copy_out(u, i, "xT3", xT[u], ln1T)

            def c_out_t(u, i):
                copy_out(u, i, "aT3", aT[u])

            def d_x_t(u, i):
                copy_out(u, i, "xT4", xT[u], ln2T)

            def d_store(u, i):
                act.wait_ge(*pool_.done(u, "sum", i))
                act.dma_start(out[bass.ds((i * SLOTS + u) * P, P), :], xb[u][:, :]).then_inc(stored[u], 16)

            def a_exp(u, i, p):
                act.wait_ge(*dve_.done(u, f"min{p}", i))
                for b in range(2):
                    n = 2 * p + b
                    a = act.activation(pb[u][p % 3][:, b, :], pb[u][p % 3][:, b, :], ACT.Exp, bias=mn[u][:, n:n + 1],
                                       scale=-1.0, accum_out=su[u][:, n:n + 1])
                a.then_inc(*act_.tick(u, f"exp{p}"))

            def a_pt(u, i, p):
                act.wait_ge(*pe_.done(u, f"pT{p}", i))
                act.activation(pT[u][p % 2][:, :, :].rearrange("p a b -> p (a b)"), bank(u, f"pT{p}")[:, :],
                               ACT.Copy).then_inc(*act_.tick(u, f"pT{p}"))

            def b_qk(u, i):
                act.wait_ge(*pe_.done(u, "qk2", i))
                act.activation(qk[u][:, :, :].rearrange("p c t -> p (c t)"), bank(u, "qk2")[:, :],
                               ACT.Copy).then_inc(*act_.tick(u, "qk2"))

            def b_exp(u, i, which):
                for n, half in enumerate("AB"):
                    act.wait_ge(*pe_.done(u, f"{which}p{half}", i))
                    if which == "q":
                        act.wait_ge(*dve_.done(u, f"kp{half}", i))
                    act.activation(pbf[u][n], bank(u, f"{which}p{half}")[:, :],
                                   ACT.Exp).then_inc(*act_.tick(u, f"e{which}{half}"))

            def b_kv(u, i):
                act.wait_ge(*pe_.done(u, "kvA", i))
                src = bank(u, "kvA")[:, :].rearrange("p (j b w) -> p b j w", j=4, b=2)
                dst = kvb[u][:, :, 0:4 * 34].rearrange("p b (j w) -> p b j w", w=34)
                for h in range(2):
                    a = act.activation(dst[64 * h:64 * h + 64, :, :, 17 * h:17 * h + 17],
                                       src[64 * h:64 * h + 64, :, :, 17 * h:17 * h + 17], ACT.Copy)
                a.then_inc(*act_.tick(u, "kv"))

            def c_q(u, i):
                act.wait_ge(*pe_.done(u, "qk3", i))
                act.activation(qk[u][:, :, :].rearrange("p c t -> p (c t)"), bank(u, "qk3")[:, :],
                               ACT.Copy).then_inc(*act_.tick(u, "qk3"))
                act.wait_ge(*act_.done(u, "qk3", i))
                for j in range(4):
                    r = slice(32 * j, 32 * j + 32)
                    a = act.activation(kB[u][r, :, :, 2 * j + 1, :].rearrange("p c b k -> p (c b) k"),
                                       qk[u][r, C:2 * C, :].rearrange("p c (b k) -> p (c b) k", b=2), ACT.Copy, scale=hmask[r, 3:4])
                a.then_inc(*act_.tick(u, "kB"))

            def c_exp(u, i, n):
                act.wait_ge(*dve_.done(u, ("d3A", "d3B")[n], i))
                act.activation(pbf[u][n], pbf[u][n], ACT.Exp, scale=-1.0).then_inc(*act_.tick(u, ("e3A", "e3B")[n]))

            def c_pt(u, i):
                for n, name in enumerate(("pT3A", "pT3B")):
                    act.wait_ge(*pe_.done(u, name, i))
                    act.activation(pT[u][n][:, :, :].rearrange("p a b -> p (a b)"), bank(u, name)[:, :],
                                   ACT.Copy).then_inc(*act_.tick(u, name))

            def d_gate(u, i):
                act.wait_ge(*dve_.done(u, "dl", i))
                act.activation(gt[u][:, 32:33], gt[u][:, 24:25], ACT.Exp).then_inc(*act_.tick(u, "eg"))

            def half(f, fi, s, si):
                def first(step, *args):
                    if f is not None:
                        step(f, fi, *args)

                def second(step, *args):
                    if s is not None:
                        step(s, si, *args)

                first(a_keys)
                second(b_exp, "k")
                first(a_values)
                second(b_exp, "q")
                first(a_x_t)
                second(b_kv)
                first(a_q)
                first(a_exp, 0)
                if s is None:
                    act.wait_ge(weights_in, 16 * NW)
                    act.dma_start(sorted_d.rearrange("(s p) n -> s p n", p=P),
                                  row_d.unsqueeze(0).to_broadcast([BLOCKS, P, XW])).then_inc(rows_cleared, 16)
                    act.dma_start(W1[:, :, :], w1.rearrange("(c p) n -> p c n", p=P)).then_inc(experts_in, 16)
                    act.dma_start(W2[:, :, :], w2.rearrange("(f p) n -> p f n", p=P)).then_inc(experts_in, 16)
                second(b_out_t)
                first(a_exp, 1)
                first(a_pt, 0)
                first(a_exp, 2)
                first(a_pt, 1)
                first(a_exp, 3)
                first(a_pt, 2)
                second(c_x_t)
                first(a_exp, 4)
                first(a_pt, 3)
                second(c_q)
                first(a_exp, 5)
                first(a_pt, 4)
                first(a_exp, 6)
                first(a_pt, 5)
                second(c_exp, 0)
                second(c_exp, 1)
                second(c_pt)
                first(a_exp, 7)
                first(a_pt, 6)
                first(a_pt, 7)
                second(c_out_t)
                second(d_x_t)
                first(b_x_t)
                second(d_gate)
                second(d_store)
                first(b_qk)

            in_turn(act, half)
            with act.Fori(0, BLOCKS // ESLOTS) as i:
                def e_xT(v):
                    act.wait_ge(*epe_.done(v, "xT", i))
                    for c in range(C):
                        a = act.activation(xTe[v][:, c, :], ebank[v][0][:, c * P:(c + 1) * P], ACT.Copy, scale=ln2T[:, c:c + 1])
                    a.then_inc(*eact_.tick(v, "xT"))

                def e_gelu(v):
                    act.wait_ge(*epe_.done(v, "up", i))
                    act.activation(he[v], ebank[v][1][:, :], ACT.Gelu).then_inc(*eact_.tick(v, "gelu"))

                e_xT(0)
                e_xT(1)
                e_gelu(0)
                e_gelu(1)
                e_xT(2)
                e_xT(3)
                e_gelu(2)
                e_gelu(3)

        @block.vector
        def _(dve):
            for u in range(SLOTS):
                dve.sem_inc(dve_.sems[u], dve_.credits[u])
                if u:
                    dve.sem_inc(chain_links[u], u * 3 * CHAIN)
            for v in range(ESLOTS):
                dve.sem_inc(edve_.sems[v], edve_.credits[v])
            dve.wait_ge(first_weights_in, 16 * NF)
            dve.wait_ge(state_set, 4)
            dve.wait_ge(zeroed, 1 + 4 * SLOTS + 2 * SLOTS)
            chained = [0] * SLOTS

            def link(u, i, ins):
                ins.then_inc(chain_links[u], 1)
                chained[u] += 1
                dve.wait_ge(chain_links[u], i * CHAIN + u * 3 * CHAIN + (chained[u] - 1) % CHAIN + 1)

            def stats(u, i, n, src):
                dve.sem_inc(wait_taken, 1)
                link(u, i, dve.bn_stats(bst[u][:, :], src[:, 0:D]))
                dve.sem_inc(wait_taken, 1)
                link(u, i, dve.bn_aggr(mv[u][:, 0:2], bst[u][:, :]))
                dve.tensor_scalar(mv[u][:, 2:3], mv[u][:, 1:2], EPS, None, ALU.add).then_inc(*dve_.tick(u, f"var{n}"))

            def normalize(u, i, n, src, dst=xn):
                dve.wait_ge(*pool_.done(u, f"rs{n}", i))
                dve.tensor_scalar(dst[u][:, 0:D], src[:, 0:D], mv[u][:, 0:1], mv[u][:, 3:4], ALU.subtract,
                                  ALU.mult).then_inc(*dve_.tick(u, f"xn{n}"))

            def a_stats(u, i):
                dve.wait_ge(x_loaded[u], (i + 1) * 16)
                stats(u, i, 1, x_in[u])

            def a_norm(u, i):
                normalize(u, i, 1, x_in[u])
                dve.wait_ge(mask_loaded[u], (i + 1) * 16)
                dve.tensor_scalar(madd[u][:, :, :], mraw[u][:, :, :], -MASKED, MASKED, ALU.mult,
                                  ALU.add).then_inc(*dve_.tick(u, "madd"))

            def a_query(u, i):
                dve.wait_ge(*act_.done(u, "q1", i))
                for j in range(4):
                    r = slice(32 * j, 32 * j + 32)
                    t = dve.tensor_scalar(qB[u][r, j, :, :, 0, :].rearrange("p c b q -> p (c b) q"),
                                          qs[u][r, :, :].rearrange("p c (b q) -> p (c b) q", b=2), hmask[r, 2:3], None, ALU.mult)
                t.then_inc(*dve_.tick(u, "qB"))

            def a_max(u, i, p):
                dve.wait_ge(*pe_.done(u, f"s{p}", i))
                dve.sem_inc(wait_taken, 1)
                for b in range(2):
                    n = 2 * p + b
                    t = dve.tensor_tensor_reduce(pb[u][p % 3][:, b, :], bank(u, f"s{p}")[:, b * SK:(b + 1) * SK],
                                                 madd[u][:, b, :], 1.0, MASKED, ALU.add, ALU.min, mn[u][:, n:n + 1])
                t.then_inc(*dve_.tick(u, f"min{p}"))

            def a_divide(u, i, p):
                dve.wait_ge(*act_.done(u, f"exp{p}", i))
                dve.reciprocal(ri[u][:, 2 * p:2 * p + 2], su[u][:, 2 * p:2 * p + 2]).then_inc(*dve_.tick(u, f"ri{p}"))
                dve.wait_ge(*dve_.done(u, f"ri{p}", i))
                for b in range(2):
                    n = 2 * p + b
                    t = dve.tensor_scalar(pb[u][p % 3][:, b, :], pb[u][p % 3][:, b, :], ri[u][:, n:n + 1], None, ALU.mult)
                t.then_inc(*dve_.tick(u, f"nrm{p}"))

            def a_out(u, i):
                dve.wait_ge(*pe_.done(u, f"pv{NP_ - 1}", i))
                o = psO[u][:, :].rearrange("p (n h q) -> p n h q", n=4, h=2)
                a = aT[u][:, :, :].rearrange("p c (b q) -> p (c b) q", b=2)
                for c in range(C):
                    t = dve.tensor_scalar(a[:, 2 * c:2 * c + 2, :], o[:, 2 * c:2 * c + 2, 0, :], hmask[:, 0:1], bvT[:, c:c + 1],
                                          ALU.mult, ALU.add)
                t.then_inc(*dve_.tick(u, "o1a"))
                dve.wait_ge(*dve_.done(u, "o1a", i))
                dve.scalar_tensor_tensor(out=a, in0=o[:, :, 1, :], scalar=hmask[:, 1:2], in1=a, op0=ALU.mult,
                                         op1=ALU.add).then_inc(*dve_.tick(u, "o1"))

            def add_residual(u, i, name, group, src, dst, pool_step=None):
                dve.wait_ge(*pe_.done(u, group, i))
                if pool_step:
                    dve.wait_ge(*pool_.done(u, pool_step, i))
                dve.tensor_tensor(dst[:, 0:D], bank(u, group)[:, 0:D], src[:, :], ALU.add).then_inc(*dve_.tick(u, name))
                dve.wait_ge(*dve_.done(u, name, i))

            def b_value(u, i):
                dve.wait_ge(*pe_.done(u, "v2", i))
                for b in range(2):
                    r = slice(SQ * b, SQ * b + SQ)
                    t = dve.tensor_copy(v2[u][r, b, 0:NP_ * 34].rearrange("p (h w) -> p h w", w=17)[:, :, 0:HD],
                                        bank(u, "v2")[r, 0:D].rearrange("p (h d) -> p h d", d=HD))
                t.then_inc(*dve_.tick(u, "v2"))

            def b_feature(u, i, which, dst):
                for n, half in enumerate("AB"):
                    dve.wait_ge(*act_.done(u, f"e{which}{half}", i))
                    dve.tensor_scalar(pbf[u][n], pbf[u][n], 1.0, None, ALU.min).then_inc(*dve_.tick(u, f"t{which}{half}"))
                    dve.wait_ge(*dve_.done(u, f"t{which}{half}", i))
                    dve.scalar_tensor_tensor(out=dst[u][:, n * 512:(n + 1) * 512], in0=bank(u, f"{which}p{half}")[:, :],
                                             scalar=1.0, in1=pbf[u][n], op0=ALU.add,
                                             op1=ALU.max).then_inc(*dve_.tick(u, f"{which}p{half}"))

            def b_kv(u, i):
                dve.wait_ge(*pe_.done(u, "kvB", i))
                src = bank(u, "kvB")[:, :].rearrange("p (j b w) -> p b j w", j=4, b=2)
                dst = kvb[u][:, :, 4 * 34:8 * 34].rearrange("p b (j w) -> p b j w", w=34)
                for h in range(2):
                    t = dve.tensor_copy(dst[64 * h:64 * h + 64, :, :, 17 * h:17 * h + 17],
                                        src[64 * h:64 * h + 64, :, :, 17 * h:17 * h + 17])
                t.then_inc(*dve_.tick(u, "kv"))

            def b_out(u, i):
                dve.wait_ge(*pe_.done(u, "aoB", i))

                def cols(c, b):
                    o = bank(u, ("aoA", "aoB")[c])[SQ * b:SQ * b + SQ, :].rearrange("p (j b w) -> p j b w", j=4, b=2)
                    return o[:, :, b, 0:34].rearrange("p j (h w) -> p j h w", h=2)

                for c in range(C):
                    for b in range(2):
                        t = dve.tensor_scalar(su[u][SQ * b:SQ * b + SQ, 8 * c:8 * c + 8].rearrange("p (j h) -> p j h", h=2),
                                              cols(c, b)[:, :, :, 16], 1e-8, None, ALU.add)
                t.then_inc(*dve_.tick(u, "den"))
                dve.wait_ge(*dve_.done(u, "den", i))
                dve.reciprocal(ri[u][:, :], su[u][:, :]).then_inc(*dve_.tick(u, "rden"))
                dve.wait_ge(*dve_.done(u, "rden", i))
                for c in range(C):
                    for b in range(2):
                        r = slice(SQ * b, SQ * b + SQ)
                        t = dve.tensor_tensor(
                            at[u][r, c * P:(c + 1) * P].rearrange("p (j h d) -> p j h d", j=4, h=2), cols(c, b)[:, :, :, 0:HD],
                            ri[u][r, 8 * c:8 * c + 8].rearrange("p (j h) -> p j h", h=2).unsqueeze(3)
                            .to_broadcast([SQ, 4, 2, HD]), ALU.mult)
                t.then_inc(*dve_.tick(u, "ao"))

            def a_residual(u, i):
                add_residual(u, i, "x1", "w1", xres[u], xa[u], "xb1")
                stats(u, i, 2, xa[u])

            def b_norm(u, i):
                normalize(u, i, 2, xa[u])

            def b_residual(u, i):
                dve.wait_ge(stored[u], (i + 1) * 16)
                add_residual(u, i, "x2", "w2", xres[u], xb[u], "xb2")
                stats(u, i, 0, xb[u])

            def c_residual(u, i):
                dve.wait_ge(*pool_.done(u, "rs0", i))
                dve.tensor_scalar(xres[u][:, :], xb[u][:, 0:D], mv[u][:, 0:1], mv[u][:, 3:4], ALU.subtract,
                                  ALU.mult).then_inc(*dve_.tick(u, "h0"))
                dve.wait_ge(*dve_.done(u, "h0", i))
                stats(u, i, 3, xres[u])

            def c_norm(u, i):
                normalize(u, i, 3, xres[u])

            def d_residual(u, i):
                add_residual(u, i, "x3", "w3", xres[u], xa[u])
                stats(u, i, 4, xa[u])

            def d_norm(u, i):
                normalize(u, i, 4, xa[u], [xr[0][0], xr[1][0]])

            def c_keys(u, i):
                dve.wait_ge(*act_.done(u, "qk3", i))
                for j in range(4):
                    r = slice(32 * j, 32 * j + 32)
                    t = dve.tensor_scalar(kB[u][r, :, :, 2 * j, :].rearrange("p c b k -> p (c b) k"),
                                          qk[u][r, C:2 * C, :].rearrange("p c (b k) -> p (c b) k", b=2), hmask[r, 2:3], None, ALU.mult)
                t.then_inc(*dve_.tick(u, "kB"))

            def c_value(u, i):
                dve.wait_ge(*pe_.done(u, "v3", i))
                src = bank(u, "v3")[:, :].rearrange("p (b j h d) -> p b j h d", b=2, j=NP_, h=2)
                dst = vB[u][:, :, 0:D].rearrange("p b (j h d) -> p b j h d", j=NP_, h=2)
                for h in range(2):
                    r = slice(64 * h, 64 * h + 64)
                    t = dve.tensor_copy(dst[r, :, :, h, :], src[r, :, :, h, :])
                t.then_inc(*dve_.tick(u, "vB"))

            def heads(ap):
                return ap.rearrange("p (h k) -> p h k", k=SQ)

            def c_max(u, i, n):
                half = "AB"[n]
                dve.wait_ge(*pe_.done(u, f"s3{half}", i))
                dve.tensor_tensor(heads(pbf[u][n]), heads(bank(u, f"s3{half}")[:, :]),
                                  causal[:, :].unsqueeze(1).to_broadcast([P, 8, SQ]),
                                  ALU.add).then_inc(*dve_.tick(u, f"s3{half}"))
                dve.wait_ge(*dve_.done(u, f"s3{half}", i))
                dve.tensor_reduce(mn[u][:, 8 * n:8 * n + 8], heads(pbf[u][n]), AX.X,
                                  ALU.min).then_inc(*dve_.tick(u, f"m3{half}"))
                dve.wait_ge(*dve_.done(u, f"m3{half}", i))
                dve.tensor_tensor(heads(pbf[u][n]), heads(pbf[u][n]),
                                  mn[u][:, 8 * n:8 * n + 8].unsqueeze(2).to_broadcast([P, 8, SQ]),
                                  ALU.subtract).then_inc(*dve_.tick(u, f"d3{half}"))

            def c_sum(u, i):
                for n, half in enumerate("AB"):
                    dve.wait_ge(*act_.done(u, f"e3{half}", i))
                    dve.tensor_reduce(su[u][:, 8 * n:8 * n + 8], heads(pbf[u][n]), AX.X,
                                      ALU.add).then_inc(*dve_.tick(u, f"sum{half}"))
                dve.wait_ge(*dve_.done(u, "sumB", i))
                dve.reciprocal(ri[u][:, :], su[u][:, :]).then_inc(*dve_.tick(u, "r3"))

            def c_out(u, i):
                dve.wait_ge(*dve_.done(u, "r3", i))
                dve.wait_ge(*pe_.done(u, "o3B", i))
                for c in range(C):
                    for b in range(2):
                        r = slice(SQ * b, SQ * b + SQ)
                        o = bank(u, ("o3A", "o3B")[c])[r, :].rearrange("p (j b w) -> p j b w", j=4, b=2)
                        t = dve.tensor_tensor(
                            at[u][r, c * P:(c + 1) * P].rearrange("p (j h d) -> p j h d", j=4, h=2),
                            o[:, :, b, 0:32].rearrange("p j (h d) -> p j h d", h=2),
                            ri[u][r, 8 * c:8 * c + 8].rearrange("p (j h) -> p j h", h=2).unsqueeze(3)
                            .to_broadcast([SQ, 4, 2, HD]), ALU.mult)
                t.then_inc(*dve_.tick(u, "o3"))

            def d_top(u, i):
                g = gt[u]
                dve.wait_ge(*pe_.done(u, "rt", i))
                dve.sem_inc(wait_taken, 1)
                dve.max(g[:, 8:16], bank(u, "rt")[:, 0:E]).then_inc(*dve_.tick(u, "top"))
                dve.wait_ge(*dve_.done(u, "top", i))
                dve.tensor_tensor(g[:, 24:25], g[:, 9:10], g[:, 8:9], ALU.subtract).then_inc(*dve_.tick(u, "dl"))
                dve.max_index(gix[u][:, :], g[:, 8:16], bank(u, "rt")[:, 0:E]).then_inc(*dve_.tick(u, "ix"))
                dve.wait_ge(*dve_.done(u, "ix", i))
                dve.tensor_tensor(ohb[u][:, :].rearrange("p (k e) -> p k e", k=TOP), iota8[:, :].unsqueeze(1).to_broadcast([P, TOP, E]),
                                  gix[u][:, 0:TOP].unsqueeze(2).to_broadcast([P, TOP, E]), ALU.is_equal).then_inc(*dve_.tick(u, "oh"))

            def d_gate(u, i):
                g = gt[u]
                dve.wait_ge(*act_.done(u, "eg", i))
                link(u, i, dve.tensor_scalar(g[:, 33:34], g[:, 32:33], 1.0, None, ALU.add))
                link(u, i, dve.reciprocal(g[:, 34:35], g[:, 33:34]))
                dve.tensor_tensor(g[:, 35:36], g[:, 34:35], g[:, 32:33],
                                  ALU.mult).then_inc(*dve_.tick(u, "gate"))

            def d_place(u, i):
                s, r = sc[u], bank(u, "rk")
                end, over, new, skip, ahead, gap, shift = (s[:, n * E:(n + 1) * E] for n in range(7))
                at_, hop, placed = s[:, 64:80], s[:, 80:96], s[:, 96:112]
                both_ = lambda ap: ap.rearrange("p (k e) -> p k e", k=TOP)
                each = lambda ap: ap.unsqueeze(1).to_broadcast([P, TOP, E])
                dve.tensor_scalar(gap, first[:, :], -1.0, unused[:, 0:1], ALU.mult, ALU.add)
                dve.wait_ge(*pe_.done(u, "rk", i))
                dve.tensor_tensor(both_(at_), both_(r[:, 0:2 * E]), each(used[:, :]), ALU.add)
                dve.tensor_tensor(end, r[:, 2 * E:3 * E], used[:, :], ALU.add).then_inc(*dve_.tick(u, "rk"))
                dve.wait_ge(*dve_.done(u, "rk", i))
                dve.tensor_tensor(both_(placed), both_(at_), each(first[:, :]), ALU.add)
                link(u, i, dve.tensor_scalar(over, end, float(P), None, ALU.is_gt))
                link(u, i, dve.scalar_tensor_tensor(out=new, in0=end, scalar=float(2 * P), in1=over, op0=ALU.is_gt, op1=ALU.add))
                link(u, i, dve.tensor_tensor(cum8[u][:, :, :], earlier[:, :, :], new.unsqueeze(1).to_broadcast([P, E, E]), ALU.mult))
                link(u, i, dve.tensor_reduce(skip, cum8[u][:, :, :], AX.X, ALU.add))
                link(u, i, dve.scalar_tensor_tensor(out=ahead, in0=skip, scalar=float(P), in1=gap, op0=ALU.mult, op1=ALU.add))
                link(u, i, dve.scalar_tensor_tensor(out=both_(hop), in0=both_(at_), scalar=float(P), in1=each(ahead), op0=ALU.is_ge, op1=ALU.mult))
                link(u, i, dve.tensor_tensor(placed, placed, hop, ALU.add))
                link(u, i, dve.tensor_tensor(placed, placed, ohb[u][:, :], ALU.mult))
                dve.tensor_reduce(gt[u][:, 40:42], both_(placed), AX.X, ALU.add)
                dve.scalar_tensor_tensor(out=used[:, :], in0=new, scalar=-float(P), in1=end, op0=ALU.mult, op1=ALU.add)
                dve.tensor_tensor(shift, over, ahead, ALU.mult)
                dve.scalar_tensor_tensor(out=first[:, :], in0=new, scalar=float(P), in1=first[:, :], op0=ALU.mult, op1=ALU.add)
                link(u, i, dve.tensor_reduce(gt[u][:, 42:43], new, AX.X, ALU.add))
                dve.tensor_tensor(first[:, :], first[:, :], shift, ALU.add)
                dve.wait_ge(*pool_.done_before(u, "sent", i))
                dve.tensor_copy(pos[u][:, :], gt[u][:, 40:42]).then_inc(*dve_.tick(u, "pos"))
                link(u, i, dve.scalar_tensor_tensor(out=unused[:, :], in0=gt[u][:, 42:43], scalar=float(P), in1=unused[:, :], op0=ALU.mult, op1=ALU.add))

            def half(f, fi, s, si):
                def first(step, *args):
                    if f is not None:
                        step(f, fi, *args)

                def second(step, *args):
                    if s is not None:
                        step(s, si, *args)

                first(a_stats)
                second(b_feature, "k", kp)
                first(a_norm)
                second(b_feature, "q", qp)
                second(b_kv)
                first(a_query)
                second(b_out)
                first(a_max, 0)
                first(a_max, 1)
                first(a_divide, 0)
                first(a_max, 2)
                second(b_residual)
                first(a_divide, 1)
                first(a_max, 3)
                second(c_residual)
                first(a_divide, 2)
                first(a_max, 4)
                second(c_norm)
                first(a_divide, 3)
                first(a_max, 5)
                second(c_keys)
                second(c_value)
                first(a_divide, 4)
                first(a_max, 6)
                second(c_max, 0)
                first(a_divide, 5)
                first(a_max, 7)
                second(c_max, 1)
                second(c_sum)
                first(a_divide, 6)
                first(a_divide, 7)
                second(c_out)
                first(a_out)
                second(d_residual)
                first(a_residual)
                second(d_norm)
                first(b_norm)
                second(d_top)
                second(d_gate)
                second(d_place)
                first(b_value)
                if s is None:
                    dve.wait_ge(weights_in, 16 * NW)

            in_turn(dve, half)
            assert chained == [CHAIN * ITERS_WRITTEN] * SLOTS, chained
            with dve.Fori(0, BLOCKS // ESLOTS) as i:
                def e_hT(v):
                    dve.wait_ge(*epe_.done(v, "hT", i))
                    dve.tensor_copy(hTe[v][:, :, :].rearrange("p a b -> p (a b)"), ebank[v][0][:, :]).then_inc(*edve_.tick(v, "hT"))

                def e_y(v):
                    dve.wait_ge(*epe_.done(v, "down", i))
                    dve.wait_ge(*epool_.done_before(v, "sent", i))
                    dve.tensor_copy(where[v][:, :], xs[v][:, D + 1:D + 2].bitcast(U32))
                    dve.tensor_scalar(ye[v][:, :], ebank[v][1][:, 0:D], xs[v][:, D + 2:D + 3], None,
                                      ALU.mult).then_inc(*edve_.tick(v, "y"))

                e_hT(0)
                e_hT(1)
                e_y(0)
                e_y(1)
                e_hT(2)
                e_hT(3)
                e_y(2)
                e_y(3)

    return nc


_INS = ["x", "ctx_1024", "mask_BxS2_bf1", "L0_xattn_Wq", "L0_xattn_bq", "L0_xattn_Wk", "L0_xattn_bk", "L0_xattn_Wv",
        "L0_xattn_bv", "L0_xattn_Wo", "L0_xattn_bo", "L0_attn_w_qkv", "L0_attn_proj_matrix", "L0_attn_w_out",
        "L0_attn_b_out", "L0_ffn_ln1_w", "L0_ffn_c_attn_w", "L0_ffn_c_proj_w", "L0_ffn_ln2_w", "L0_ffn_router_w",
        "L0_ffn_w1", "L0_ffn_w2"]


def kernel(**inputs):
    import concourse.bacc as bacc
    from concourse.bass_utils import run_bass_kernel_spmd

    arrays = {n: np.ascontiguousarray(inputs[n]) for n in _INS}
    arrays["x"] = arrays["x"].reshape(B * SQ, D)
    arrays["ctx_1024"] = np.ascontiguousarray(arrays["ctx_1024"].transpose(0, 2, 1)).reshape(B * D, SK)
    q = np.arange(P) % SQ
    arrays["ident"] = np.eye(P, dtype=np.float32)
    parity = (np.arange(P)[:, None] // HD % 2 == np.arange(2)[None, :]).astype(np.float32)
    arrays["hmask"] = np.concatenate([parity, np.where(parity > 0, -SCALE, 0.0).astype(np.float32)], axis=1)
    arrays["causal"] = np.where(np.arange(SQ)[None, :] > q[:, None], MASKED, 0.0).astype(np.float32)
    arrays["iota8"] = np.tile(np.arange(E, dtype=np.float32), (P, 1))
    arrays["before"] = np.triu(np.ones((P, P), np.float32), 1).astype(mybir.dt.np(BF16))
    arrays["earlier"] = np.broadcast_to(np.tril(np.ones((E, E), np.float32), -1), (P, E, E)).copy()
    empty = np.zeros((P, XW), np.uint32)
    empty[:, D + 1] = NOWHERE
    arrays["empty_row"] = empty.view(np.float32)
    arrays["token"] = (np.arange(SLOTS * P).reshape(SLOTS, P, 1)).astype(np.float32)

    nc = bacc.Bacc("TRN2", target_bir_lowering=False, num_devices=1)
    aps = [nc.dram_tensor(f"in_{n}", a.shape, mybir.dt.from_np(a.dtype), kind="ExternalInput").ap()
           for n, a in arrays.items()]
    out = nc.dram_tensor("out_0", (B * SQ, D), F32, kind="ExternalOutput").ap()
    scratch = [nc.dram_tensor(n, shape, F32, kind="Internal").ap()
               for n, shape in (("sorted_rows", (BLOCKS * P, XW)),)]
    build(nc, *aps, *scratch, out)
    r = run_bass_kernel_spmd(nc, [{f"in_{n}": a for n, a in arrays.items()}], core_ids=[0])
    return r.results[0]["out_0"].reshape(B, SQ, D)
```
